# Optimizing a Trainium2 kernel written in Bass

```python
import numpy as np
import jax
import jax.numpy as jnp

def _softmax(x, axis=-1):
    return jax.nn.softmax(x, axis=axis)

def _gelu(x):
    return jax.nn.gelu(x, approximate=True)

def _silu(x):
    return jax.nn.silu(x)

def _sigmoid(x):
    return jax.nn.sigmoid(x)

def _layernorm(x, axis=-1, eps=1e-05):
    m = jnp.mean(x, axis=axis, keepdims=True)
    v = jnp.var(x, axis=axis, keepdims=True)
    return (x - m) / jnp.sqrt(v + eps)

def _scatter_add(tgt, idx, src, axis=0):
    return tgt.at[idx].add(src)

def _segment_sum(src, seg, n):
    return jax.ops.segment_sum(src, seg, n)
kernel_name = 'mk_seq_preln_d4_jaxref_r8_f32268'

def setup_inputs(seed: int=0):
    np.random.seed(seed)
    _w = jnp.asarray

    def _L0_attn_setup():
        import jax, jax.numpy as jnp
        import numpy as np
        B, S, E, H = (2, 256, 128, 16)
        key = jax.random.key(seed)
        k0, k1, k2 = jax.random.split(key, 3)
        x = jax.random.normal(k0, (B, S, E), jnp.float32)
        w_in = jax.random.normal(k1, (3 * E, E), jnp.float32) / np.sqrt(E)
        b_in = jnp.zeros((3 * E,), jnp.float32)
        w_out = jax.random.normal(k2, (E, E), jnp.float32) / np.sqrt(E)
        b_out = jnp.zeros((E,), jnp.float32)
        return {'x': x, 'w_in': w_in, 'b_in': b_in, 'w_out': w_out, 'b_out': b_out}
    _L0_attn_in = _L0_attn_setup()

    def _L0_ffn_setup():
        import jax, jax.numpy as jnp
        import numpy as np
        H = 128
        I = 64
        E = 64
        G = 8
        TOPK_GROUP = 4
        K = 8
        I_SH = 128
        SCALE = 2.5

        def _route(x, router_w, e_bias):
            T = x.shape[0]
            scores = jax.nn.sigmoid(x.astype(jnp.float32) @ router_w.T.astype(jnp.float32))
            sfc = jax.lax.stop_gradient(scores) + e_bias[None, :]
            group_scores = jax.lax.top_k(sfc.reshape(T, G, E // G), 2)[0].sum(-1)
            _, gidx = jax.lax.top_k(group_scores, TOPK_GROUP)
            gmask = jax.nn.one_hot(gidx, G, dtype=sfc.dtype).sum(1)
            smask = jnp.repeat(gmask, E // G, axis=1)
            masked = jnp.where(smask > 0, sfc, 0.0)
            _, topk_idx = jax.lax.top_k(masked, K)
            w = jnp.take_along_axis(scores, topk_idx, axis=1)
            w = w / (w.sum(-1, keepdims=True) + 1e-20)
            return (topk_idx, w * SCALE)
        key = jax.random.key(seed)
        ks = jax.random.split(key, 9)
        s = 0.02
        return {'hidden_states': jax.random.normal(ks[0], (2, 128, H), jnp.float32), 'router_w': jax.random.normal(ks[1], (E, H), jnp.float32) * s, 'e_bias': jnp.zeros((E,), jnp.float32), 'Wg': jax.random.normal(ks[2], (E, H, I), jnp.float32) * s, 'Wu': jax.random.normal(ks[3], (E, H, I), jnp.float32) * s, 'Wd': jax.random.normal(ks[4], (E, I, H), jnp.float32) * s, 'SWg': jax.random.normal(ks[5], (H, I_SH), jnp.float32) * s, 'SWu': jax.random.normal(ks[6], (H, I_SH), jnp.float32) * s, 'SWd': jax.random.normal(ks[7], (I_SH, H), jnp.float32) * s}
    _L0_ffn_in = _L0_ffn_setup()

    def _L1_attn_setup():
        import jax, jax.numpy as jnp
        import numpy as np
        D_MODEL = 128
        N_HEAD = 16
        HEAD_DIM = D_MODEL // N_HEAD
        D_INNER = 512
        N_LAYER = 4
        NEG = jnp.finfo(jnp.float32).min

        def _ln(x, w, b):
            m = x.mean(-1, keepdims=True)
            v = ((x - m) ** 2).mean(-1, keepdims=True)
            return (x - m) * jax.lax.rsqrt(v + 1e-06) * w + b

        def _pos_emb(k_len):
            pos = jnp.arange(k_len - 1, -1, -1, dtype=jnp.float32)
            inv = 1.0 / 10000.0 ** (jnp.arange(0, HEAD_DIM, 2, dtype=jnp.float32) / HEAD_DIM)
            s = pos[:, None] * inv[None, :]
            return jnp.concatenate([jnp.sin(s), jnp.cos(s)], axis=-1)

        def _rel_shift(x, q_len, k_len):
            B, H = (x.shape[0], x.shape[1])
            zp = jnp.zeros((B, H, q_len, 1), x.dtype)
            xp = jnp.concatenate([zp, x], axis=-1).reshape(B, H, k_len + 1, q_len)
            return xp[:, :, 1:, :].reshape(B, H, q_len, k_len)

        def _attn(xn, Wq, bq, Wk, bk, Wv, bv, Wo, bo, u):
            B, S, _ = xn.shape
            sh = lambda t: t.reshape(B, S, N_HEAD, HEAD_DIM).transpose(0, 2, 1, 3)
            q = sh(xn @ Wq.T + bq)
            k = sh(xn @ Wk.T + bk)
            v = sh(xn @ Wv.T + bv)
            scores = jnp.einsum('bhqd,bhkd->bhqk', q, k)
            r = _pos_emb(S)
            rel = jnp.einsum('bhqd,ld->bhql', q + u[None, :, None, :], r)
            scores = (scores + _rel_shift(rel, S, S)) * HEAD_DIM ** (-0.5)
            mask = jnp.arange(S)[None, :] > jnp.arange(S)[:, None]
            scores = jnp.where(mask[None, None], NEG, scores)
            p = jax.nn.softmax(scores, axis=-1)
            ctx = jnp.einsum('bhqk,bhkd->bhqd', p, v).transpose(0, 2, 1, 3).reshape(B, S, D_MODEL)
            return ctx @ Wo.T + bo
        key = jax.random.key(seed)
        ks = jax.random.split(key, 20)
        B, S = (4, 128)
        p = lambda k, shp, s=0.02: jax.random.normal(k, shp, dtype=jnp.float32) * s
        L = N_LAYER
        return {'x': jax.random.normal(ks[0], (B, S, D_MODEL), dtype=jnp.float32), 'Wq': p(ks[1], (L, D_MODEL, D_MODEL)), 'bq': jnp.zeros((L, D_MODEL)), 'Wk': p(ks[2], (L, D_MODEL, D_MODEL)), 'bk': jnp.zeros((L, D_MODEL)), 'Wv': p(ks[3], (L, D_MODEL, D_MODEL)), 'bv': jnp.zeros((L, D_MODEL)), 'Wo': p(ks[4], (L, D_MODEL, D_MODEL)), 'bo': jnp.zeros((L, D_MODEL)), 'u_bias': p(ks[5], (L, N_HEAD, HEAD_DIM), 0.02), 'W1': p(ks[6], (L, D_INNER, D_MODEL)), 'b1': jnp.zeros((L, D_INNER)), 'W2': p(ks[7], (L, D_MODEL, D_INNER)), 'b2': jnp.zeros((L, D_MODEL)), 'ln1_w': jnp.ones((L, D_MODEL)), 'ln1_b': jnp.zeros((L, D_MODEL)), 'ln2_w': jnp.ones((L, D_MODEL)), 'ln2_b': jnp.zeros((L, D_MODEL))}
    _L1_attn_in = _L1_attn_setup()

    def _L1_ffn_setup():
        import jax, jax.numpy as jnp
        import numpy as np
        HIDDEN = 128
        NUM_EXPERTS = 8
        BATCH, SEQ = (4, 512)
        key = jax.random.key(seed)
        ks = jax.random.split(key, 6)
        s = 1.0 / np.sqrt(HIDDEN)
        tokens = jax.random.normal(ks[0], (BATCH, SEQ, HIDDEN), dtype=jnp.float32)
        gate_w = jax.random.uniform(ks[1], (NUM_EXPERTS, HIDDEN), jnp.float32, -s, s)
        expert_w = jax.random.uniform(ks[2], (NUM_EXPERTS, HIDDEN, HIDDEN), jnp.float32, -s, s)
        expert_b = jax.random.uniform(ks[3], (NUM_EXPERTS, HIDDEN), jnp.float32, -s, s)
        combine_w = jax.random.uniform(ks[4], (HIDDEN, HIDDEN), jnp.float32, -s, s)
        return {'tokens': tokens, 'gate_w': gate_w, 'expert_w': expert_w, 'expert_b': expert_b, 'combine_w': combine_w}
    _L1_ffn_in = _L1_ffn_setup()

    def _L2_attn_setup():
        import jax, jax.numpy as jnp
        import numpy as np
        B, S, D = (4, 512, 128)
        H = 16
        K = D // H
        M = 32
        FF = 512
        EPS = 1e-06

        def _layernorm(x, g, b):
            mu = jnp.mean(x, axis=-1, keepdims=True)
            var = jnp.mean(jnp.square(x - mu), axis=-1, keepdims=True)
            return (x - mu) * jax.lax.rsqrt(var + EPS) * g + b

        def _phi(u, omega):
            proj = jnp.einsum('bhsk,mk->bhsm', u, omega)
            sq = 0.5 * jnp.sum(u * u, axis=-1, keepdims=True)
            stab = jnp.max(proj, axis=-1, keepdims=True)
            m = jnp.asarray(M, u.dtype)
            return jnp.exp(proj - sq - stab) / jnp.sqrt(m) + 1e-06

        def _performer_attn(x, wq, wk, wv, wo, omega):
            q = jnp.einsum('bsd,dhk->bhsk', x, wq)
            k = jnp.einsum('bsd,dhk->bhsk', x, wk)
            v = jnp.einsum('bsd,dhk->bhsk', x, wv)
            scale = jnp.asarray(K, x.dtype) ** (-0.25)
            pq = _phi(q * scale, omega)
            pk = _phi(k * scale, omega)
            kv = jnp.einsum('bhsm,bhsk->bhmk', pk, v)
            z = jnp.sum(pk, axis=2)
            num = jnp.einsum('bhsm,bhmk->bhsk', pq, kv)
            den = jnp.einsum('bhsm,bhm->bhs', pq, z)
            out = num / den[..., None]
            out = out.transpose(0, 2, 1, 3).reshape(x.shape[0], x.shape[1], H * K)
            return out @ wo
        key = jax.random.key(seed)
        ks = jax.random.split(key, 12)
        s_in = 1.0 / np.sqrt(D)
        s_ff = 1.0 / np.sqrt(FF)
        return {'x': jax.random.normal(ks[0], (B, S, D), jnp.float32), 'wq': jax.random.normal(ks[1], (D, H, K), jnp.float32) * s_in, 'wk': jax.random.normal(ks[2], (D, H, K), jnp.float32) * s_in, 'wv': jax.random.normal(ks[3], (D, H, K), jnp.float32) * s_in, 'wo': jax.random.normal(ks[4], (H * K, D), jnp.float32) * s_in, 'omega': jax.random.normal(ks[5], (M, K), jnp.float32), 'ln1_g': jnp.ones((D,), jnp.float32), 'ln1_b': jnp.zeros((D,), jnp.float32), 'w1': jax.random.normal(ks[6], (D, FF), jnp.float32) * s_in, 'b1': jnp.zeros((FF,), jnp.float32), 'w2': jax.random.normal(ks[7], (FF, D), jnp.float32) * s_ff, 'b2': jnp.zeros((D,), jnp.float32), 'ln2_g': jnp.ones((D,), jnp.float32), 'ln2_b': jnp.zeros((D,), jnp.float32)}
    _L2_attn_in = _L2_attn_setup()

    def _L2_ffn_setup():
        import jax, jax.numpy as jnp
        import numpy as np
        BLOCK = 16
        _GRID = jnp.array([0.0, 0.5, 1.0, 1.5, 2.0, 3.0, 4.0, 6.0], dtype=jnp.float32)
        _MID = jnp.array([0.25, 0.75, 1.25, 1.75, 2.5, 3.5, 5.0], dtype=jnp.float32)

        def fp4_quant_dequant(x):
            shape = x.shape
            xb = x.reshape(shape[:-1] + (shape[-1] // BLOCK, BLOCK))
            scale = jnp.max(jnp.abs(xb), axis=-1, keepdims=True) / 6.0
            scale = jnp.maximum(scale, jnp.float32(1e-12))
            xn = xb / scale
            idx = jnp.searchsorted(_MID, jnp.abs(xn))
            q = _GRID[idx] * jnp.sign(xn) * scale
            return q.reshape(shape)

        def fp4_linear(x, w):
            xq = fp4_quant_dequant(x)
            wq = fp4_quant_dequant(w)
            return jnp.einsum('bsk,nk->bsn', xq, wq)
        key = jax.random.key(seed)
        k1, k2, k3, k4 = jax.random.split(key, 4)
        H, I = (128, 352)
        x = jax.random.normal(k1, (4, 512, H), dtype=jnp.float32)
        w_gate = jax.random.normal(k2, (I, H), dtype=jnp.float32) * 0.02
        w_up = jax.random.normal(k3, (I, H), dtype=jnp.float32) * 0.02
        w_down = jax.random.normal(k4, (H, I), dtype=jnp.float32) * 0.02
        return {'x': x, 'w_gate': w_gate, 'w_up': w_up, 'w_down': w_down}
    _L2_ffn_in = _L2_ffn_setup()

    def _L3_attn_setup():
        import jax, jax.numpy as jnp
        import numpy as np
        import math
        DK = 128
        key = jax.random.key(seed)
        k1, k2 = jax.random.split(key)
        x = jax.random.normal(k1, (4, 256, 128), dtype=jnp.float32)
        W = jax.random.normal(k2, (128, 3 * DK), dtype=jnp.float32) * (1.0 / math.sqrt(128))
        b = jnp.zeros((3 * DK,), dtype=jnp.float32)
        return {'x': x, 'W': W, 'b': b}
    _L3_attn_in = _L3_attn_setup()

    def _L3_ffn_setup():
        import jax, jax.numpy as jnp
        import numpy as np
        B, T, D, R, E = (32, 128, 128, 64, 8)
        key = jax.random.key(seed)
        ks = jax.random.split(key, 12)
        inp = {}
        inp['x'] = jax.random.normal(ks[0], (B, T, D), dtype=jnp.float32)
        inp['base_W'] = jax.random.normal(ks[1], (D, D), dtype=jnp.float32) * (1.0 / np.sqrt(D))
        inp['base_b'] = jax.random.normal(ks[2], (D,), dtype=jnp.float32) * 0.01
        inp['disc_mu'] = jax.random.normal(ks[3], (E, D), dtype=jnp.float32) * 0.5
        inp['disc_sigma'] = jax.random.uniform(ks[4], (E, D), dtype=jnp.float32, minval=0.5, maxval=1.5)
        inp['down_W'] = jax.random.normal(ks[5], (E, D, R), dtype=jnp.float32) * (1.0 / np.sqrt(D))
        inp['down_b'] = jax.random.normal(ks[6], (E, R), dtype=jnp.float32) * 0.01
        inp['up_W'] = jax.random.normal(ks[7], (E, R, D), dtype=jnp.float32) * (1.0 / np.sqrt(R))
        inp['up_b'] = jax.random.normal(ks[8], (E, D), dtype=jnp.float32) * 0.01
        inp['conv_W'] = jax.random.normal(ks[9], (E, D, D), dtype=jnp.float32) * 0.02
        inp['conv_b'] = jax.random.normal(ks[10], (E, D), dtype=jnp.float32) * 0.01
        return inp
    _L3_ffn_in = _L3_ffn_setup()
    _d = {'L0_attn_x': _L0_attn_in['x'], 'L0_attn_w_in': _L0_attn_in['w_in'], 'L0_attn_b_in': _L0_attn_in['b_in'], 'L0_attn_w_out': _L0_attn_in['w_out'], 'L0_attn_b_out': _L0_attn_in['b_out'], 'L0_ffn_router_w': _L0_ffn_in['router_w'], 'L0_ffn_e_bias': _L0_ffn_in['e_bias'], 'L0_ffn_Wg': _L0_ffn_in['Wg'], 'L0_ffn_Wu': _L0_ffn_in['Wu'], 'L0_ffn_Wd': _L0_ffn_in['Wd'], 'L0_ffn_SWg': _L0_ffn_in['SWg'], 'L0_ffn_SWu': _L0_ffn_in['SWu'], 'L0_ffn_SWd': _L0_ffn_in['SWd'], 'L1_attn_Wq': _L1_attn_in['Wq'], 'L1_attn_bq': _L1_attn_in['bq'], 'L1_attn_Wk': _L1_attn_in['Wk'], 'L1_attn_bk': _L1_attn_in['bk'], 'L1_attn_Wv': _L1_attn_in['Wv'], 'L1_attn_bv': _L1_attn_in['bv'], 'L1_attn_Wo': _L1_attn_in['Wo'], 'L1_attn_bo': _L1_attn_in['bo'], 'L1_attn_u_bias': _L1_attn_in['u_bias'], 'L1_attn_W1': _L1_attn_in['W1'], 'L1_attn_b1': _L1_attn_in['b1'], 'L1_attn_W2': _L1_attn_in['W2'], 'L1_attn_b2': _L1_attn_in['b2'], 'L1_attn_ln1_w': _L1_attn_in['ln1_w'], 'L1_attn_ln1_b': _L1_attn_in['ln1_b'], 'L1_attn_ln2_w': _L1_attn_in['ln2_w'], 'L1_attn_ln2_b': _L1_attn_in['ln2_b'], 'L1_ffn_gate_w': _L1_ffn_in['gate_w'], 'L1_ffn_expert_w': _L1_ffn_in['expert_w'], 'L1_ffn_expert_b': _L1_ffn_in['expert_b'], 'L1_ffn_combine_w': _L1_ffn_in['combine_w'], 'L2_attn_wq': _L2_attn_in['wq'], 'L2_attn_wk': _L2_attn_in['wk'], 'L2_attn_wv': _L2_attn_in['wv'], 'L2_attn_wo': _L2_attn_in['wo'], 'L2_attn_omega': _L2_attn_in['omega'], 'L2_attn_ln1_g': _L2_attn_in['ln1_g'], 'L2_attn_ln1_b': _L2_attn_in['ln1_b'], 'L2_attn_w1': _L2_attn_in['w1'], 'L2_attn_b1': _L2_attn_in['b1'], 'L2_attn_w2': _L2_attn_in['w2'], 'L2_attn_b2': _L2_attn_in['b2'], 'L2_attn_ln2_g': _L2_attn_in['ln2_g'], 'L2_attn_ln2_b': _L2_attn_in['ln2_b'], 'L2_ffn_w_gate': _L2_ffn_in['w_gate'], 'L2_ffn_w_up': _L2_ffn_in['w_up'], 'L2_ffn_w_down': _L2_ffn_in['w_down'], 'L3_attn_W': _L3_attn_in['W'], 'L3_attn_b': _L3_attn_in['b'], 'L3_ffn_base_W': _L3_ffn_in['base_W'], 'L3_ffn_base_b': _L3_ffn_in['base_b'], 'L3_ffn_disc_mu': _L3_ffn_in['disc_mu'], 'L3_ffn_disc_sigma': _L3_ffn_in['disc_sigma'], 'L3_ffn_down_W': _L3_ffn_in['down_W'], 'L3_ffn_down_b': _L3_ffn_in['down_b'], 'L3_ffn_up_W': _L3_ffn_in['up_W'], 'L3_ffn_up_b': _L3_ffn_in['up_b'], 'L3_ffn_conv_W': _L3_ffn_in['conv_W'], 'L3_ffn_conv_b': _L3_ffn_in['conv_b']}
    _x0 = _d['L0_attn_x']
    _d['L0_attn_x'] = jax.random.normal(jax.random.fold_in(jax.random.key(seed), 1), (32, 256, 128), dtype=_x0.dtype)
    del _x0
    return _d

def reference(L0_attn_x, L0_attn_w_in, L0_attn_b_in, L0_attn_w_out, L0_attn_b_out, L0_ffn_router_w, L0_ffn_e_bias, L0_ffn_Wg, L0_ffn_Wu, L0_ffn_Wd, L0_ffn_SWg, L0_ffn_SWu, L0_ffn_SWd, L1_attn_Wq, L1_attn_bq, L1_attn_Wk, L1_attn_bk, L1_attn_Wv, L1_attn_bv, L1_attn_Wo, L1_attn_bo, L1_attn_u_bias, L1_attn_W1, L1_attn_b1, L1_attn_W2, L1_attn_b2, L1_attn_ln1_w, L1_attn_ln1_b, L1_attn_ln2_w, L1_attn_ln2_b, L1_ffn_gate_w, L1_ffn_expert_w, L1_ffn_expert_b, L1_ffn_combine_w, L2_attn_wq, L2_attn_wk, L2_attn_wv, L2_attn_wo, L2_attn_omega, L2_attn_ln1_g, L2_attn_ln1_b, L2_attn_w1, L2_attn_b1, L2_attn_w2, L2_attn_b2, L2_attn_ln2_g, L2_attn_ln2_b, L2_ffn_w_gate, L2_ffn_w_up, L2_ffn_w_down, L3_attn_W, L3_attn_b, L3_ffn_base_W, L3_ffn_base_b, L3_ffn_disc_mu, L3_ffn_disc_sigma, L3_ffn_down_W, L3_ffn_down_b, L3_ffn_up_W, L3_ffn_up_b, L3_ffn_conv_W, L3_ffn_conv_b):

    def _L0_attn_ref(x, w_in, b_in, w_out, b_out):
        import jax, jax.numpy as jnp
        import numpy as np
        B, S, E, H = (2, 256, 128, 16)
        bsz, slen, esz = x.shape
        hsz = esz // H
        qkv = x @ w_in.T + b_in
        q, k, v = jnp.split(qkv, 3, axis=-1)

        def to_heads(t):
            return t.reshape(bsz, slen, H, hsz).transpose(0, 2, 1, 3)
        q, k, v = (to_heads(q), to_heads(k), to_heads(v))
        scale = np.float32(1.0 / np.sqrt(hsz))
        scores = jnp.einsum('bhqd,bhkd->bhqk', q * scale, k)
        causal_bias = jnp.where(jnp.tril(jnp.ones((slen, slen), dtype=bool)), 0.0, -jnp.inf).astype(x.dtype)
        scores = scores + causal_bias
        attn = jax.nn.softmax(scores, axis=-1)
        out = jnp.einsum('bhqk,bhkd->bhqd', attn, v)
        out = out.transpose(0, 2, 1, 3).reshape(bsz, slen, esz)
        out = out @ w_out.T + b_out
        out = jnp.where(jnp.isnan(out), jnp.zeros((), out.dtype), out)
        return out

    def _L0_ffn_ref(hidden_states, router_w, e_bias, Wg, Wu, Wd, SWg, SWu, SWd):
        import jax, jax.numpy as jnp
        import numpy as np
        H = 128
        I = 64
        E = 64
        G = 8
        TOPK_GROUP = 4
        K = 8
        I_SH = 128
        SCALE = 2.5

        def _route(x, router_w, e_bias):
            T = x.shape[0]
            scores = jax.nn.sigmoid(x.astype(jnp.float32) @ router_w.T.astype(jnp.float32))
            sfc = jax.lax.stop_gradient(scores) + e_bias[None, :]
            group_scores = jax.lax.top_k(sfc.reshape(T, G, E // G), 2)[0].sum(-1)
            _, gidx = jax.lax.top_k(group_scores, TOPK_GROUP)
            gmask = jax.nn.one_hot(gidx, G, dtype=sfc.dtype).sum(1)
            smask = jnp.repeat(gmask, E // G, axis=1)
            masked = jnp.where(smask > 0, sfc, 0.0)
            _, topk_idx = jax.lax.top_k(masked, K)
            w = jnp.take_along_axis(scores, topk_idx, axis=1)
            w = w / (w.sum(-1, keepdims=True) + 1e-20)
            return (topk_idx, w * SCALE)
        orig_shape = hidden_states.shape
        x = hidden_states.reshape(-1, orig_shape[-1])
        T = x.shape[0]
        topk_idx, topk_w = _route(x, router_w, e_bias)
        coef = jnp.zeros((T, E), topk_w.dtype).at[jnp.arange(T)[:, None], topk_idx].add(topk_w)
        g = jnp.einsum('th,ehi->tei', x, Wg)
        u = jnp.einsum('th,ehi->tei', x, Wu)
        h = jax.nn.silu(g) * u * coef[:, :, None]
        moe_out = jnp.einsum('tei,eih->th', h, Wd)
        shared = jax.nn.silu(x @ SWg) * (x @ SWu) @ SWd
        return (moe_out + shared).reshape(orig_shape)

    def _L1_attn_ref(x, Wq, bq, Wk, bk, Wv, bv, Wo, bo, u_bias, W1, b1, W2, b2, ln1_w, ln1_b, ln2_w, ln2_b):
        import jax, jax.numpy as jnp
        import numpy as np
        D_MODEL = 128
        N_HEAD = 16
        HEAD_DIM = D_MODEL // N_HEAD
        D_INNER = 512
        N_LAYER = 4
        NEG = jnp.finfo(jnp.float32).min

        def _ln(x, w, b):
            m = x.mean(-1, keepdims=True)
            v = ((x - m) ** 2).mean(-1, keepdims=True)
            return (x - m) * jax.lax.rsqrt(v + 1e-06) * w + b

        def _pos_emb(k_len):
            pos = jnp.arange(k_len - 1, -1, -1, dtype=jnp.float32)
            inv = 1.0 / 10000.0 ** (jnp.arange(0, HEAD_DIM, 2, dtype=jnp.float32) / HEAD_DIM)
            s = pos[:, None] * inv[None, :]
            return jnp.concatenate([jnp.sin(s), jnp.cos(s)], axis=-1)

        def _rel_shift(x, q_len, k_len):
            B, H = (x.shape[0], x.shape[1])
            zp = jnp.zeros((B, H, q_len, 1), x.dtype)
            xp = jnp.concatenate([zp, x], axis=-1).reshape(B, H, k_len + 1, q_len)
            return xp[:, :, 1:, :].reshape(B, H, q_len, k_len)

        def _attn(xn, Wq, bq, Wk, bk, Wv, bv, Wo, bo, u):
            B, S, _ = xn.shape
            sh = lambda t: t.reshape(B, S, N_HEAD, HEAD_DIM).transpose(0, 2, 1, 3)
            q = sh(xn @ Wq.T + bq)
            k = sh(xn @ Wk.T + bk)
            v = sh(xn @ Wv.T + bv)
            scores = jnp.einsum('bhqd,bhkd->bhqk', q, k)
            r = _pos_emb(S)
            rel = jnp.einsum('bhqd,ld->bhql', q + u[None, :, None, :], r)
            scores = (scores + _rel_shift(rel, S, S)) * HEAD_DIM ** (-0.5)
            mask = jnp.arange(S)[None, :] > jnp.arange(S)[:, None]
            scores = jnp.where(mask[None, None], NEG, scores)
            p = jax.nn.softmax(scores, axis=-1)
            ctx = jnp.einsum('bhqk,bhkd->bhqd', p, v).transpose(0, 2, 1, 3).reshape(B, S, D_MODEL)
            return ctx @ Wo.T + bo
        h = x
        for l in range(N_LAYER):
            xn = _ln(h, ln1_w[l], ln1_b[l])
            a = _attn(xn, Wq[l], bq[l], Wk[l], bk[l], Wv[l], bv[l], Wo[l], bo[l], u_bias[l])
            h = h + a
            fn = _ln(h, ln2_w[l], ln2_b[l])
            ff = jax.nn.gelu(fn @ W1[l].T + b1[l], approximate=False) @ W2[l].T + b2[l]
            h = h + ff
        return h

    def _L1_ffn_ref(tokens, gate_w, expert_w, expert_b, combine_w):
        import jax, jax.numpy as jnp
        import numpy as np
        HIDDEN = 128
        NUM_EXPERTS = 8
        BATCH, SEQ = (4, 512)
        B, S, H = tokens.shape
        logits = jnp.einsum('bsh,eh->bse', tokens, gate_w)
        probs = jax.nn.softmax(logits, axis=-1)
        top2_w, top2_idx = jax.lax.top_k(probs, 2)
        flat = tokens.reshape(B * S, H)
        flat_idx = top2_idx.reshape(B * S, 2)
        flat_w = top2_w.reshape(B * S, 2)
        expert_out = jax.nn.silu(jnp.einsum('nh,edh->ned', flat, expert_w) + expert_b[None, :, :])
        gathered = jnp.take_along_axis(expert_out, flat_idx[:, :, None], axis=1)
        mixed = jnp.sum(gathered * flat_w[:, :, None], axis=1)
        out = jnp.einsum('bsh,dh->bsd', mixed.reshape(B, S, H), combine_w)
        return out

    def _L2_attn_ref(x, wq, wk, wv, wo, omega, ln1_g, ln1_b, w1, b1, w2, b2, ln2_g, ln2_b):
        import jax, jax.numpy as jnp
        import numpy as np
        B, S, D = (4, 512, 128)
        H = 16
        K = D // H
        M = 32
        FF = 512
        EPS = 1e-06

        def _layernorm(x, g, b):
            mu = jnp.mean(x, axis=-1, keepdims=True)
            var = jnp.mean(jnp.square(x - mu), axis=-1, keepdims=True)
            return (x - mu) * jax.lax.rsqrt(var + EPS) * g + b

        def _phi(u, omega):
            proj = jnp.einsum('bhsk,mk->bhsm', u, omega)
            sq = 0.5 * jnp.sum(u * u, axis=-1, keepdims=True)
            stab = jnp.max(proj, axis=-1, keepdims=True)
            m = jnp.asarray(M, u.dtype)
            return jnp.exp(proj - sq - stab) / jnp.sqrt(m) + 1e-06

        def _performer_attn(x, wq, wk, wv, wo, omega):
            q = jnp.einsum('bsd,dhk->bhsk', x, wq)
            k = jnp.einsum('bsd,dhk->bhsk', x, wk)
            v = jnp.einsum('bsd,dhk->bhsk', x, wv)
            scale = jnp.asarray(K, x.dtype) ** (-0.25)
            pq = _phi(q * scale, omega)
            pk = _phi(k * scale, omega)
            kv = jnp.einsum('bhsm,bhsk->bhmk', pk, v)
            z = jnp.sum(pk, axis=2)
            num = jnp.einsum('bhsm,bhmk->bhsk', pq, kv)
            den = jnp.einsum('bhsm,bhm->bhs', pq, z)
            out = num / den[..., None]
            out = out.transpose(0, 2, 1, 3).reshape(x.shape[0], x.shape[1], H * K)
            return out @ wo
        h = _performer_attn(x, wq, wk, wv, wo, omega)
        x = _layernorm(x + h, ln1_g, ln1_b)
        h2 = jax.nn.gelu(x @ w1 + b1, approximate=False) @ w2 + b2
        x = _layernorm(x + h2, ln2_g, ln2_b)
        return x

    def _L2_ffn_ref(x, w_gate, w_up, w_down):
        import jax, jax.numpy as jnp
        import numpy as np
        BLOCK = 16
        _GRID = jnp.array([0.0, 0.5, 1.0, 1.5, 2.0, 3.0, 4.0, 6.0], dtype=jnp.float32)
        _MID = jnp.array([0.25, 0.75, 1.25, 1.75, 2.5, 3.5, 5.0], dtype=jnp.float32)

        def fp4_quant_dequant(x):
            shape = x.shape
            xb = x.reshape(shape[:-1] + (shape[-1] // BLOCK, BLOCK))
            scale = jnp.max(jnp.abs(xb), axis=-1, keepdims=True) / 6.0
            scale = jnp.maximum(scale, jnp.float32(1e-12))
            xn = xb / scale
            idx = jnp.searchsorted(_MID, jnp.abs(xn))
            q = _GRID[idx] * jnp.sign(xn) * scale
            return q.reshape(shape)

        def fp4_linear(x, w):
            xq = fp4_quant_dequant(x)
            wq = fp4_quant_dequant(w)
            return jnp.einsum('bsk,nk->bsn', xq, wq)
        gate = fp4_linear(x, w_gate)
        y = fp4_linear(x, w_up)
        h = jax.nn.silu(gate) * y
        return fp4_linear(h, w_down)

    def _L3_attn_ref(x, W, b):
        import jax, jax.numpy as jnp
        import numpy as np
        import math
        DK = 128
        qkv = jnp.einsum('btc,cd->btd', x, W) + b
        q, k, v = jnp.split(qkv, 3, axis=-1)
        scale = 1.0 / math.sqrt(DK)
        weights = jnp.einsum('btc,bTc->btT', q, k) * scale
        T = weights.shape[-1]
        mask = jnp.tril(jnp.ones((T, T), dtype=jnp.float32))
        logits = jnp.where(mask == 0, jnp.float32(-9000000000000000.0), weights)
        attention = jax.nn.softmax(logits, axis=-1)
        values = jnp.einsum('btT,bTc->btc', attention, v)
        return values

    def _L3_ffn_ref(x, base_W, base_b, disc_mu, disc_sigma, down_W, down_b, up_W, up_b, conv_W, conv_b):
        import jax, jax.numpy as jnp
        import numpy as np
        B, T, D, R, E = (32, 128, 128, 64, 8)
        base = jnp.einsum('btd,od->bto', x, base_W) + base_b
        m1 = x.mean(axis=1)
        m2 = (x * x).mean(axis=1)
        inv_var = 1.0 / (disc_sigma * disc_sigma)
        losses = (jnp.einsum('bd,ed->eb', m2, inv_var) - 2.0 * jnp.einsum('bd,ed->eb', m1, disc_mu * inv_var) + jnp.sum(disc_mu * disc_mu * inv_var, axis=1)[:, None]) / D
        idx = jnp.argmin(losses, axis=0)
        Wd, bd = (down_W[idx], down_b[idx])
        Wu, bu = (up_W[idx], up_b[idx])
        Wc, bc = (conv_W[idx], conv_b[idx])
        h = jax.nn.relu(jnp.einsum('btd,bdr->btr', x, Wd) + bd[:, None, :])
        a = jnp.einsum('btr,brd->btd', h, Wu) + bu[:, None, :]
        y = jnp.einsum('btd,bod->bto', a, Wc) + bc[:, None, :]
        return base + y
    x = L0_attn_x
    x = x + _L0_attn_ref(_layernorm(x, axis=-1), L0_attn_w_in, L0_attn_b_in, L0_attn_w_out, L0_attn_b_out)
    x = x + _L0_ffn_ref(_layernorm(x, axis=-1), L0_ffn_router_w, L0_ffn_e_bias, L0_ffn_Wg, L0_ffn_Wu, L0_ffn_Wd, L0_ffn_SWg, L0_ffn_SWu, L0_ffn_SWd)
    x = x + _L1_attn_ref(_layernorm(x, axis=-1), L1_attn_Wq, L1_attn_bq, L1_attn_Wk, L1_attn_bk, L1_attn_Wv, L1_attn_bv, L1_attn_Wo, L1_attn_bo, L1_attn_u_bias, L1_attn_W1, L1_attn_b1, L1_attn_W2, L1_attn_b2, L1_attn_ln1_w, L1_attn_ln1_b, L1_attn_ln2_w, L1_attn_ln2_b)
    x = x + _L1_ffn_ref(_layernorm(x, axis=-1), L1_ffn_gate_w, L1_ffn_expert_w, L1_ffn_expert_b, L1_ffn_combine_w)
    x = x + _L2_attn_ref(_layernorm(x, axis=-1), L2_attn_wq, L2_attn_wk, L2_attn_wv, L2_attn_wo, L2_attn_omega, L2_attn_ln1_g, L2_attn_ln1_b, L2_attn_w1, L2_attn_b1, L2_attn_w2, L2_attn_b2, L2_attn_ln2_g, L2_attn_ln2_b)
    x = x + _L2_ffn_ref(_layernorm(x, axis=-1), L2_ffn_w_gate, L2_ffn_w_up, L2_ffn_w_down)
    x = x + _L3_attn_ref(_layernorm(x, axis=-1), L3_attn_W, L3_attn_b)
    x = x + _L3_ffn_ref(_layernorm(x, axis=-1), L3_ffn_base_W, L3_ffn_base_b, L3_ffn_disc_mu, L3_ffn_disc_sigma, L3_ffn_down_W, L3_ffn_down_b, L3_ffn_up_W, L3_ffn_up_b, L3_ffn_conv_W, L3_ffn_conv_b)
    return x

_drawn_inputs = setup_inputs


def setup_inputs(seed=0):
    import zlib

    import numpy as np

    out = dict(_drawn_inputs(seed))
    spreads = {'L0_attn_b_in': (0.0, 0.1),
     'L0_attn_b_out': (0.0, 0.1),
     'L0_ffn_e_bias': (0.0, 0.8),
     'L1_attn_bq': (0.0, 0.8),
     'L1_attn_bk': (0.0, 2.0),
     'L1_attn_bv': (0.0, 0.279),
     'L1_attn_bo': (0.0, 0.1),
     'L1_attn_b1': (0.0, 0.275),
     'L1_attn_b2': (0.0, 0.1),
     'L1_attn_ln1_w': (1.0, 0.6),
     'L1_attn_ln1_b': (0.0, 0.445),
     'L1_attn_ln2_w': (1.0, 0.6),
     'L1_attn_ln2_b': (0.0, 0.448),
     'L2_attn_ln1_g': (1.0, 0.2),
     'L2_attn_ln1_b': (0.0, 0.1),
     'L2_attn_b1': (0.0, 0.37),
     'L2_attn_b2': (0.0, 0.1),
     'L2_attn_ln2_g': (1.0, 0.2),
     'L2_attn_ln2_b': (0.0, 0.1),
     'L3_attn_b': (0.0, 0.719)}
    factors = {'L0_ffn_router_w': 8.0,
     'L0_ffn_Wg': 8.0,
     'L0_ffn_Wu': 8.0,
     'L0_ffn_Wd': 8.0,
     'L0_ffn_SWg': 8.0,
     'L0_ffn_SWu': 8.0,
     'L0_ffn_SWd': 8.0,
     'L1_attn_Wq': 8.0,
     'L1_attn_Wk': 8.0,
     'L1_attn_u_bias': 8.0,
     'L1_ffn_expert_b': 8.0,
     'L2_ffn_w_gate': 8.0,
     'L2_ffn_w_up': 8.0,
     'L2_ffn_w_down': 8.0,
     'L3_ffn_base_b': 53.208,
     'L3_ffn_down_b': 64.0,
     'L3_ffn_up_b': 64.0,
     'L3_ffn_conv_b': 59.335,
     'L3_ffn_disc_mu': 2.982,
     'L3_ffn_down_W': 3.981,
     'L3_ffn_up_W': 3.268,
     'L3_ffn_conv_W': 3.152}
    for name, (base, spread) in spreads.items():
        noise = np.random.default_rng([zlib.crc32(name.encode()), seed]).standard_normal(out[name].shape)
        drawn = base * np.exp(spread * noise) if base else spread * noise
        out[name] = jnp.asarray(drawn.astype(out[name].dtype))
    for name, factor in factors.items():
        out[name] = (out[name] * factor).astype(out[name].dtype)
    return out
```

```python
import math

import concourse.bass as bass
from concourse import mybir
from contextlib import ExitStack

F32, BF16, I32 = mybir.dt.float32, mybir.dt.bfloat16, mybir.dt.int32
ALU = mybir.AluOpType
ACT = mybir.ActivationFunctionType
AX = mybir.AxisListType

P = 128
D = 128
SEQS, SEQ = 32, 256
TILES = SEQS * SEQ // P
QT = SEQ // P
BLK = 512
BT = BLK // P
BLOCKS = TILES // BT
HEADS, HD = 16, 8
GROUPS, GH = 4, 4
NEG = -1.0e30


class Chain:

    def __init__(self, eng):
        self.eng = eng

    def link(self, ins):
        self.eng.drain()


def rows(buf, first, count):
    return buf[:, bass.ds(first, count), :]


def ln_stats(v, chain, src, stats, moments, done):
    nt = src.shape[1]
    for t in range(nt):
        ins = v.bn_stats(stats[:, t, :], src[:, t, :])
    chain.link(ins)
    for t in range(nt):
        ins = v.bn_aggr(moments[:, t, :], stats[:, t, :])
    ins.then_inc(done, 1)


def ln_rstd(g, chain, moments, veps, minus_half, rstd, eps, done, apart):
    nt = rstd.shape[1]
    g.sem_inc(apart, 1)
    chain.link(g.tensor_scalar_add(veps[:, 0:nt], moments[:, 0:nt, 1], eps))
    g.tensor_tensor(rstd[:, 0:nt], veps[:, 0:nt], minus_half[:, 0:nt], op=ALU.pow).then_inc(done, 1)


def ln_apply(v, src, moments, rstd, xn):
    for t in range(src.shape[1]):
        ins = v.tensor_scalar(xn[:, t, :], src[:, t, :], moments[:, t, 0:1], rstd[:, t:t + 1],
                              ALU.subtract, ALU.mult)
    return ins


class Held:

    def __init__(self, nc, stack, tag):
        self.nc, self.stack, self.tag, self.sems = nc, stack, tag, []

    def sb(self, name, shape, dt=F32):
        return self.stack.enter_context(self.nc.sbuf_tensor(self.tag + name, shape, dt))

    def ps(self, name, shape, dt=F32):
        return self.stack.enter_context(self.nc.psum_tensor(self.tag + name, shape, dt))

    def sem(self, names):
        made = [self.stack.enter_context(self.nc.semaphore(self.tag + n)) for n in names.split()]
        self.sems += made
        return made if len(made) > 1 else made[0]

    def clear(self):
        for s in self.sems:
            self.nc.gpsimd.sem_clear(s)
        self.nc.all_engine_barrier()


def rounds(eng, step, count, behind=False):
    step(-1, True, False, False)
    step(0, True, True, False)
    with eng.Fori(0, count - 2) as i:
        step(i + 1, True, True, behind)
    step(count - 1, False, True, behind)
    if behind:
        step(count, False, False, True)


def later(n, least):
    return not isinstance(n, int) or n >= least

QPART = [0, 1, 2, 0, 1, 0]
KPART = [0, 0, 0, 1, 1, 2]


def attention(nc, core, tag, store, eps, w, rel, layer=None):
    NS = 3 if rel else 2
    K = 96 if rel else 48
    READS = 6 * NS
    W_IN = 16 * (14 if rel else 8)
    SCALE = float(HD) ** -0.5
    with ExitStack() as held:
        def sb(name, shape, dt=F32):
            return held.enter_context(nc.sbuf_tensor(tag + name, shape, dt))

        def ps(name, shape, dt=F32):
            return held.enter_context(nc.psum_tensor(tag + name, shape, dt))

        sems = []

        def sem(name):
            s = held.enter_context(nc.semaphore(tag + name))
            sems.append(s)
            return s

        wq = sb("wq", [P, 3 * D]); wo = sb("wo", [P, D])
        bqk = sb("bqk", [P, 2]); bv = sb("bv", [1, D]); bo = sb("bo", [1, D])
        ones1 = sb("ones1", [1, P])
        mhalf = sb("mhalf", [P, QT])
        maskq = sb("maskq", [P, P], BF16); maskk = sb("maskk", [P, P], BF16)
        esel = sb("esel", [32, HEADS, P], BF16)
        stats = sb("stats", [P, QT, 6]); moments = sb("moments", [P, QT, 2])
        veps = sb("veps", [P, QT]); rstd = sb("rstd", [P, QT])
        xn = sb("xn", [P, QT, D]); xnT = [sb(f"xnT{b}", [P, SEQ]) for b in range(2)]
        f32s = sb("f32s", [P, NS, SEQ]); rest = sb("rest", [P, NS, SEQ])
        parts = [sb(f"parts{b}", [P, NS, 3, SEQ], BF16) for b in range(2)]
        sq = [sb(f"sq{b}", [K, HEADS, SEQ], BF16) for b in range(2)]
        sk = [sb(f"sk{b}", [K, HEADS, SEQ], BF16) for b in range(2)]
        vaug = [sb(f"vaug{b}", [P, QT, HEADS, 32]) for b in range(2)]
        mx = sb("mx", [P, QT, HEADS]); mrest = sb("mrest", [P, QT, HEADS])
        mparts = sb("mparts", [P, QT, 2, HEADS], BF16)
        mT = sb("mT", [32, SEQ], BF16)
        prob = [sb(f"prob{b}", [P, 3 * BLK]) for b in range(2)]
        ctxp = [sb(f"ctxp{b}", [P, GROUPS, SEQ]) for b in range(2)]
        rec = sb("rec", [P, QT, HEADS]); cn = sb("cn", [P, QT, D]); cT = sb("cT", [P, SEQ])
        if rel:
            lnw = sb("lnw", [P, 2]); u12 = sb("u12", [P, 2 * D])
            b12 = sb("b12", [P, 4]); b12s = sb("b12s", [P, 2])
            turn = sb("turn", [P, 2, SEQ]); u1 = sb("u1", [P, SEQ]); u2 = sb("u2", [P, SEQ])
        else:
            guard = sb("guard", [P, QT, D]); isnum = sb("isnum", [P, QT, D], I32)
            zeros = sb("zeros", [P, QT, D])
            osb = sb("osb", [P, QT, D])
        scratch = [nc.dram_tensor(f"{tag}scratch{b}", (NS, 3, P, SEQ), BF16).ap() for b in range(2)]

        slot = [ps(f"slot{b}", [P, 3 * BLK]) for b in range(2)]
        ring = ps("ring", [P, BLK])
        pctx = ps("pctx", [P, BLK])
        bank = [slot[0][:, 0:BLK], slot[0][:, BLK:2 * BLK], slot[0][:, 2 * BLK:3 * BLK],
                slot[1][:, 0:BLK], slot[1][:, BLK:2 * BLK], slot[1][:, 2 * BLK:3 * BLK]]
        AT = dict(T=ring[:, 0:SEQ], C0=bank[0], C1=bank[1], Q=bank[2][:, 0:SEQ], K=ring[:, 0:SEQ],
                  V=bank[3][:, 0:SEQ], U1=bank[4][:, 0:SEQ], U2=bank[5][:, 0:SEQ],
                  M=ring[:, 0:P].bitcast(BF16)[0:32, :], CT=pctx[:, 0:SEQ], OP=pctx[:, 0:SEQ])

        (w_in, setup, stats_done, rstd_done, xn_done, xnT_done, first_pe, v_pe, max_pe, out_pe, q_taken, k_taken, v_taken,
         u_taken, f32_done, parts_done, wrote0, wrote1, stack0, stack1, slot_pe, mx_done,
         mp_done, mT_done, exp_done, pv_done, ctx_taken, c_taken, cT_done, op_taken, apart,
         ) = [sem(x) for x in (
             "w_in setup stats_done rstd_done xn_done xnT_done first_pe v_pe max_pe out_pe q_taken k_taken v_taken u_taken "
             "f32_done parts_done wrote0 wrote1 stack0 stack1 slot_pe mx_done mp_done mT_done "
             "exp_done pv_done ctx_taken c_taken cT_done op_taken apart").split()]
        wrote, stack = [wrote0, wrote1], [stack0, stack1]
        S1 = ["T", "Q", "K"] + (["U1", "U2"] if rel else [])
        S3 = ["C0", "C1", "CT", "OP"]

        def first(m, name):
            return m * len(S1) + S1.index(name) + 1

        def last(o, name):
            return o * len(S3) + S3.index(name) + 1

        def every_round(eng, step):
            step(-2, 0, -1, True, False, False, False)
            step(-1, 1, -1, True, True, False, False)
            step(0, 0, 0, True, True, True, False)
            with eng.Fori(0, (SEQS - 4) // 2) as i:
                step(i * 2 + 1, 1, i, True, True, True, True)
                step(i * 2 + 2, 0, i + 1, True, True, True, True)
            step(SEQS - 3, 1, SEQS // 2 - 2, True, True, True, True)
            step(SEQS - 2, 0, SEQS // 2 - 1, False, True, True, True)
            step(SEQS - 1, 1, SEQS // 2 - 1, False, False, True, True)
            step(SEQS, 0, SEQS // 2, False, False, False, True)

        with nc.Block() as block:
            @block.sync
            def _(sp):
                loads = [(wq, w["wq"]), (wo, w["wo"]), (bqk, w["bqk"]), (bv, w["bv"]), (bo, w["bo"])]
                if rel:
                    loads += [(lnw, w["lnw"]), (u12, w["u12"]), (b12, w["b12"])]
                for dst, src in loads:
                    sp.dma_start(dst[:, :], src if layer is None else src[layer]).then_inc(w_in, 16)
                sp.dma_start(maskq[:, :], core["maskq"]).then_inc(w_in, 16)
                sp.dma_start(maskk[:, :], core["maskk"]).then_inc(w_in, 16)
                sp.dma_start(esel[:, :, :], core["esel"]).then_inc(w_in, 16)
                if rel:
                    sp.dma_start(turn[:, :, :], core["turn"]).then_inc(w_in, 16)
                    for b in range(2):
                        sp.dma_start(sk[b][48:96, :, :], core["kturn"].unsqueeze(1).broadcast_to((48, HEADS, SEQ))
                                     ).then_inc(w_in, 16)

                def step(n, b, half, qk, val, att, outp):
                    if not qk:
                        return
                    m = n + 2
                    sp.wait_ge(parts_done, m + 1)
                    if not isinstance(m, int) or m >= 2:
                        sp.wait_ge(pv_done, (m - 1) * GROUPS)
                    sp.dma_start(scratch[b].rearrange("c s p t -> p (c s) t"),
                                 parts[b][:, :, :, :].rearrange("p c s t -> p (c s) t")).then_inc(wrote[b], 16)
                    sp.wait_ge(wrote[b], (half + 2) * 16)
                    for c in range(6):
                        for comp, dst, part in ((0, sq[b], QPART[c]), (1, sk[b], KPART[c]),
                                                (2, sq[b], QPART[c]))[:NS]:
                            lo = c * HD + (48 if comp == 2 else 0)
                            sp.dma_start(dst[lo:lo + HD, :, :],
                                         scratch[b][comp, part].rearrange("(h r) t -> r h t", r=HD)
                                         ).then_inc(stack[b], 16)
                every_round(sp, step)

            @block.gpsimd
            def _(g):
                chain = Chain(g)
                g.memset(mhalf[:, :], -0.5).then_inc(setup, 1)
                g.memset(ones1[:, :], 1.0).then_inc(setup, 1)
                for b in range(2):
                    g.memset(vaug[b][:, :, :, HD:32], 0.0).then_inc(setup, 1)
                g.wait_ge(setup, 4)
                for b in range(2):
                    g.memset(vaug[b][:, :, :, HD:HD + 1], 1.0).then_inc(setup, 1)
                if not rel:
                    g.memset(zeros[:, :, :], 0.0).then_inc(setup, 1)
                else:
                    g.wait_ge(w_in, W_IN)
                    g.tensor_tensor(b12s[:, :], b12[:, 0:2], b12[:, 2:4], op=ALU.add).then_inc(setup, 1)
                g.wait_ge(setup, 7)

                def step(n, b, half, qk, val, att, outp):
                    if not qk:
                        return
                    m = n + 2
                    g.wait_ge(stats_done, m + 1)
                    ln_rstd(g, chain, moments, veps, mhalf, rstd, eps, rstd_done, apart)
                    g.wait_ge(q_taken, m + 1)
                    g.wait_ge(k_taken, m + 1)
                    if rel:
                        g.wait_ge(f32_done, m + 1)
                    if not isinstance(m, int) or m >= 2:
                        g.wait_ge(wrote[b], (half + 1) * 16)
                    g.sem_inc(apart, 1)
                    pt = parts[b]
                    chain.link(g.tensor_copy(pt[:, :, 0, :], f32s[:, :, :]))
                    chain.link(g.tensor_tensor(rest[:, :, :], f32s[:, :, :], pt[:, :, 0, :], op=ALU.subtract))
                    chain.link(g.tensor_copy(pt[:, :, 1, :], rest[:, :, :]))
                    g.tensor_tensor(pt[:, :, 2, :], rest[:, :, :], pt[:, :, 1, :], op=ALU.subtract
                                    ).then_inc(parts_done, 1)
                every_round(g, step)

            @block.vector
            def _(v):
                chain = Chain(v)
                v.wait_ge(w_in, W_IN)
                v.wait_ge(setup, 7)

                def step(n, b, half, qk, val, att, outp):
                    m, o = n + 2, n - 1
                    v.drain()
                    if qk:
                        src = rows(store, m * QT, QT)
                        ln_stats(v, chain, src, stats, moments, stats_done)
                        v.wait_ge(rstd_done, m + 1)
                        if not isinstance(m, int) or m >= 1:
                            v.wait_ge(xnT_done, m)
                        ln_apply(v, src, moments, rstd, xn).then_inc(xn_done, 1)
                    if att:
                        for gr in range(GROUPS):
                            v.wait_ge(slot_pe, n * 8 + gr + 1)
                            sl = slot[gr % 2]
                            for t in range(QT):
                                w_ = P * (t + 1)
                                src = (sl[:, 0:BLK] if t == 0 else sl[:, BLK:3 * BLK]).rearrange(
                                    "p (h k) -> p h k", k=w_)
                                ins = v.tensor_reduce(mx[:, t, gr * GH:(gr + 1) * GH], src, op=ALU.max,
                                                      axis=AX.X, negate=True)
                            ins.then_inc(mx_done, 1)
                        v.wait_ge(mx_done, n * 4 + 4)
                        if not isinstance(n, int) or n >= 1:
                            v.wait_ge(mT_done, n)
                        chain.link(v.tensor_copy(mparts[:, :, 0, :], mx[:, :, :]))
                        v.tensor_tensor(mparts[:, :, 1, :], mx[:, :, :], mparts[:, :, 0, :],
                                        op=ALU.subtract).then_inc(mp_done, 1)
                    if outp:
                        for t in range(QT):
                            v.wait_ge(out_pe, last(o, "C%d" % t))
                            src = AT["C%d" % t].rearrange("p (h e) -> p h e", e=32)
                            chain.link(v.reciprocal(rec[:, t, :].unsqueeze(2), src[:, :, HD:HD + 1]))
                            v.tensor_tensor(cn[:, t, :].rearrange("p (h e) -> p h e", e=HD),
                                            src[:, :, 0:HD], rec[:, t, :].unsqueeze(2).broadcast_to((P, HEADS, HD)),
                                            op=ALU.mult).then_inc(c_taken, 1)
                    if qk and rel:
                        v.wait_ge(first_pe, first(m, "U1"))
                        v.scalar_tensor_tensor(out=u1[:, :], in0=AT["U1"], scalar=b12s[:, 0:1],
                                               in1=turn[:, 0, :], op0=ALU.add, op1=ALU.mult).then_inc(u_taken, 1)
                        v.wait_ge(first_pe, first(m, "U2"))
                        v.scalar_tensor_tensor(out=u2[:, :], in0=AT["U2"], scalar=b12s[:, 1:2],
                                               in1=turn[:, 1, :], op0=ALU.add, op1=ALU.mult).then_inc(u_taken, 1)
                        v.wait_ge(u_taken, m * 2 + 2)
                        if not isinstance(m, int) or m >= 1:
                            v.wait_ge(parts_done, m)
                        v.tensor_tensor(f32s[:, 2, :], u1[:, :], u2[:, :], op=ALU.add).then_inc(f32_done, 1)
                    if outp:
                        v.wait_ge(out_pe, last(o, "OP"))
                        dst = rows(store, o * QT, QT)
                        got = AT["OP"].rearrange("p (t d) -> p t d", d=D)
                        if rel:
                            v.tensor_tensor(dst, got, dst, op=ALU.add).then_inc(op_taken, 1)
                        else:
                            chain.link(v.tensor_copy(osb[:, :, :], got))
                            chain.link(v.tensor_tensor(isnum[:, :, :], osb[:, :, :], osb[:, :, :], op=ALU.is_equal))
                            chain.link(v.tensor_copy(guard[:, :, :], zeros[:, :, :]))
                            chain.link(v.copy_predicated(guard[:, :, :], isnum[:, :, :], osb[:, :, :]))
                            v.tensor_tensor(dst, guard[:, :, :], dst, op=ALU.add).then_inc(op_taken, 1)
                every_round(v, step)

            @block.scalar
            def _(act):
                act.wait_ge(w_in, W_IN)
                act.wait_ge(setup, 7)

                def step(n, b, half, qk, val, att, outp):
                    m, vb, o = n + 2, 1 - b, n - 1
                    if qk:
                        act.wait_ge(first_pe, first(m, "T"))
                        if not isinstance(m, int) or m >= 2:
                            act.wait_ge(v_pe, m - 1)
                        if rel:
                            act.activation(xnT[b][:, :], AT["T"], ACT.Identity, bias=lnw[:, 1:2],
                                           scale=lnw[:, 0:1]).then_inc(xnT_done, 1)
                        else:
                            act.activation(xnT[b][:, :], AT["T"], ACT.Copy).then_inc(xnT_done, 1)
                        if not isinstance(m, int) or m >= 1:
                            act.wait_ge(parts_done, m)
                        act.wait_ge(first_pe, first(m, "Q"))
                        act.activation(f32s[:, 0, :], AT["Q"], ACT.Identity, bias=bqk[:, 0:1]
                                       ).then_inc(q_taken, 1)
                        act.wait_ge(first_pe, first(m, "K"))
                        act.activation(f32s[:, 1, :], AT["K"], ACT.Identity, bias=bqk[:, 1:2]
                                       ).then_inc(k_taken, 1)
                    if val:
                        act.wait_ge(v_pe, n + 2)
                        act.activation(vaug[vb][:, :, :, 0:HD],
                                       AT["V"].rearrange("p (t h e) -> p t h e", t=QT, e=HD),
                                       ACT.Copy).then_inc(v_taken, 1)
                    if att:
                        act.wait_ge(max_pe, n + 1)
                        act.activation(mT[:, :], AT["M"], ACT.Copy).then_inc(mT_done, 1)
                    if outp:
                        act.wait_ge(out_pe, last(o, "CT"))
                        act.activation(cT[:, :], AT["CT"], ACT.Copy).then_inc(cT_done, 1)
                    if att:
                        def exps(gr):
                            act.wait_ge(slot_pe, n * 8 + 4 + gr + 1)
                            if gr >= 2 or not isinstance(n, int) or n >= 1:
                                act.wait_ge(pv_done, n * 4 + gr - 1)
                            act.activation(prob[gr % 2][:, :], slot[gr % 2][:, :], ACT.Exp, scale=SCALE
                                           ).then_inc(exp_done, 1)

                        def take(gr):
                            act.wait_ge(pv_done, n * 4 + gr + 1)
                            act.activation(ctxp[b][:, gr, :], pctx[:, 0:SEQ], ACT.Copy).then_inc(ctx_taken, 1)
                        exps(0)
                        exps(1)
                        take(0)
                        exps(2)
                        take(1)
                        exps(3)
                        take(2)
                        take(3)
                every_round(act, step)

            @block.tensor
            def _(pe):
                pe.wait_ge(w_in, W_IN)
                pe.wait_ge(setup, 7)
                ident, identb = core["ident"], core["identb"]

                def step(n, b, half, qk, val, att, outp):
                    m, vb, o, ob = n + 2, 1 - b, n - 1, 1 - b
                    known = isinstance(n, int)

                    def project(name, lhs):
                        pe.matmul(AT[name], lhs, xnT[b][:, :], start=True, stop=True
                                  ).then_inc(first_pe, 1)

                    def maxima(gr):
                        sl = slot[gr % 2]
                        if gr >= 2:
                            pe.wait_ge(mx_done, n * 4 + gr - 1)
                        for t in range(QT):
                            w_ = P * (t + 1)
                            for j in range(GH):
                                h = gr * GH + j
                                base = (0 if t == 0 else BLK) + j * w_
                                pe.matmul(sl[:, base:base + w_], sq[b][0:K, h, t * P:(t + 1) * P],
                                          sk[b][0:K, h, 0:w_], start=True, stop=False)
                                ins = pe.matmul(sl[:, base + w_ - P:base + w_], identb, maskq[:, :],
                                                start=False, stop=True)
                        ins.then_inc(slot_pe, 1)

                    def scores(gr):
                        sl = slot[gr % 2]
                        if gr >= 2:
                            pe.wait_ge(exp_done, n * 4 + gr - 1)
                        for t in range(QT):
                            w_ = SEQ - P * t
                            for j in range(GH):
                                h = gr * GH + j
                                base = (0 if t == 0 else 2 * BLK) + j * w_
                                pe.matmul(sl[:, base:base + w_], esel[:, h, :], mT[:, t * P:SEQ],
                                          start=True, stop=False)
                                pe.matmul(sl[:, base:base + w_], sk[b][0:K, h, t * P:(t + 1) * P],
                                          sq[b][0:K, h, t * P:SEQ], start=False, stop=False)
                                ins = pe.matmul(sl[:, base:base + P], identb, maskk[:, :], start=False, stop=True)
                        ins.then_inc(slot_pe, 1)

                    def values(gr):
                        pe.wait_ge(exp_done, n * 4 + gr + 1)
                        if gr >= 1:
                            pe.wait_ge(ctx_taken, n * 4 + gr)
                        elif outp:
                            pe.wait_ge(op_taken, o + 1)
                        pb = prob[gr % 2]
                        for j in range(GH):
                            h = gr * GH + j
                            out = pctx[32 * j:32 * j + 32, 0:SEQ]
                            pe.matmul(out, vaug[b][:, 0, h, :], pb[:, j * SEQ:(j + 1) * SEQ],
                                      start=True, stop=False)
                            ins = pe.matmul(out[:, P:SEQ], vaug[b][:, 1, h, :],
                                            pb[:, 2 * BLK + j * P:2 * BLK + (j + 1) * P], start=False, stop=True)
                        ins.then_inc(pv_done, 1)

                    if att:
                        pe.wait_ge(stack[b], (half + 1) * 16 * READS)
                        if known and n == 0:
                            pe.wait_ge(q_taken, 2)
                        maxima(0)
                        if known and n == 0:
                            pe.wait_ge(v_taken, 1)
                            if rel:
                                pe.wait_ge(u_taken, 4)
                        maxima(1)
                    if qk:
                        pe.wait_ge(xn_done, m + 1)
                        if not known or m >= 1:
                            pe.wait_ge(k_taken, m)
                        for t in range(QT):
                            ins = pe.transpose(AT["T"][:, t * P:(t + 1) * P], xn[:, t, :], ident)
                        ins.then_inc(first_pe, 1)
                    if att:
                        maxima(2)
                        maxima(3)
                        pe.wait_ge(mx_done, n * 4 + 3)
                    if outp:
                        pe.wait_ge(ctx_taken, o * 4 + 4)
                        for t in range(QT):
                            for gr in range(GROUPS):
                                ins = pe.transpose(AT["C%d" % t][:, gr * P:(gr + 1) * P],
                                                   ctxp[ob][:, gr, t * P:(t + 1) * P], ident)
                            ins.then_inc(out_pe, 1)
                    if qk:
                        pe.wait_ge(xnT_done, m + 1)
                        project("Q", wq[:, 0:D])
                        project("K", wq[:, D:2 * D])
                    if att:
                        pe.wait_ge(mx_done, n * 4 + 4)
                    if val:
                        for t in range(QT):
                            out = AT["V"][:, t * D:(t + 1) * D]
                            pe.matmul(out, xnT[vb][:, t * P:(t + 1) * P], wq[:, 2 * D:3 * D], start=True, stop=False)
                            ins = pe.matmul(out, ones1[:, :], bv[:, :], start=False, stop=True)
                        ins.then_inc(v_pe, 1)
                    if qk:
                        if rel:
                            if known and m == 1:
                                pe.wait_ge(u_taken, 2)
                            project("U1", u12[:, 0:D])
                            project("U2", u12[:, D:2 * D])
                    if att:
                        pe.wait_ge(mp_done, n + 1)
                        if qk:
                            pe.wait_ge(k_taken, m + 1)
                        for t in range(QT):
                            ins = pe.transpose(AT["M"][:, t * P:(t + 1) * P],
                                               mparts[:, t, :, :].rearrange("p c h -> p (c h)"), identb)
                        ins.then_inc(max_pe, 1)
                    if outp:
                        pe.wait_ge(c_taken, o * 2 + 2)
                        for t in range(QT):
                            ins = pe.transpose(AT["CT"][:, t * P:(t + 1) * P], cn[:, t, :], ident)
                        ins.then_inc(out_pe, 1)
                        pe.wait_ge(cT_done, o + 1)
                        for t in range(QT):
                            out = AT["OP"][:, t * D:(t + 1) * D]
                            pe.matmul(out, cT[:, t * P:(t + 1) * P], wo[:, :], start=True, stop=False)
                            ins = pe.matmul(out, ones1[:, :], bo[:, :], start=False, stop=True)
                        ins.then_inc(out_pe, 1)
                    if att:
                        pe.wait_ge(mT_done, n + 1)
                        if qk:
                            pe.wait_ge(q_taken, m + 1)
                        scores(0)
                        if val:
                            pe.wait_ge(v_taken, n + 2)
                        if qk and rel:
                            pe.wait_ge(u_taken, m * 2 + 2)
                        scores(1)
                        values(0)
                        scores(2)
                        values(1)
                        scores(3)
                        values(2)
                        values(3)
                every_round(pe, step)
        for s in sems:
            nc.gpsimd.sem_clear(s)
        nc.all_engine_barrier()

def feed_forward(nc, core, tag, store, eps, w, add_to_store, layer=None):
    CH = 4
    with ExitStack() as stack:
        k = Held(nc, stack, tag)
        w1 = k.sb("w1", [P, CH * P]); w2 = k.sb("w2", [P, CH, D])
        lnw = k.sb("lnw", [P, 2]); b1 = k.sb("b1", [P, CH]); b2 = k.sb("b2", [P, 1])
        stats = k.sb("stats", [P, BT, 6]); moments = k.sb("moments", [P, BT, 2])
        veps = k.sb("veps", [P, BT]); rstd = k.sb("rstd", [P, BT]); mhalf = k.sb("mhalf", [P, BT])
        xn = k.sb("xn", [P, BT, D]); xnT = k.sb("xnT", [P, BLK])
        act_out = k.sb("act_out", [P, CH, BLK]); oT = k.sb("oT", [P, BLK])
        pT = k.ps("pT", [P, BLK]); pH = [k.ps(f"pH{c}", [P, BLK]) for c in range(CH)]
        pO = k.ps("pO", [P, BLK]); pR = k.ps("pR", [P, BLK])
        (w_in, setup, apart, stats_done, rstd_done, xn_done, t_pe, xnT_done, h_pe, gelu_done, o_pe, o_done,
         r_pe, r_taken) = k.sem("w_in setup apart stats_done rstd_done xn_done t_pe xnT_done h_pe gelu_done "
                                "o_pe o_done r_pe r_taken")
        W_IN = 16 * 5

        with nc.Block() as block:
            @block.sync
            def _(sp):
                for dst, name in ((w1[:, :], "w1"), (w2[:, :, :], "w2"), (lnw[:, :], "ln"), (b1[:, :], "b1"),
                                  (b2[:, :], "b2")):
                    sp.dma_start(dst, w[name] if layer is None else w[name][layer]).then_inc(w_in, 16)

            @block.gpsimd
            def _(g):
                chain = Chain(g)
                g.memset(mhalf[:, :], -0.5).then_inc(setup, 1)
                g.wait_ge(setup, 1)

                def step(n, ahead, now, back):
                    if ahead:
                        g.wait_ge(stats_done, n + 2)
                        ln_rstd(g, chain, moments, veps, mhalf, rstd, eps, rstd_done, apart)
                rounds(g, step, BLOCKS)

            @block.vector
            def _(v):
                chain = Chain(v)

                def step(n, ahead, now, back):
                    if ahead:
                        m = n + 1
                        src = rows(store, m * BT, BT)
                        v.drain()
                        ln_stats(v, chain, src, stats, moments, stats_done)
                        v.wait_ge(rstd_done, m + 1)
                        if later(m, 1):
                            v.wait_ge(xnT_done, m)
                        ln_apply(v, src, moments, rstd, xn).then_inc(xn_done, 1)
                    if now:
                        v.wait_ge(r_pe, n + 1)
                        dst = rows(store, n * BT, BT)
                        got = pR[:, :].rearrange("p (t d) -> p t d", d=D)
                        if add_to_store:
                            v.tensor_tensor(dst, got, dst, op=ALU.add).then_inc(r_taken, 1)
                        else:
                            v.tensor_copy(dst, got).then_inc(r_taken, 1)
                rounds(v, step, BLOCKS)

            @block.scalar
            def _(act):
                act.wait_ge(w_in, W_IN)

                def step(n, ahead, now, back):
                    if now:
                        for c in range(CH):
                            act.wait_ge(h_pe, n * CH + c + 1)
                            act.activation(act_out[:, c, :], pH[c][:, :], ACT.Gelu, bias=b1[:, c:c + 1]
                                           ).then_inc(gelu_done, 1)
                    if ahead:
                        act.wait_ge(t_pe, n + 2)
                        act.activation(xnT[:, :], pT[:, :], ACT.Identity, bias=lnw[:, 1:2], scale=lnw[:, 0:1]
                                       ).then_inc(xnT_done, 1)
                    if now:
                        act.wait_ge(o_pe, n + 1)
                        if later(n, 1):
                            act.wait_ge(r_pe, n)
                        act.activation(oT[:, :], pO[:, :], ACT.Identity, bias=b2[:, 0:1]).then_inc(o_done, 1)
                rounds(act, step, BLOCKS)

            @block.tensor
            def _(pe):
                pe.wait_ge(w_in, W_IN)

                def step(n, ahead, now, back):
                    if now:
                        pe.wait_ge(xnT_done, n + 1)
                        for c in range(CH):
                            pe.matmul(pH[c][:, :], w1[:, c * P:(c + 1) * P], xnT[:, :], start=True, stop=True
                                      ).then_inc(h_pe, 1)
                        if not add_to_store:
                            pe.matmul(pO[:, :], core["ident"], xnT[:, :], start=True, stop=False)
                    if ahead:
                        pe.wait_ge(xn_done, n + 2)
                        for t in range(BT):
                            ins = pe.transpose(pT[:, t * P:(t + 1) * P], xn[:, t, :], core["ident"])
                        ins.then_inc(t_pe, 1)
                    if now:
                        for c in range(CH):
                            pe.wait_ge(gelu_done, n * CH + c + 1)
                            ins = pe.matmul(pO[:, :], w2[:, c, :], act_out[:, c, :],
                                            start=(c == 0 and add_to_store), stop=(c == CH - 1))
                        ins.then_inc(o_pe, 1)
                        pe.wait_ge(o_done, n + 1)
                        if later(n, 1):
                            pe.wait_ge(r_taken, n)
                        for t in range(BT):
                            ins = pe.transpose(pR[:, t * P:(t + 1) * P], oT[:, t * P:(t + 1) * P], core["ident"])
                        ins.then_inc(r_pe, 1)
                rounds(pe, step, BLOCKS)
        k.clear()


def normalise(nc, core, tag, src_store, eps, then, w=None):
    with ExitStack() as stack:
        k = Held(nc, stack, tag)
        stats = k.sb("stats", [P, BT, 6]); moments = k.sb("moments", [P, BT, 2])
        veps = k.sb("veps", [P, BT]); rstd = k.sb("rstd", [P, BT]); mhalf = k.sb("mhalf", [P, BT])
        xn = k.sb("xn", [P, BT, D]); scaled = k.sb("scaled", [P, BT, D])
        gb = k.sb("gb", [P, 2, D])
        w_in, setup, apart, stats_done, rstd_done = k.sem("w_in setup apart stats_done rstd_done")
        with nc.Block() as block:
            if then == "add":
                @block.sync
                def _(sp):
                    sp.dma_start(gb[:, :, :], w.partition_broadcast(P)).then_inc(w_in, 16)

            @block.gpsimd
            def _(g):
                chain = Chain(g)
                g.memset(mhalf[:, :], -0.5).then_inc(setup, 1)
                g.wait_ge(setup, 1)
                with g.Fori(0, BLOCKS) as n:
                    g.wait_ge(stats_done, n + 1)
                    ln_rstd(g, chain, moments, veps, mhalf, rstd, eps, rstd_done, apart)

            @block.vector
            def _(v):
                chain = Chain(v)
                if then == "add":
                    v.wait_ge(w_in, 16)
                with v.Fori(0, BLOCKS) as n:
                    src = rows(src_store, n * BT, BT)
                    ln_stats(v, chain, src, stats, moments, stats_done)
                    v.wait_ge(rstd_done, n + 1)
                    if then == "init":
                        chain.link(ln_apply(v, src, moments, rstd, rows(core["h"], n * BT, BT)))
                    else:
                        chain.link(ln_apply(v, src, moments, rstd, xn))
                        chain.link(v.tensor_tensor(scaled[:, :, :], xn[:, :, :],
                                                   gb[:, 0:1, :].broadcast_to((P, BT, D)), op=ALU.mult))
                        chain.link(v.tensor_tensor(xn[:, :, :], scaled[:, :, :],
                                                   gb[:, 1:2, :].broadcast_to((P, BT, D)), op=ALU.add))
                        dst = rows(core["x"], n * BT, BT)
                        chain.link(v.tensor_tensor(dst, xn[:, :, :], dst, op=ALU.add))
        k.clear()

def routed_experts(nc, core, tag, w):
    E, GR, EG, TOPK, KG = 64, 8, 8, 8, 4
    CH = E // 2
    OUT_AT, T_AT, LOGIT_AT, COEF_AT = 1, 4, 8, 29
    ROUTE_AT = 11
    with ExitStack() as stack:
        k = Held(nc, stack, tag)
        wg = k.sb("wg", [P, (CH + 1) * P]); wu = k.sb("wu", [P, (CH + 1) * P]); wd = k.sb("wd", [P, CH + 1, D])
        wr = k.sb("wr", [P, E]); bias = k.sb("bias", [P, 1, E]); tri = k.sb("tri", [P, GR * GR])
        selhm = k.sb("selhm", [P, CH, P], BF16); sell = k.sb("sell", [E, CH, P], BF16)
        stats = k.sb("stats", [P, BT, 6]); moments = k.sb("moments", [P, BT, 2])
        veps = k.sb("veps", [P, BT]); rstd = k.sb("rstd", [P, BT]); mhalf = k.sb("mhalf", [P, BT])
        xn = k.sb("xn", [P, BT, D]); nextT = k.sb("nextT", [P, BLK]); xnT = k.sb("xnT", [P, BLK])
        score = k.sb("score", [P, BT, E]); sfc = k.sb("sfc", [P, BT * GR, EG])
        hi4 = k.sb("hi4", [P, BT * GR, 4]); lo4 = k.sb("lo4", [P, BT * GR, 4])
        hi2 = k.sb("hi2", [P, BT * GR, 2]); lo2 = k.sb("lo2", [P, BT * GR, 2]); mid2 = k.sb("mid2", [P, BT * GR, 2])
        hi1 = k.sb("hi1", [P, BT * GR, 1]); lo1 = k.sb("lo1", [P, BT * GR, 1]); mid1 = k.sb("mid1", [P, BT * GR, 1])
        gs = k.sb("gs", [P, BT * GR]); more = k.sb("more", [P, BT * GR, GR]); same = k.sb("same", [P, BT * GR, GR])
        rank = k.sb("rank", [P, BT * GR]); gmask = k.sb("gmask", [P, BT * GR])
        masked = k.sb("masked", [P, BT, E]); top = k.sb("top", [P, BT, 8]); left = k.sb("left", [P, BT, E])
        picked = k.sb("picked", [P, BT, E]); wsum = k.sb("wsum", [P, BT]); winv = k.sb("winv", [P, BT])
        coef = k.sb("coef", [P, BT, E]); crest = k.sb("crest", [P, BT, E])
        chm = k.sb("chm", [P, BT, 2, E], BF16); cl = k.sb("cl", [P, BT, E], BF16)
        nextc = k.sb("nextc", [P, BLK], BF16); nextl = k.sb("nextl", [E, BLK], BF16)
        nowc = k.sb("nowc", [P, BLK], BF16); nowl = k.sb("nowl", [E, BLK], BF16)
        silu = [k.sb(f"silu{b}", [P, BLK]) for b in range(2)]
        gated = k.sb("gated", [P, BLK]); hidden = [k.sb(f"hidden{b}", [P, BLK]) for b in range(2)]
        oT = k.sb("oT", [P, BLK])
        pG = [k.ps(f"pG{b}", [P, BLK]) for b in range(2)]; pU = [k.ps(f"pU{b}", [P, BLK]) for b in range(2)]
        pC = [k.ps(f"pC{b}", [P, BLK]) for b in range(2)]
        pO = k.ps("pO", [P, BLK]); misc = k.ps("misc", [P, BLK])
        miscb = misc[:, :].bitcast(BF16)
        (w_in, setup, apart, stats_done, rstd_done, xn_done, t_pe, nextT_done, logit_pe, score_done, coef_done,
         coef_pe, nextc_done, now_ready, g_pe, silu_done, uc_pe, hidden_done, o_pe, o_done, r_pe, r_taken
         ) = k.sem("w_in setup apart stats_done rstd_done xn_done t_pe nextT_done logit_pe score_done coef_done "
                   "coef_pe nextc_done now_ready g_pe silu_done uc_pe hidden_done o_pe o_done r_pe r_taken")
        NC = CH + 1
        W_IN = 16 * 11

        with nc.Block() as block:
            @block.sync
            def _(sp):
                for dst, src in ((wg[:, 0:CH * P], w["wg"]), (wg[:, CH * P:], w["swg"]), (wu[:, 0:CH * P], w["wu"]),
                                 (wu[:, CH * P:], w["swu"]), (wd[:, 0:CH, :], w["wd"]), (wd[:, CH, :], w["swd"]),
                                 (wr[:, :], w["router"]), (bias[:, 0, :], w["bias"].partition_broadcast(P)),
                                 (tri[:, :], core["tri"].partition_broadcast(P)),
                                 (selhm[:, :, :], core["selhm"]), (sell[:, :, :], core["sell"])):
                    sp.dma_start(dst, src).then_inc(w_in, 16)

            @block.gpsimd
            def _(g):
                chain = Chain(g)
                g.memset(mhalf[:, :], -0.5).then_inc(setup, 1)
                g.wait_ge(setup, 1)

                def step(n, ahead, now, back):
                    if ahead:
                        g.wait_ge(stats_done, n + 2)
                        ln_rstd(g, chain, moments, veps, mhalf, rstd, 1e-5, rstd_done, apart)
                rounds(g, step, BLOCKS, behind=True)

            @block.vector
            def _(v):
                chain = Chain(v)
                v.wait_ge(w_in, W_IN)

                def tt(out, a, b, op):
                    chain.link(v.tensor_tensor(out, a, b, op=op))

                def route(part, m):
                    if part == 0:
                        v.wait_ge(score_done, m + 1)
                        tt(sfc[:, :, :].rearrange("p (t g) e -> p t (g e)", g=GR), score[:, :, :],
                           bias[:, :, :].broadcast_to((P, BT, E)), ALU.add)
                        tt(hi4[:, :, :], sfc[:, :, 0:4], sfc[:, :, 4:8], ALU.max)
                        tt(lo4[:, :, :], sfc[:, :, 0:4], sfc[:, :, 4:8], ALU.min)
                        tt(hi2[:, :, :], hi4[:, :, 0:2], hi4[:, :, 2:4], ALU.max)
                    if part == 1:
                        tt(mid2[:, :, :], hi4[:, :, 0:2], hi4[:, :, 2:4], ALU.min)
                        tt(lo2[:, :, :], lo4[:, :, 0:2], lo4[:, :, 2:4], ALU.max)
                        tt(lo2[:, :, :], lo2[:, :, :], mid2[:, :, :], ALU.max)
                        tt(hi1[:, :, :], hi2[:, :, 0:1], hi2[:, :, 1:2], ALU.max)
                        tt(mid1[:, :, :], hi2[:, :, 0:1], hi2[:, :, 1:2], ALU.min)
                    if part == 2:
                        tt(lo1[:, :, :], lo2[:, :, 0:1], lo2[:, :, 1:2], ALU.max)
                        tt(lo1[:, :, :], lo1[:, :, :], mid1[:, :, :], ALU.max)
                        tt(gs[:, :].unsqueeze(2), hi1[:, :, :], lo1[:, :, :], ALU.add)
                        other = gs[:, :].rearrange("p (t o g) -> p t o g", o=1, g=GR).broadcast_to((P, BT, GR, GR))
                        own = gs[:, :].rearrange("p (t g o) -> p t g o", g=GR, o=1).broadcast_to((P, BT, GR, GR))
                        tt(more[:, :, :].rearrange("p (t g) h -> p t g h", g=GR), other, own, ALU.is_gt)
                    if part == 3:
                        other = gs[:, :].rearrange("p (t o g) -> p t o g", o=1, g=GR).broadcast_to((P, BT, GR, GR))
                        own = gs[:, :].rearrange("p (t g o) -> p t g o", g=GR, o=1).broadcast_to((P, BT, GR, GR))
                        tt(same[:, :, :].rearrange("p (t g) h -> p t g h", g=GR), other, own, ALU.is_equal)
                        before = tri[:, :].unsqueeze(1).broadcast_to((P, BT, GR * GR))
                        flat = same[:, :, :].rearrange("p (t g) h -> p t (g h)", g=GR)
                        tt(flat, flat, before, ALU.mult)
                        tt(more[:, :, :], more[:, :, :], same[:, :, :], ALU.add)
                    if part == 4:
                        chain.link(v.tensor_reduce(rank[:, :], more[:, :, :], op=ALU.add, axis=AX.X))
                        chain.link(v.tensor_scalar(gmask[:, :], rank[:, :], float(KG), None, ALU.is_lt))
                        tt(masked[:, :, :].rearrange("p t (g e) -> p (t g) e", e=EG), sfc[:, :, :],
                           gmask[:, :].unsqueeze(2).broadcast_to((P, BT * GR, EG)), ALU.mult)
                    if part == 5:
                        for t in range(BT):
                            ins = v.max(top[:, t, :], masked[:, t, :])
                        chain.link(ins)
                        for t in range(BT):
                            ins = v.match_replace(left[:, t, :], top[:, t, :], masked[:, t, :], -3.0e38)
                        chain.link(ins)
                    if part == 6:
                        chain.link(v.tensor_scalar(picked[:, :, :], left[:, :, :], -2.0e38, None, ALU.is_lt))
                        tt(picked[:, :, :], picked[:, :, :], score[:, :, :], ALU.mult)
                        chain.link(v.tensor_reduce(wsum[:, :], picked[:, :, :], op=ALU.add, axis=AX.X))
                        chain.link(v.tensor_scalar_add(wsum[:, :], wsum[:, :], 1e-20))
                        chain.link(v.reciprocal(winv[:, :], wsum[:, :]))
                    if part == 7:
                        tt(coef[:, :, :], picked[:, :, :], winv[:, :].unsqueeze(2).broadcast_to((P, BT, E)), ALU.mult)
                        chain.link(v.tensor_scalar(coef[:, :, :], coef[:, :, :], 2.5, None, ALU.mult))
                    if part == 8:
                        chain.link(v.tensor_copy(chm[:, :, 0, :], coef[:, :, :]))
                        tt(crest[:, :, :], coef[:, :, :], chm[:, :, 0, :], ALU.subtract)
                        chain.link(v.tensor_copy(chm[:, :, 1, :], crest[:, :, :]))
                        v.tensor_tensor(cl[:, :, :], crest[:, :, :], chm[:, :, 1, :], op=ALU.subtract
                                        ).then_inc(coef_done, 1)
                PARTS = 9

                def step(n, ahead, now, back):
                    m = n + 1
                    v.drain()
                    if ahead:
                        src = rows(core["x"], m * BT, BT)
                        ln_stats(v, chain, src, stats, moments, stats_done)
                        v.wait_ge(rstd_done, m + 1)
                        if later(m, 1):
                            v.wait_ge(nextT_done, m)
                        ln_apply(v, src, moments, rstd, xn).then_inc(xn_done, 1)
                    for c in range(NC if now else 0):
                        if c == OUT_AT + 1 and back:
                            v.wait_ge(r_pe, n)
                            dst = rows(core["x"], (n - 1) * BT, BT)
                            v.tensor_tensor(dst, misc[:, :].rearrange("p (t d) -> p t d", d=D), dst, op=ALU.add
                                            ).then_inc(r_taken, 1)
                        if ahead and ROUTE_AT <= c < ROUTE_AT + PARTS:
                            route(c - ROUTE_AT, m)
                        v.wait_ge(silu_done, n * NC + c + 1)
                        v.wait_ge(uc_pe, n * NC + c + 1)
                        if c < CH:
                            chain.link(v.tensor_tensor(gated[:, :], pU[c % 2][:, :], silu[c % 2][:, :], op=ALU.mult))
                            v.tensor_tensor(hidden[c % 2][:, :], pC[c % 2][:, :], gated[:, :], op=ALU.mult
                                            ).then_inc(hidden_done, 1)
                            v.drain()
                        else:
                            v.tensor_tensor(hidden[c % 2][:, :], pU[c % 2][:, :], silu[c % 2][:, :], op=ALU.mult
                                            ).then_inc(hidden_done, 1)
                    if ahead and not now:
                        for part in range(PARTS):
                            route(part, m)
                    if ahead:
                        v.wait_ge(nextc_done, m + 1)
                        if now:
                            v.wait_ge(uc_pe, (n + 1) * NC)
                        v.tensor_copy(xnT[:, :], nextT[:, :])
                        v.tensor_copy(nowc[:, :], nextc[:, :])
                        v.tensor_copy(nowl[:, :], nextl[:, :]).then_inc(now_ready, 1)
                    if back and not now:
                        v.wait_ge(r_pe, n)
                        dst = rows(core["x"], (n - 1) * BT, BT)
                        v.tensor_tensor(dst, misc[:, :].rearrange("p (t d) -> p t d", d=D), dst, op=ALU.add
                                        ).then_inc(r_taken, 1)
                rounds(v, step, BLOCKS, behind=True)

            @block.scalar
            def _(act):
                act.wait_ge(w_in, W_IN)

                def take_T(m):
                    act.wait_ge(t_pe, m + 1)
                    if later(m, 1):
                        act.wait_ge(now_ready, m)
                    act.activation(nextT[:, :], misc[:, :], ACT.Copy).then_inc(nextT_done, 1)

                def take_logits(m):
                    act.wait_ge(logit_pe, m + 1)
                    if later(m, 1):
                        act.wait_ge(coef_done, m)
                    act.activation(score[:, :, :], misc[:, 0:BT * E].rearrange("p (t e) -> p t e", e=E),
                                   ACT.Sigmoid).then_inc(score_done, 1)

                def take_coef(m):
                    act.wait_ge(coef_pe, m + 1)
                    act.activation(nextc[:, :], miscb[:, 0:BLK], ACT.Copy)
                    act.activation(nextl[:, :], miscb[0:E, BLK:2 * BLK], ACT.Copy).then_inc(nextc_done, 1)

                def step(n, ahead, now, back):
                    m = n + 1
                    for c in range(NC if now else 0):
                        if ahead and c == T_AT:
                            take_T(m)
                        if ahead and c == LOGIT_AT:
                            take_logits(m)
                        if ahead and c == COEF_AT:
                            take_coef(m)
                        act.wait_ge(g_pe, n * NC + c + 1)
                        if c >= 2 or later(n, 1):
                            act.wait_ge(hidden_done, n * NC + c - 1)
                        act.activation(silu[c % 2][:, :], pG[c % 2][:, :], ACT.Silu).then_inc(silu_done, 1)
                    if ahead and not now:
                        take_T(m)
                        take_logits(m)
                        take_coef(m)
                    if now:
                        act.wait_ge(o_pe, n + 1)
                        if later(n, 1):
                            act.wait_ge(r_pe, n)
                        act.activation(oT[:, :], pO[:, :], ACT.Copy).then_inc(o_done, 1)
                rounds(act, step, BLOCKS, behind=True)

            @block.tensor
            def _(pe):
                pe.wait_ge(w_in, W_IN)
                ident, identb = core["ident"], core["identb"]

                def make_T(m):
                    pe.wait_ge(xn_done, m + 1)
                    if later(m, 1):
                        pe.wait_ge(nextc_done, m)
                    for t in range(BT):
                        ins = pe.transpose(misc[:, t * P:(t + 1) * P], xn[:, t, :], ident)
                    ins.then_inc(t_pe, 1)

                def make_logits(m):
                    pe.wait_ge(nextT_done, m + 1)
                    for t in range(BT):
                        ins = pe.matmul(misc[:, t * E:(t + 1) * E], nextT[:, t * P:(t + 1) * P], wr[:, :],
                                        start=True, stop=True)
                    ins.then_inc(logit_pe, 1)

                def make_coef(m):
                    pe.wait_ge(coef_done, m + 1)
                    for t in range(BT):
                        pe.transpose(miscb[:, t * P:(t + 1) * P], chm[:, t, :, :].rearrange("p c e -> p (c e)"),
                                     identb)
                        ins = pe.transpose(miscb[0:E, BLK + t * P:BLK + (t + 1) * P], cl[:, t, :], identb)
                    ins.then_inc(coef_pe, 1)

                def make_out(o):
                    pe.wait_ge(o_done, o + 1)
                    for t in range(BT):
                        ins = pe.transpose(misc[:, t * P:(t + 1) * P], oT[:, t * P:(t + 1) * P], ident)
                    ins.then_inc(r_pe, 1)

                def step(n, ahead, now, back):
                    m = n + 1

                    def down(c):
                        pe.wait_ge(hidden_done, n * NC + c + 1)
                        if c == 0 and later(n, 1):
                            pe.wait_ge(o_done, n)
                        ins = pe.matmul(pO[:, :], wd[:, c, :], hidden[c % 2][:, :], start=(c == 0),
                                        stop=(c == NC - 1))
                        if c == NC - 1:
                            ins.then_inc(o_pe, 1)

                    if now:
                        pe.wait_ge(now_ready, n + 1)
                    for c in range(NC if now else 0):
                        if c == OUT_AT and back:
                            pe.wait_ge(nextc_done, n + 1)
                            make_out(n - 1)
                        if ahead and c == T_AT:
                            if back:
                                pe.wait_ge(r_taken, n)
                            make_T(m)
                        if ahead and c == LOGIT_AT:
                            make_logits(m)
                        if ahead and c == COEF_AT:
                            make_coef(m)
                        if c >= 2 or later(n, 1):
                            pe.wait_ge(hidden_done, n * NC + c - 1)
                        pe.matmul(pG[c % 2][:, :], wg[:, c * P:(c + 1) * P], xnT[:, :], start=True, stop=True
                                  ).then_inc(g_pe, 1)
                        ins = pe.matmul(pU[c % 2][:, :], wu[:, c * P:(c + 1) * P], xnT[:, :], start=True, stop=True)
                        if c < CH:
                            pe.matmul(pC[c % 2][:, :], selhm[:, c, :], nowc[:, :], start=True, stop=False)
                            ins = pe.matmul(pC[c % 2][:, :], sell[:, c, :], nowl[:, :], start=False, stop=True)
                        ins.then_inc(uc_pe, 1)
                        if c >= 1:
                            down(c - 1)
                    if now:
                        down(NC - 1)
                    if ahead and not now:
                        make_T(m)
                        make_logits(m)
                        make_coef(m)
                    if back and not now:
                        make_out(n - 1)
                rounds(pe, step, BLOCKS, behind=True)
        k.clear()

def top2_experts(nc, core, tag, w):
    E = 8
    with ExitStack() as stack:
        k = Held(nc, stack, tag)
        we = k.sb("we", [P, E * D]); wgate = k.sb("wgate", [P, E]); wc = k.sb("wc", [P, D])
        be = k.sb("be", [P, E * D]); tri = k.sb("tri", [P, E * E])
        stats = k.sb("stats", [P, BT, 6]); moments = k.sb("moments", [P, BT, 2])
        veps = k.sb("veps", [P, BT]); rstd = k.sb("rstd", [P, BT]); mhalf = k.sb("mhalf", [P, BT])
        xn = k.sb("xn", [P, BT, D]); xnT = k.sb("xnT", [P, BLK])
        lg = k.sb("lg", [P, BT, E]); mx = k.sb("mx", [P, BT]); ex = k.sb("ex", [P, BT, E])
        sm = k.sb("sm", [P, BT]); inv = k.sb("inv", [P, BT]); pr = k.sb("pr", [P, BT, E])
        more = k.sb("more", [P, BT * E, E]); same = k.sb("same", [P, BT * E, E]); rank = k.sb("rank", [P, BT, E])
        coef = k.sb("coef", [P, BT, E])
        pre = [k.sb(f"pre{b}", [P, E * D]) for b in range(2)]
        silu = [k.sb(f"silu{b}", [P, E, D]) for b in range(2)]
        part = [k.sb(f"part{b}", [P, E, D]) for b in range(2)]
        mixed = [k.sb(f"mixed{b}", [P, D]) for b in range(2)]; mixT = k.sb("mixT", [P, D])
        pT = k.ps("pT", [P, BLK]); pL = k.ps("pL", [P, BLK])
        pE = [k.ps(f"pE{b}", [P, E * D]) for b in range(2)]
        pM = k.ps("pM", [P, BLK]); pO = k.ps("pO", [P, BLK])
        (w_in, setup, apart, stats_done, rstd_done, xn_done, t_pe, xnT_done, logit_pe, max_done, exp_done,
         coef_done, e_pe, pre_done, silu_done, part_done, mixed_done, m_pe, mixT_done, o_pe, o_taken
         ) = k.sem("w_in setup apart stats_done rstd_done xn_done t_pe xnT_done logit_pe max_done exp_done "
                   "coef_done e_pe pre_done silu_done part_done mixed_done m_pe mixT_done o_pe o_taken")
        W_IN = 16 * 5
        with nc.Block() as block:
            @block.sync
            def _(sp):
                for dst, src in ((we, w["we"]), (wgate, w["gate"]), (wc, w["wc"]),
                                 (be, w["be"].partition_broadcast(P)), (tri, core["tri"].partition_broadcast(P))):
                    sp.dma_start(dst[:, :], src).then_inc(w_in, 16)

            @block.gpsimd
            def _(g):
                chain = Chain(g)
                g.memset(mhalf[:, :], -0.5).then_inc(setup, 1)
                g.wait_ge(setup, 1)
                with g.Fori(0, BLOCKS) as n:
                    g.wait_ge(stats_done, n + 1)
                    ln_rstd(g, chain, moments, veps, mhalf, rstd, 1e-5, rstd_done, apart)
                    for t in range(BT):
                        g.wait_ge(coef_done, n + 1)
                        g.wait_ge(silu_done, n * BT + t + 1)
                        g.sem_inc(apart, 1)
                        if t >= 2:
                            g.wait_ge(mixed_done, n * BT + t - 1)
                        g.tensor_tensor(part[t % 2][:, :, :], silu[t % 2][:, :, :],
                                        coef[:, t, :].unsqueeze(2).broadcast_to((P, E, D)), op=ALU.mult
                                        ).then_inc(part_done, 1)

            @block.vector
            def _(v):
                chain = Chain(v)
                v.wait_ge(w_in, W_IN)

                def tt(out, a, b, op):
                    chain.link(v.tensor_tensor(out, a, b, op=op))
                with v.Fori(0, BLOCKS) as n:
                    src = rows(core["x"], n * BT, BT)
                    tt(src, src, rows(core["h"], n * BT, BT), ALU.add)
                    ln_stats(v, chain, src, stats, moments, stats_done)
                    v.wait_ge(rstd_done, n + 1)
                    ln_apply(v, src, moments, rstd, xn).then_inc(xn_done, 1)
                    v.wait_ge(logit_pe, n + 1)
                    logits = pL[:, 0:BT * E].rearrange("p (t e) -> p t e", e=E)
                    chain.link(v.tensor_reduce(mx[:, :], logits, op=ALU.max, axis=AX.X))
                    v.tensor_tensor(lg[:, :, :], logits, mx[:, :].unsqueeze(2).broadcast_to((P, BT, E)),
                                    op=ALU.subtract).then_inc(max_done, 1)
                    v.wait_ge(exp_done, n + 1)
                    chain.link(v.tensor_reduce(sm[:, :], ex[:, :, :], op=ALU.add, axis=AX.X))
                    chain.link(v.reciprocal(inv[:, :], sm[:, :]))
                    tt(pr[:, :, :], ex[:, :, :], inv[:, :].unsqueeze(2).broadcast_to((P, BT, E)), ALU.mult)
                    other = pr[:, :, :].unsqueeze(2).broadcast_to((P, BT, E, E))
                    own = pr[:, :, :].unsqueeze(3).broadcast_to((P, BT, E, E))
                    tt(more[:, :, :].rearrange("p (t g) h -> p t g h", g=E), other, own, ALU.is_gt)
                    tt(same[:, :, :].rearrange("p (t g) h -> p t g h", g=E), other, own, ALU.is_equal)
                    flat = same[:, :, :].rearrange("p (t g) h -> p t (g h)", g=E)
                    tt(flat, flat, tri[:, :].unsqueeze(1).broadcast_to((P, BT, E * E)), ALU.mult)
                    tt(more[:, :, :], more[:, :, :], same[:, :, :], ALU.add)
                    chain.link(v.tensor_reduce(rank[:, :, :].rearrange("p t e -> p (t e)"), more[:, :, :],
                                               op=ALU.add, axis=AX.X))
                    chain.link(v.tensor_scalar(rank[:, :, :], rank[:, :, :], 2.0, None, ALU.is_lt))
                    v.tensor_tensor(coef[:, :, :], rank[:, :, :], pr[:, :, :], op=ALU.mult).then_inc(coef_done, 1)
                    for t in range(BT + 1):
                        if t < BT:
                            v.wait_ge(e_pe, n * BT + t + 1)
                            v.tensor_tensor(pre[t % 2][:, :], pE[t % 2][:, :], be[:, :], op=ALU.add
                                            ).then_inc(pre_done, 1)
                        if t >= 1:
                            v.wait_ge(part_done, n * BT + t)
                            v.tensor_reduce(mixed[(t - 1) % 2][:, :],
                                            part[(t - 1) % 2][:, :, :].rearrange("p e d -> p d e"),
                                            op=ALU.add, axis=AX.X).then_inc(mixed_done, 1)
                    v.wait_ge(o_pe, n * BT + BT)
                    tt(src, pO[:, :].rearrange("p (t d) -> p t d", d=D), src, ALU.add)

            @block.scalar
            def _(act):
                act.wait_ge(w_in, W_IN)
                with act.Fori(0, BLOCKS) as n:
                    act.wait_ge(t_pe, n + 1)
                    act.activation(xnT[:, :], pT[:, :], ACT.Copy).then_inc(xnT_done, 1)
                    act.wait_ge(max_done, n + 1)
                    act.activation(ex[:, :, :], lg[:, :, :], ACT.Exp).then_inc(exp_done, 1)
                    for t in range(BT + 1):
                        if t < BT:
                            act.wait_ge(pre_done, n * BT + t + 1)
                            act.activation(silu[t % 2][:, :, :].rearrange("p e d -> p (e d)"), pre[t % 2][:, :],
                                           ACT.Silu).then_inc(silu_done, 1)
                        if t >= 1:
                            act.wait_ge(m_pe, n * BT + t)
                            act.activation(mixT[:, :], pM[:, 0:D], ACT.Copy).then_inc(mixT_done, 1)

            @block.tensor
            def _(pe):
                pe.wait_ge(w_in, W_IN)
                with pe.Fori(0, BLOCKS) as n:
                    pe.wait_ge(xn_done, n + 1)
                    for t in range(BT):
                        ins = pe.transpose(pT[:, t * P:(t + 1) * P], xn[:, t, :], core["ident"])
                    ins.then_inc(t_pe, 1)
                    pe.wait_ge(xnT_done, n + 1)
                    for t in range(BT):
                        ins = pe.matmul(pL[:, t * E:(t + 1) * E], xnT[:, t * P:(t + 1) * P], wgate[:, :],
                                        start=True, stop=True)
                    ins.then_inc(logit_pe, 1)
                    for t in range(BT + 1):
                        if t < BT:
                            if t >= 2:
                                pe.wait_ge(pre_done, n * BT + t - 1)
                            for half in range(2):
                                ins = pe.matmul(pE[t % 2][:, half * BLK:(half + 1) * BLK], xnT[:, t * P:(t + 1) * P],
                                                we[:, half * BLK:(half + 1) * BLK], start=True, stop=True)
                            ins.then_inc(e_pe, 1)
                        if t >= 1:
                            pe.wait_ge(mixed_done, n * BT + t)
                            pe.transpose(pM[:, 0:D], mixed[(t - 1) % 2][:, :], core["ident"]).then_inc(m_pe, 1)
                            pe.wait_ge(mixT_done, n * BT + t)
                            pe.matmul(pO[:, (t - 1) * D:t * D], mixT[:, :], wc[:, :], start=True, stop=True
                                      ).then_inc(o_pe, 1)
        k.clear()


def performer(nc, core, tag, w):
    M = 32
    HM = HEADS * M
    KS = float(HD) ** -0.25
    LOGM = -0.5 * math.log(M)
    with ExitStack() as stack:
        k = Held(nc, stack, tag)
        wqkv = k.sb("wqkv", [P, 3 * D]); wT = k.sb("wT", [P, 2, P]); omega = k.sb("omega", [P, HM])
        wf = k.sb("wf", [P, 2, HM]); wo = k.sb("wo", [P, D]); diag = k.sb("diag", [P, GH * 9])
        logm = k.sb("logm", [P, 1])
        stats = k.sb("stats", [P, QT, 6]); moments = k.sb("moments", [P, QT, 2])
        veps = k.sb("veps", [P, QT]); rstd = k.sb("rstd", [P, QT]); mhalf = k.sb("mhalf", [P, QT])
        xn = k.sb("xn", [P, QT, D]); xnT = k.sb("xnT", [P, SEQ])
        sqr = k.sb("sqr", [P, 2 * D]); sqsum = k.sb("sqsum", [P, 2 * HEADS]); stab = k.sb("stab", [P, 2 * HEADS])
        shift = k.sb("shift", [P, 2 * HEADS]); arg = k.sb("arg", [P, 2, HM]); ex = k.sb("ex", [P, 2, HM])
        phi = k.sb("phi", [P, QT, 2, HM]); vaug = k.sb("vaug", [P, QT, HEADS, 9])
        phiT = k.sb("phiT", [P, QT, HM]); kv = k.sb("kv", [P, GROUPS, GH * 9])
        rec = k.sb("rec", [P, HEADS]); ctx = k.sb("ctx", [P, QT, D]); ctxT = k.sb("ctxT", [P, SEQ])
        pT = k.ps("pT", [P, BLK]); pF = k.ps("pF", [P, 2 * HM]); pV = k.ps("pV", [P, BLK])
        pP = k.ps("pP", [P, BLK]); pK = k.ps("pK", [P, BLK]); pN = k.ps("pN", [P, BLK]); pO = k.ps("pO", [P, BLK])
        (w_in, setup, apart, wf_pe, wf_done, stats_done, rstd_done, xn_done, t_pe, xnT_done, f_pe, f_taken, sq_done,
         arg_done, ex_done, phi_done, v_done, pp_pe, phiT_done, kv_pe, kv_done, n_pe, ctx_done, c_pe, ctxT_done,
         o_pe, o_taken) = k.sem(
            "w_in setup apart wf_pe wf_done stats_done rstd_done xn_done t_pe xnT_done f_pe f_taken sq_done "
            "arg_done ex_done phi_done v_done pp_pe phiT_done kv_pe kv_done n_pe ctx_done c_pe ctxT_done "
            "o_pe o_taken")
        W_IN = 16 * (4 + HEADS)
        with nc.Block() as block:
            @block.sync
            def _(sp):
                sp.dma_start(wqkv[:, :], w["wqkv"]).then_inc(w_in, 16)
                sp.dma_start(wT[:, :, :], w["wT"]).then_inc(w_in, 16)
                sp.dma_start(wo[:, :], w["wo"]).then_inc(w_in, 16)
                sp.dma_start(diag[:, :], core["diag"]).then_inc(w_in, 16)
                sp.wait_ge(setup, 1)
                for h in range(HEADS):
                    sp.dma_start(omega[h * HD:(h + 1) * HD, h * M:(h + 1) * M], w["omega"]).then_inc(w_in, 16)

            @block.gpsimd
            def _(g):
                chain = Chain(g)
                g.memset(omega[:, :], 0.0).then_inc(setup, 1)
                g.memset(mhalf[:, :], -0.5).then_inc(setup, 1)
                g.memset(vaug[:, :, :, 8:9], 1.0).then_inc(setup, 1)
                g.memset(logm[:, :], LOGM).then_inc(setup, 1)
                g.wait_ge(setup, 4)
                with g.Fori(0, SEQS) as n:
                    g.wait_ge(stats_done, n + 1)
                    ln_rstd(g, chain, moments, veps, mhalf, rstd, 1e-5, rstd_done, apart)
                    for t in range(QT):
                        g.wait_ge(ex_done, n * QT + t + 1)
                        g.sem_inc(apart, 1)
                        g.tensor_scalar_add(phi[:, t, :, :], ex[:, :, :], 1e-6).then_inc(phi_done, 1)

            @block.vector
            def _(v):
                chain = Chain(v)
                v.wait_ge(w_in, W_IN)
                v.wait_ge(setup, 4)
                with v.Fori(0, SEQS) as n:
                    src = rows(core["x"], n * QT, QT)
                    v.drain()
                    ln_stats(v, chain, src, stats, moments, stats_done)
                    v.wait_ge(rstd_done, n + 1)
                    ln_apply(v, src, moments, rstd, xn).then_inc(xn_done, 1)
                    for t in range(QT):
                        v.drain()
                        v.wait_ge(f_pe, n * QT + t + 1)
                        feats = pF[:, :].rearrange("p (h m) -> p h m", m=M)
                        chain.link(v.tensor_reduce(stab[:, :], feats, op=ALU.max, axis=AX.X))
                        v.wait_ge(sq_done, n * QT + t + 1)
                        chain.link(v.tensor_reduce(sqsum[:, :], sqr[:, :].rearrange("p (h e) -> p h e", e=HD),
                                                   op=ALU.add, axis=AX.X))
                        chain.link(v.tensor_tensor(shift[:, :], stab[:, :], sqsum[:, :], op=ALU.add))
                        v.tensor_tensor(arg[:, :, :].rearrange("p c (h m) -> p (c h) m", m=M), feats,
                                        shift[:, :].unsqueeze(2).broadcast_to((P, 2 * HEADS, M)), op=ALU.subtract
                                        ).then_inc(arg_done, 1)
                    v.wait_ge(kv_pe, n + 1)
                    v.tensor_tensor(kv[:, :, :], pK[:, 0:GROUPS * GH * 9].rearrange("p (g c) -> p g c", g=GROUPS),
                                    diag[:, :].unsqueeze(1).broadcast_to((P, GROUPS, GH * 9)), op=ALU.mult
                                    ).then_inc(kv_done, 1)
                    for t in range(QT):
                        v.drain()
                        v.wait_ge(n_pe, n * QT + t + 1)
                        num = pN[:, 0:HEADS * 9].rearrange("p (h e) -> p h e", e=9)
                        chain.link(v.reciprocal(rec[:, :].unsqueeze(2), num[:, :, 8:9]))
                        v.tensor_tensor(ctx[:, t, :].rearrange("p (h e) -> p h e", e=HD), num[:, :, 0:HD],
                                        rec[:, :].unsqueeze(2).broadcast_to((P, HEADS, HD)), op=ALU.mult
                                        ).then_inc(ctx_done, 1)
                    v.wait_ge(o_pe, n + 1)
                    v.tensor_tensor(rows(core["h"], n * QT, QT), pO[:, 0:SEQ].rearrange("p (t d) -> p t d", d=D),
                                    xn[:, :, :], op=ALU.add)

            @block.scalar
            def _(act):
                act.wait_ge(w_in, W_IN)
                act.wait_ge(setup, 4)
                act.wait_ge(wf_pe, 1)
                act.activation(wf[:, :, :].rearrange("p c m -> p (c m)"), pF[:, :], ACT.Copy, scale=KS
                               ).then_inc(wf_done, 1)
                with act.Fori(0, SEQS) as n:
                    act.wait_ge(t_pe, n + 1)
                    act.activation(xnT[:, :], pT[:, 0:SEQ], ACT.Copy).then_inc(xnT_done, 1)
                    for t in range(QT):
                        act.wait_ge(f_pe, n * QT + t + 1)
                        act.activation(sqr[:, :], pV[:, 0:2 * D], ACT.Square, scale=KS * 0.5 ** 0.5
                                       ).then_inc(sq_done, 1)
                        act.activation(vaug[:, t, :, 0:HD], pV[:, 2 * D:3 * D].rearrange("p (h e) -> p h e", e=HD),
                                       ACT.Copy).then_inc(v_done, 1)
                        act.wait_ge(arg_done, n * QT + t + 1)
                        if t == 1:
                            act.wait_ge(phi_done, n * QT + 1)
                        act.activation(ex[:, :, :], arg[:, :, :], ACT.Exp, bias=logm[:, 0:1]).then_inc(ex_done, 1)
                    for t in range(QT):
                        act.wait_ge(pp_pe, n * QT + t + 1)
                        act.activation(phiT[:, t, :], pP[:, :], ACT.Copy).then_inc(phiT_done, 1)
                    act.wait_ge(c_pe, n + 1)
                    act.activation(ctxT[:, :], pT[:, 0:SEQ], ACT.Copy).then_inc(ctxT_done, 1)

            @block.tensor
            def _(pe):
                pe.wait_ge(w_in, W_IN)
                pe.wait_ge(setup, 4)
                ident = core["ident"]
                for c in range(2):
                    ins = pe.matmul(pF[:, c * HM:(c + 1) * HM], wT[:, c, :], omega[:, :], start=True, stop=True)
                ins.then_inc(wf_pe, 1)
                pe.wait_ge(wf_done, 1)
                with pe.Fori(0, SEQS) as n:
                    pe.wait_ge(xn_done, n + 1)
                    for t in range(QT):
                        ins = pe.transpose(pT[:, t * P:(t + 1) * P], xn[:, t, :], ident)
                    ins.then_inc(t_pe, 1)
                    pe.wait_ge(xnT_done, n + 1)
                    for t in range(QT):
                        if t == 1:
                            pe.wait_ge(arg_done, n * QT + 1)
                            pe.wait_ge(v_done, n * QT + 1)
                        tok = xnT[:, t * P:(t + 1) * P]
                        for c in range(2):
                            pe.matmul(pF[:, c * HM:(c + 1) * HM], tok, wf[:, c, :], start=True, stop=True)
                        pe.matmul(pV[:, 0:3 * D], tok, wqkv[:, :], start=True, stop=True).then_inc(f_pe, 1)
                    pe.wait_ge(phi_done, n * QT + 2)
                    pe.wait_ge(v_done, n * QT + 2)
                    for gr in range(GROUPS):
                        for t in range(QT):
                            ins = pe.matmul(pK[:, gr * 36:(gr + 1) * 36], phi[:, t, 1, gr * P:(gr + 1) * P],
                                            vaug[:, t, gr * GH:(gr + 1) * GH, :].rearrange("p h e -> p (h e)"),
                                            start=(t == 0), stop=(t == QT - 1))
                    ins.then_inc(kv_pe, 1)
                    for t in range(QT):
                        if t == 1:
                            pe.wait_ge(phiT_done, n * QT + 1)
                        for gr in range(GROUPS):
                            ins = pe.transpose(pP[:, gr * P:(gr + 1) * P], phi[:, t, 0, gr * P:(gr + 1) * P], ident)
                        ins.then_inc(pp_pe, 1)
                    pe.wait_ge(kv_done, n + 1)
                    for t in range(QT):
                        pe.wait_ge(phiT_done, n * QT + t + 1)
                        if t == 1:
                            pe.wait_ge(ctx_done, n * QT + 1)
                        for gr in range(GROUPS):
                            ins = pe.matmul(pN[:, gr * 36:(gr + 1) * 36], phiT[:, t, gr * P:(gr + 1) * P],
                                            kv[:, gr, :], start=True, stop=True)
                        ins.then_inc(n_pe, 1)
                    pe.wait_ge(ctx_done, n * QT + 2)
                    for t in range(QT):
                        ins = pe.transpose(pT[:, t * P:(t + 1) * P], ctx[:, t, :], ident)
                    ins.then_inc(c_pe, 1)
                    pe.wait_ge(ctxT_done, n + 1)
                    for t in range(QT):
                        ins = pe.matmul(pO[:, t * D:(t + 1) * D], ctxT[:, t * P:(t + 1) * P], wo[:, :],
                                        start=True, stop=True)
                    ins.then_inc(o_pe, 1)
        k.clear()

def fp4_feed_forward(nc, core, tag, w):
    I, B16 = 352, 16
    WIDE = BT * I
    CUTS = [(0, 128), (128, 128), (256, 96)]
    with ExitStack() as stack:
        k = Held(nc, stack, tag)
        raw = k.sb("raw", [P, 6, D]); rawd = k.sb("rawd", [P, I]); wdone = k.sb("wdone", [P, 6, D])
        wdoned = k.sb("wdoned", [P, I])
        wgu = k.sb("wgu", [P, 2 * I]); wd = k.sb("wd", [P, 3, D])
        stats = k.sb("stats", [P, BT, 6]); moments = k.sb("moments", [P, BT, 2])
        veps = k.sb("veps", [P, BT]); rstd = k.sb("rstd", [P, BT]); mhalf = k.sb("mhalf", [P, BT])
        xn = k.sb("xn", [P, BT, D]); xq = k.sb("xq", [P, BT, D]); xqT = k.sb("xqT", [P, BLK])
        amax = k.sb("amax", [P, WIDE // B16]); scl = k.sb("scl", [P, WIDE // B16]); inv = k.sb("inv", [P, WIDE // B16])
        mag = k.sb("mag", [P, WIDE]); low = k.sb("low", [P, WIDE]); high = k.sb("high", [P, WIDE])
        silu = [k.sb(f"silu{b}", [P, I]) for b in range(2)]
        hid = k.sb("hid", [P, BT, I]); hq = k.sb("hq", [P, BT, I])
        hT = [k.sb(f"hT{b}", [P, 3 * P]) for b in range(2)]
        pT = k.ps("pT", [P, BLK])
        pG = [k.ps(f"pG{b}", [P, BLK]) for b in range(2)]; pU = [k.ps(f"pU{b}", [P, BLK]) for b in range(2)]
        pH = k.ps("pH", [P, BLK]); pO = k.ps("pO", [P, BLK])
        (w_in, setup, apart, wq_done, wt_pe, wt_done, stats_done, rstd_done, xq_done, t_pe, xqT_done, gu_pe, silu_done,
         hid_done, hq_done, h_pe, hT_done, o_pe) = k.sem(
            "w_in setup apart wq_done wt_pe wt_done stats_done rstd_done xq_done t_pe xqT_done gu_pe silu_done "
            "hid_done hq_done h_pe hT_done o_pe")
        with nc.Block() as block:
            @block.sync
            def _(sp):
                sp.wait_ge(setup, 2)
                for c, name in ((0, "wg"), (3, "wu")):
                    sp.dma_start(raw[:, c:c + 2, :], w[name][0:2 * P, :].rearrange("(c p) d -> p c d", p=P)
                                 ).then_inc(w_in, 16)
                    sp.dma_start(raw[0:I - 2 * P, c + 2, :], w[name][2 * P:I, :]).then_inc(w_in, 16)
                sp.dma_start(rawd[:, :], w["wd"]).then_inc(w_in, 16)

            @block.gpsimd
            def _(g):
                chain = Chain(g)
                g.memset(mhalf[:, :], -0.5).then_inc(setup, 1)
                g.memset(raw[:, :, :], 0.0).then_inc(setup, 1)
                g.wait_ge(setup, 2)
                with g.Fori(0, BLOCKS) as n:
                    g.wait_ge(stats_done, n + 1)
                    ln_rstd(g, chain, moments, veps, mhalf, rstd, 1e-5, rstd_done, apart)

            @block.vector
            def _(v):
                chain = Chain(v)
                v.wait_ge(w_in, 80)

                def quantise(src, dst, width):
                    nb = width // B16
                    am, sc, iv = amax[:, 0:nb], scl[:, 0:nb], inv[:, 0:nb]
                    ma, lo, hi = mag[:, 0:width], low[:, 0:width], high[:, 0:width]
                    by16 = lambda x: x.rearrange("p (b e) -> p b e", e=B16)
                    link = chain.link
                    link(v.tensor_reduce(am, by16(src), op=ALU.max, axis=AX.X, apply_absolute_value=True))
                    link(v.tensor_scalar(sc, am, 1.0 / 6.0, 1e-12, ALU.mult, ALU.max))
                    link(v.reciprocal(iv, sc))
                    link(v.tensor_tensor(by16(ma), by16(src), iv.unsqueeze(2).broadcast_to((P, nb, B16)), op=ALU.mult))
                    link(v.tensor_scalar(ma.bitcast(I32), ma.bitcast(I32), 0x7FFFFFFF, None, ALU.bitwise_and))
                    link(v.tensor_scalar(lo, ma, 0.25, None, ALU.is_gt))
                    for mid in (0.75, 1.25, 1.75):
                        link(v.scalar_tensor_tensor(out=lo, in0=ma, scalar=mid, in1=lo, op0=ALU.is_gt, op1=ALU.add))
                    link(v.tensor_scalar(hi, ma, 5.0, 2.0, ALU.is_gt, ALU.mult))
                    for mid in (2.5, 3.5):
                        link(v.scalar_tensor_tensor(out=hi, in0=ma, scalar=mid, in1=hi, op0=ALU.is_gt, op1=ALU.add))
                    link(v.scalar_tensor_tensor(out=hi, in0=lo, scalar=0.5, in1=hi, op0=ALU.mult, op1=ALU.add))
                    link(v.tensor_tensor(by16(lo), by16(hi), sc.unsqueeze(2).broadcast_to((P, nb, B16)), op=ALU.mult))
                    return v.scalar_tensor_tensor(out=dst.bitcast(I32), in0=src.bitcast(I32), scalar=-2147483648,
                                                  in1=lo.bitcast(I32), op0=ALU.bitwise_and, op1=ALU.bitwise_or)

                chain.link(quantise(raw[:, :, :].rearrange("p c d -> p (c d)"),
                                    wdone[:, :, :].rearrange("p c d -> p (c d)"), 6 * D))
                quantise(rawd[:, :], wdoned[:, :], I).then_inc(wq_done, 1)
                with v.Fori(0, BLOCKS) as n:
                    v.drain()
                    src = rows(core["x"], n * BT, BT)
                    ln_stats(v, chain, src, stats, moments, stats_done)
                    v.wait_ge(rstd_done, n + 1)
                    chain.link(ln_apply(v, src, moments, rstd, xn))
                    quantise(xn[:, :, :].rearrange("p t d -> p (t d)"), xq[:, :, :].rearrange("p t d -> p (t d)"),
                             BLK).then_inc(xq_done, 1)
                    for t in range(BT):
                        v.wait_ge(silu_done, n * BT + t + 1)
                        v.tensor_tensor(hid[:, t, :], pU[t % 2][:, 0:I], silu[t % 2][:, :], op=ALU.mult
                                        ).then_inc(hid_done, 1)
                    v.drain()
                    quantise(hid[:, :, :].rearrange("p t d -> p (t d)"), hq[:, :, :].rearrange("p t d -> p (t d)"),
                             WIDE).then_inc(hq_done, 1)
                    v.wait_ge(o_pe, n + 1)
                    v.tensor_tensor(src, pO[:, :].rearrange("p (t d) -> p t d", d=D), src, op=ALU.add)

            @block.scalar
            def _(act):
                act.wait_ge(wt_pe, 1)
                for c in range(2):
                    act.activation(wgu[:, c * I:(c + 1) * I], pG[c][:, 0:I], ACT.Copy)
                for c, (lo, cnt) in enumerate(CUTS):
                    ins = act.activation(wd[0:cnt, c, :], pH[0:cnt, c * P:(c + 1) * P], ACT.Copy)
                ins.then_inc(wt_done, 1)
                with act.Fori(0, BLOCKS) as n:
                    act.wait_ge(t_pe, n + 1)
                    act.activation(xqT[:, :], pT[:, :], ACT.Copy).then_inc(xqT_done, 1)
                    for t in range(BT):
                        act.wait_ge(gu_pe, n * BT + t + 1)
                        if t >= 2:
                            act.wait_ge(hid_done, n * BT + t - 1)
                        act.activation(silu[t % 2][:, :], pG[t % 2][:, 0:I], ACT.Silu).then_inc(silu_done, 1)
                    for t in range(BT):
                        act.wait_ge(h_pe, n * BT + t + 1)
                        act.activation(hT[t % 2][:, 0:2 * P], pH[:, 0:2 * P], ACT.Copy)
                        act.activation(hT[t % 2][0:96, 2 * P:3 * P], pH[0:96, 2 * P:3 * P], ACT.Copy
                                       ).then_inc(hT_done, 1)

            @block.tensor
            def _(pe):
                ident = core["ident"]
                pe.wait_ge(wq_done, 1)
                for c in range(2):
                    for j, (lo, cnt) in enumerate(CUTS):
                        pe.transpose(pG[c][:, lo:lo + cnt], wdone[0:cnt, 3 * c + j, :], ident[0:cnt, 0:cnt])
                for j, (lo, cnt) in enumerate(CUTS):
                    ins = pe.transpose(pH[0:cnt, j * P:(j + 1) * P], wdoned[:, lo:lo + cnt], ident)
                ins.then_inc(wt_pe, 1)
                pe.wait_ge(wt_done, 1)
                with pe.Fori(0, BLOCKS) as n:
                    pe.wait_ge(xq_done, n + 1)
                    for t in range(BT):
                        ins = pe.transpose(pT[:, t * P:(t + 1) * P], xq[:, t, :], ident)
                    ins.then_inc(t_pe, 1)
                    pe.wait_ge(xqT_done, n + 1)
                    for t in range(BT):
                        if t >= 2:
                            pe.wait_ge(hid_done, n * BT + t - 1)
                        tok = xqT[:, t * P:(t + 1) * P]
                        pe.matmul(pG[t % 2][:, 0:I], tok, wgu[:, 0:I], start=True, stop=True)
                        pe.matmul(pU[t % 2][:, 0:I], tok, wgu[:, I:2 * I], start=True, stop=True).then_inc(gu_pe, 1)
                    pe.wait_ge(hq_done, n + 1)
                    for t in range(BT + 1):
                        if t < BT:
                            if t >= 1:
                                pe.wait_ge(hT_done, n * BT + t)
                            for j, (lo, cnt) in enumerate(CUTS):
                                ins = pe.transpose(pH[0:cnt, j * P:(j + 1) * P], hq[:, t, lo:lo + cnt], ident)
                            ins.then_inc(h_pe, 1)
                        if t >= 1:
                            pe.wait_ge(hT_done, n * BT + t)
                            for j, (lo, cnt) in enumerate(CUTS):
                                ins = pe.matmul(pO[:, (t - 1) * D:t * D], hT[(t - 1) % 2][0:cnt, j * P:(j + 1) * P],
                                                wd[0:cnt, j, :], start=(j == 0), stop=(j == 2))
                    ins.then_inc(o_pe, 1)
        k.clear()


def one_head_attention(nc, core, tag, w):
    SCALE = float(D) ** -0.5
    with ExitStack() as stack:
        k = Held(nc, stack, tag)
        wqkv = k.sb("wqkv", [P, 3 * D]); bqk = k.sb("bqk", [P, 2]); bv = k.sb("bv", [1, D])
        ones1 = k.sb("ones1", [1, P]); maskq = k.sb("maskq", [P, P], BF16)
        stats = k.sb("stats", [P, QT, 6]); moments = k.sb("moments", [P, QT, 2])
        veps = k.sb("veps", [P, QT]); rstd = k.sb("rstd", [P, QT]); mhalf = k.sb("mhalf", [P, QT])
        xn = k.sb("xn", [P, QT, D]); xnT = k.sb("xnT", [P, SEQ])
        q = k.sb("q", [P, SEQ]); key = k.sb("key", [P, SEQ]); val = k.sb("val", [P, QT, D])
        mx = k.sb("mx", [P, QT]); negm = k.sb("negm", [P, QT]); ssum = k.sb("ssum", [P, QT]); rec = k.sb("rec", [P, QT])
        prob = k.sb("prob", [P, 3 * P]); probT = k.sb("probT", [P, 3 * P])
        pT = k.ps("pT", [P, BLK]); pQ = k.ps("pQ", [P, BLK]); pK = k.ps("pK", [P, BLK]); pV = k.ps("pV", [P, BLK])
        pS = k.ps("pS", [P, BLK]); pP = k.ps("pP", [P, BLK]); pO = k.ps("pO", [P, BLK])
        (w_in, setup, apart, stats_done, rstd_done, xn_done, t_pe, xnT_done, qkv_pe, qkv_done, s_pe, max_done,
         exp_done, pt_pe, probT_done, o_pe) = k.sem(
            "w_in setup apart stats_done rstd_done xn_done t_pe xnT_done qkv_pe qkv_done s_pe max_done "
            "exp_done pt_pe probT_done o_pe")
        COLS = [(0, 0, P), (1, P, 3 * P)]
        with nc.Block() as block:
            @block.sync
            def _(sp):
                for dst, src in ((wqkv, w["w"]), (bqk, w["bqk"]), (bv, w["bv"]), (maskq, core["maskq"])):
                    sp.dma_start(dst[:, :], src).then_inc(w_in, 16)

            @block.gpsimd
            def _(g):
                chain = Chain(g)
                g.memset(mhalf[:, :], -0.5).then_inc(setup, 1)
                g.memset(ones1[:, :], 1.0).then_inc(setup, 1)
                g.wait_ge(setup, 2)
                with g.Fori(0, SEQS) as n:
                    g.wait_ge(stats_done, n + 1)
                    ln_rstd(g, chain, moments, veps, mhalf, rstd, 1e-5, rstd_done, apart)

            @block.vector
            def _(v):
                chain = Chain(v)
                with v.Fori(0, SEQS) as n:
                    src = rows(core["x"], n * QT, QT)
                    v.drain()
                    ln_stats(v, chain, src, stats, moments, stats_done)
                    v.wait_ge(rstd_done, n + 1)
                    ln_apply(v, src, moments, rstd, xn).then_inc(xn_done, 1)
                    v.wait_ge(s_pe, n + 1)
                    for t, lo, hi in COLS:
                        ins = v.tensor_reduce(mx[:, t:t + 1], pS[:, lo:hi], op=ALU.max, axis=AX.X, negate=True)
                    chain.link(ins)
                    v.tensor_scalar(negm[:, :], mx[:, :], SCALE, None, ALU.mult).then_inc(max_done, 1)
                    v.wait_ge(exp_done, n + 1)
                    chain.link(v.reciprocal(rec[:, :], ssum[:, :]))
                    v.wait_ge(o_pe, n + 1)
                    for t in range(QT):
                        v.scalar_tensor_tensor(out=src[:, t, :], in0=pO[:, t * D:(t + 1) * D], scalar=rec[:, t:t + 1],
                                               in1=src[:, t, :], op0=ALU.mult, op1=ALU.add)

            @block.scalar
            def _(act):
                act.wait_ge(w_in, 64)
                with act.Fori(0, SEQS) as n:
                    act.wait_ge(t_pe, n + 1)
                    act.activation(xnT[:, :], pT[:, 0:SEQ], ACT.Copy).then_inc(xnT_done, 1)
                    act.wait_ge(qkv_pe, n + 1)
                    act.activation(q[:, :], pQ[:, 0:SEQ], ACT.Identity, bias=bqk[:, 0:1])
                    act.activation(key[:, :], pK[:, 0:SEQ], ACT.Identity, bias=bqk[:, 1:2])
                    act.activation(val[:, :, :].rearrange("p t d -> p (t d)"), pV[:, 0:SEQ], ACT.Copy
                                   ).then_inc(qkv_done, 1)
                    act.wait_ge(max_done, n + 1)
                    for t, lo, hi in COLS:
                        ins = act.activation(prob[:, lo:hi], pS[:, lo:hi], ACT.Exp, bias=negm[:, t:t + 1],
                                             scale=SCALE, accum_out=ssum[:, t:t + 1])
                    ins.then_inc(exp_done, 1)
                    act.wait_ge(pt_pe, n + 1)
                    act.activation(probT[:, :], pP[:, 0:3 * P], ACT.Copy).then_inc(probT_done, 1)

            @block.tensor
            def _(pe):
                ident = core["ident"]
                pe.wait_ge(w_in, 64)
                pe.wait_ge(setup, 2)
                with pe.Fori(0, SEQS) as n:
                    pe.wait_ge(xn_done, n + 1)
                    for t in range(QT):
                        ins = pe.transpose(pT[:, t * P:(t + 1) * P], xn[:, t, :], ident)
                    ins.then_inc(t_pe, 1)
                    pe.wait_ge(xnT_done, n + 1)
                    pe.matmul(pQ[:, 0:SEQ], wqkv[:, 0:D], xnT[:, :], start=True, stop=True)
                    pe.matmul(pK[:, 0:SEQ], wqkv[:, D:2 * D], xnT[:, :], start=True, stop=True)
                    for t in range(QT):
                        out = pV[:, t * D:(t + 1) * D]
                        pe.matmul(out, xnT[:, t * P:(t + 1) * P], wqkv[:, 2 * D:3 * D], start=True, stop=False)
                        ins = pe.matmul(out, ones1[:, :], bv[:, :], start=False, stop=True)
                    ins.then_inc(qkv_pe, 1)
                    pe.wait_ge(qkv_done, n + 1)
                    for t, lo, hi in COLS:
                        pe.matmul(pS[:, lo:hi], q[:, t * P:(t + 1) * P], key[:, 0:hi - lo], start=True, stop=False)
                        ins = pe.matmul(pS[:, hi - P:hi], core["identb"], maskq[:, :], start=False, stop=True)
                    ins.then_inc(s_pe, 1)
                    pe.wait_ge(exp_done, n + 1)
                    for c in range(3):
                        ins = pe.transpose(pP[:, c * P:(c + 1) * P], prob[:, c * P:(c + 1) * P], ident)
                    ins.then_inc(pt_pe, 1)
                    pe.wait_ge(probT_done, n + 1)
                    pe.matmul(pO[:, 0:D], probT[:, 0:P], val[:, 0, :], start=True, stop=True)
                    pe.matmul(pO[:, D:2 * D], probT[:, P:2 * P], val[:, 0, :], start=True, stop=False)
                    pe.matmul(pO[:, D:2 * D], probT[:, 2 * P:3 * P], val[:, 1, :], start=False, stop=True
                              ).then_inc(o_pe, 1)
        k.clear()


def adapters(nc, core, tag, w):
    E, R = 8, 64
    W = R + D + D + 3
    with ExitStack() as stack:
        k = Held(nc, stack, tag)
        every = k.sb("every", [P, E, W]); biases = k.sb("biases", [P, 3, E]); base = k.sb("base", [P, D]); baseb = k.sb("baseb", [P, 1])
        mu = k.sb("mu", [P, E]); sigma = k.sb("sigma", [P, E]); var = k.sb("var", [P, E]); iv = k.sb("iv", [P, E])
        muiv = k.sb("muiv", [P, E]); cross = k.sb("cross", [P, E]); square = k.sb("square", [P, E])
        iota = k.sb("iota", [1, E]); ones1 = k.sb("ones1", [1, P]); onescol = k.sb("onescol", [P, 1])
        stats = k.sb("stats", [P, QT, 6]); moments = k.sb("moments", [P, QT, 2])
        veps = k.sb("veps", [P, QT]); rstd = k.sb("rstd", [P, QT]); mhalf = k.sb("mhalf", [P, QT])
        xn = k.sb("xn", [P, QT, D]); xnT = k.sb("xnT", [P, SEQ]); sqr = k.sb("sqr", [P, SEQ])
        sum1 = k.sb("sum1", [P, 1]); sum2 = k.sb("sum2", [P, 1]); mean1 = k.sb("mean1", [P, 1])
        mean2 = k.sb("mean2", [P, 1])
        gain = k.sb("gain", [1, E]); best = k.sb("best", [1, E]); at = k.sb("at", [1, E], mybir.dt.uint32)
        atf = k.sb("atf", [1, 1]); hot = k.sb("hot", [1, E]); hotb = k.sb("hotb", [P, E])
        mine = [k.sb(f"mine{b}", [P, W]) for b in range(2)]; outb = k.sb("outb", [P, 1])
        hT = k.sb("hT", [R, SEQ]); aT = k.sb("aT", [P, SEQ]); yT = k.sb("yT", [P, SEQ])
        pT = k.ps("pT", [P, BLK]); pL = k.ps("pL", [P, BLK]); pB = k.ps("pB", [P, BLK]); pH = k.ps("pH", [P, BLK])
        pA = k.ps("pA", [P, BLK]); pY = k.ps("pY", [P, BLK]); pR = k.ps("pR", [P, BLK])
        (w_in, setup, apart, disc_done, stats_done, rstd_done, xn_done, t_pe, xnT_done, sq_done, mean_done, l_pe,
         hot_done, b_pe, mine_done, h_pe, hT_done, a_pe, aT_done, y_pe, yT_done, r_pe) = k.sem(
            "w_in setup apart disc_done stats_done rstd_done xn_done t_pe xnT_done sq_done mean_done l_pe "
            "hot_done b_pe mine_done h_pe hT_done a_pe aT_done y_pe yT_done r_pe")
        W_IN = 16 * 11
        DOWN, UP, CONV, BD, BU, BC = 0, R, R + D, R + 2 * D, R + 2 * D + 1, R + 2 * D + 2
        with nc.Block() as block:
            @block.sync
            def _(sp):
                sp.wait_ge(setup, 2)
                for dst, src in ((every[:, :, DOWN:DOWN + R], w["down"]), (every[0:R, :, UP:UP + D], w["up"]),
                                 (every[:, :, CONV:CONV + D], w["conv"]), (biases[0:R, 0, :], w["downb"]),
                                 (biases[:, 1, :], w["upb"]), (biases[:, 2, :], w["convb"]),
                                 (base[:, :], w["base"]), (baseb[:, :], w["baseb"]), (mu[:, :], w["mu"]),
                                 (sigma[:, :], w["sigma"]), (iota[:, :], core["iota8"])):
                    sp.dma_start(dst, src).then_inc(w_in, 16)

            @block.gpsimd
            def _(g):
                chain = Chain(g)
                g.memset(every[:, :, :], 0.0).then_inc(setup, 1)
                g.memset(biases[:, :, :], 0.0).then_inc(setup, 1)
                g.memset(mhalf[:, :], -0.5).then_inc(setup, 1)
                g.memset(ones1[:, :], 1.0).then_inc(setup, 1)
                g.memset(onescol[:, :], 1.0).then_inc(setup, 1)
                g.wait_ge(setup, 5)
                with g.Fori(0, SEQS) as n:
                    g.wait_ge(stats_done, n + 1)
                    ln_rstd(g, chain, moments, veps, mhalf, rstd, 1e-5, rstd_done, apart)

            @block.vector
            def _(v):
                chain = Chain(v)
                link = chain.link
                v.wait_ge(w_in, W_IN)
                v.wait_ge(setup, 5)
                v.tensor_copy(every[:, :, BD:BC + 1], biases[:, :, :].rearrange("p b e -> p e b"))
                link(v.tensor_tensor(var[:, :], sigma[:, :], sigma[:, :], op=ALU.mult))
                link(v.reciprocal(iv[:, :], var[:, :]))
                link(v.tensor_tensor(muiv[:, :], mu[:, :], iv[:, :], op=ALU.mult))
                link(v.tensor_scalar(cross[:, :], muiv[:, :], -2.0, None, ALU.mult))
                v.tensor_tensor(square[:, :], muiv[:, :], mu[:, :], op=ALU.mult).then_inc(disc_done, 1)
                with v.Fori(0, SEQS) as n:
                    src = rows(core["x"], n * QT, QT)
                    v.drain()
                    ln_stats(v, chain, src, stats, moments, stats_done)
                    v.wait_ge(rstd_done, n + 1)
                    ln_apply(v, src, moments, rstd, xn).then_inc(xn_done, 1)
                    v.wait_ge(xnT_done, n + 1)
                    link(v.tensor_reduce(sum1[:, :], xnT[:, :], op=ALU.add, axis=AX.X))
                    v.wait_ge(sq_done, n + 1)
                    v.tensor_scalar(mean1[:, :], sum1[:, :], 1.0 / SEQ, None, ALU.mult)
                    v.tensor_scalar(mean2[:, :], sum2[:, :], 1.0 / SEQ, None, ALU.mult).then_inc(mean_done, 1)
                    v.wait_ge(l_pe, n + 1)
                    link(v.tensor_scalar(gain[:, :], pL[0:1, 0:E], -1.0 / D, None, ALU.mult))
                    link(v.max(best[:, :], gain[:, :]))
                    link(v.max_index(at[:, :], best[:, :], gain[:, :]))
                    link(v.tensor_copy(atf[:, :], at[:, 0:1]))
                    v.tensor_scalar(hot[:, :], iota[:, :], atf[:, 0:1], None, ALU.is_equal).then_inc(hot_done, 1)
                    v.wait_ge(b_pe, n + 1)
                    link(v.tensor_copy(hotb[:, :], pB[:, 0:E]))
                    link(v.tensor_scalar(mine[0][:, :], every[:, 0, :], hotb[:, 0:1], None, ALU.mult))
                    for e in range(1, E):
                        link(v.scalar_tensor_tensor(out=mine[e % 2][:, :], in0=every[:, e, :], scalar=hotb[:, e:e + 1],
                                                    in1=mine[1 - e % 2][:, :], op0=ALU.mult, op1=ALU.add))
                    v.tensor_tensor(outb[:, :], mine[1][:, BC:BC + 1], baseb[:, :], op=ALU.add
                                    ).then_inc(mine_done, 1)
                    v.wait_ge(r_pe, n + 1)
                    v.tensor_tensor(src, pR[:, 0:SEQ].rearrange("p (t d) -> p t d", d=D), src, op=ALU.add)

            @block.scalar
            def _(act):
                mw = mine[1]
                with act.Fori(0, SEQS) as n:
                    act.wait_ge(t_pe, n + 1)
                    act.activation(xnT[:, :], pT[:, 0:SEQ], ACT.Copy).then_inc(xnT_done, 1)
                    act.activation(sqr[:, :], pT[:, 0:SEQ], ACT.Square, accum_out=sum2[:, 0:1]).then_inc(sq_done, 1)
                    act.wait_ge(mine_done, n + 1)
                    act.wait_ge(h_pe, n + 1)
                    act.activation(hT[:, :], pH[0:R, 0:SEQ], ACT.Relu, bias=mw[0:R, BD:BD + 1]).then_inc(hT_done, 1)
                    act.wait_ge(a_pe, n + 1)
                    act.activation(aT[:, :], pA[:, 0:SEQ], ACT.Identity, bias=mw[:, BU:BU + 1]).then_inc(aT_done, 1)
                    act.wait_ge(y_pe, n + 1)
                    act.activation(yT[:, :], pY[:, 0:SEQ], ACT.Identity, bias=outb[:, 0:1]).then_inc(yT_done, 1)

            @block.tensor
            def _(pe):
                ident, mw = core["ident"], mine[1]
                pe.wait_ge(w_in, W_IN)
                pe.wait_ge(disc_done, 1)
                with pe.Fori(0, SEQS) as n:
                    pe.wait_ge(xn_done, n + 1)
                    for t in range(QT):
                        ins = pe.transpose(pT[:, t * P:(t + 1) * P], xn[:, t, :], ident)
                    ins.then_inc(t_pe, 1)
                    pe.wait_ge(mean_done, n + 1)
                    pe.matmul(pL[0:1, 0:E], mean2[:, :], iv[:, :], start=True, stop=False)
                    pe.matmul(pL[0:1, 0:E], mean1[:, :], cross[:, :], start=False, stop=False)
                    pe.matmul(pL[0:1, 0:E], onescol[:, :], square[:, :], start=False, stop=True).then_inc(l_pe, 1)
                    pe.wait_ge(hot_done, n + 1)
                    pe.matmul(pB[:, 0:E], ones1[:, :], hot[:, :], start=True, stop=True).then_inc(b_pe, 1)
                    pe.wait_ge(mine_done, n + 1)
                    pe.matmul(pH[0:R, 0:SEQ], mw[:, DOWN:DOWN + R], xnT[:, :], start=True, stop=True).then_inc(h_pe, 1)
                    pe.matmul(pY[:, 0:SEQ], base[:, :], xnT[:, :], start=True, stop=False)
                    pe.wait_ge(hT_done, n + 1)
                    pe.matmul(pA[:, 0:SEQ], mw[0:R, UP:UP + D], hT[:, :], start=True, stop=True).then_inc(a_pe, 1)
                    pe.wait_ge(aT_done, n + 1)
                    pe.matmul(pY[:, 0:SEQ], mw[:, CONV:CONV + D], aT[:, :], start=False, stop=True).then_inc(y_pe, 1)
                    pe.wait_ge(yT_done, n + 1)
                    for t in range(QT):
                        ins = pe.transpose(pR[:, t * P:(t + 1) * P], yT[:, t * P:(t + 1) * P], ident)
                    ins.then_inc(r_pe, 1)
        k.clear()

def part_of(a, prefix):
    return {n[len(prefix):]: x for n, x in a.items() if n.startswith(prefix)}


def stage_a0(nc, core, a):
    attention(nc, core, "a0_", core["x"], 1e-5, part_of(a, "a0_"), False)


def stage_f0(nc, core, a):
    routed_experts(nc, core, "f0_", part_of(a, "f0_"))


def stage_a1(nc, core, a):
    normalise(nc, core, "i1_", core["x"], 1e-5, "init")
    with nc.Fori(0, 4) as layer:
        attention(nc, core, "a1_", core["h"], 1e-6, part_of(a, "a1_"), True, layer)
        feed_forward(nc, core, "f1_", core["h"], 1e-6, part_of(a, "f1_"), True, layer)


def stage_r1(nc, core, a):
    top2_experts(nc, core, "r1_", part_of(a, "r1_"))


def stage_l2(nc, core, a):
    performer(nc, core, "p2_", part_of(a, "p2_"))
    feed_forward(nc, core, "g2_", core["h"], 1e-6, part_of(a, "g2_"), False)
    normalise(nc, core, "n2_", core["h"], 1e-6, "add", a["n2_gb"])


def stage_q2(nc, core, a):
    fp4_feed_forward(nc, core, "q2_", part_of(a, "q2_"))


def stage_a3(nc, core, a):
    one_head_attention(nc, core, "a3_", part_of(a, "a3_"))


def stage_f3(nc, core, a):
    adapters(nc, core, "f3_", part_of(a, "f3_"))



def load_core(nc, a, pool):
    core = {}
    x = pool("x_store", [P, TILES, D])
    h = pool("h_store", [P, TILES, D])
    ident = pool("ident", [P, P])
    identb = pool("identb", [P, P], BF16)
    got = nc.alloc_semaphore("core_in")
    with nc.Block() as block:
        @block.sync
        def _(sp):
            sp.dma_start(ident[:, :], a["ident"]).then_inc(got, 16)
            sp.dma_start(identb[:, :], a["identb"]).then_inc(got, 16)
            for c in range(8):
                sp.dma_start(x[:, c * 8:(c + 1) * 8, :],
                             a["x"].rearrange("s (t p) d -> p (s t) d", p=P)[:, c * 8:(c + 1) * 8, :]
                             ).then_inc(got, 16)
            sp.wait_ge(got, 160)
    core.update(x=x, h=h, ident=ident[:, :], identb=identb[:, :])
    for name in ("maskq", "maskk", "esel", "turn", "kturn", "tri", "selhm", "sell", "diag", "iota8"):
        core[name] = a[name]
    return core


def store_out(nc, store, out):
    put = nc.alloc_semaphore("out_written")
    with nc.Block() as block:
        @block.sync
        def _(sp):
            for c in range(8):
                sp.dma_start(out.rearrange("s (t p) d -> p (s t) d", p=P)[:, c * 8:(c + 1) * 8, :],
                             store[:, c * 8:(c + 1) * 8, :]).then_inc(put, 16)
            sp.wait_ge(put, 128)

def constants():
    import numpy as np
    c = {}
    eye = np.eye(P, dtype=np.float32)
    q, k = np.arange(P)[:, None], np.arange(P)[None, :]
    above = np.where(k > q, NEG, 0.0).astype(np.float32)
    b16 = lambda t: t.astype(mybir.dt.np(BF16))
    c["ident"], c["identb"] = eye, b16(eye)
    c["maskq"], c["maskk"] = b16(above), b16(above.T)
    e = np.zeros((32, HEADS, P), np.float32)
    for h in range(HEADS):
        e[h, h], e[16 + h, h] = 1, 1
    c["esel"] = b16(e)
    inv = 1.0 / 10000.0 ** (np.arange(0, HD, 2) / HD)
    ang = np.arange(SEQ)[None, :] * inv[:, None]
    sin, cos = np.sin(ang), np.cos(ang)
    turn = np.stack([np.concatenate([sin, -cos]), np.concatenate([cos, sin])], 1)
    c["turn"] = np.tile(turn, (HEADS, 1, 1)).astype(np.float32)
    kt = np.concatenate([cos, sin]).astype(np.float32)
    parts = []
    for _ in range(3):
        parts.append(b16(kt))
        kt = kt - parts[-1].astype(np.float32)
    c["kturn"] = np.concatenate([parts[i] for i in KPART])
    c["diag"] = np.kron(np.eye(GH, dtype=np.float32), np.ones((32, 9), np.float32))
    c["iota8"] = np.arange(8, dtype=np.float32)[None]
    c["tri"] = np.tril(np.ones((8, 8), np.float32), -1).reshape(64)
    sel = np.zeros((64, 32, 128), np.float32)
    for e in range(64):
        sel[e, e // 2, 64 * (e % 2):64 * (e % 2) + 64] = 1
    c["selhm"], c["sell"] = b16(np.concatenate([sel, sel])), b16(sel)
    return c


TURN_A = [h * HD + r % 4 for h in range(HEADS) for r in range(HD)]
TURN_B = [h * HD + 4 + r % 4 for h in range(HEADS) for r in range(HD)]


def layout_rel(wq, wk, wv, wo, bq, bk, bv, bo, u, lnw, lnb):
    import numpy as np
    T = lambda m: m.transpose(0, 2, 1)
    uf = u.reshape(u.shape[0], D)
    return dict(
        wq=np.concatenate([T(wq), T(wk), T(wv)], 2), wo=T(wo),
        bqk=np.stack([bq, bk], 2), bv=bv[:, None, :], bo=bo[:, None, :], lnw=np.stack([lnw, lnb], 2),
        u12=np.concatenate([T(wq)[:, :, TURN_A], T(wq)[:, :, TURN_B]], 2),
        b12=np.stack([bq[:, TURN_A], bq[:, TURN_B], uf[:, TURN_A], uf[:, TURN_B]], 2))


def layout_all(i):
    import numpy as np
    T = lambda m: m.transpose(0, 2, 1)
    a = {}
    a["a0_wq"], a["a0_wo"] = i["L0_attn_w_in"].T, i["L0_attn_w_out"].T
    a["a0_bqk"] = i["L0_attn_b_in"][:2 * D].reshape(2, D).T
    a["a0_bv"], a["a0_bo"] = i["L0_attn_b_in"][None, 2 * D:], i["L0_attn_b_out"][None]
    a["f0_wg"] = i["L0_ffn_Wg"].transpose(1, 0, 2).reshape(D, -1)
    a["f0_wu"] = i["L0_ffn_Wu"].transpose(1, 0, 2).reshape(D, -1)
    a["f0_wd"] = i["L0_ffn_Wd"].reshape(32, P, D).transpose(1, 0, 2)
    a["f0_swg"], a["f0_swu"], a["f0_swd"] = i["L0_ffn_SWg"], i["L0_ffn_SWu"], i["L0_ffn_SWd"]
    a["f0_router"], a["f0_bias"] = i["L0_ffn_router_w"].T, i["L0_ffn_e_bias"]
    for n, x in layout_rel(*(i["L1_attn_" + n] for n in ("Wq", "Wk", "Wv", "Wo", "bq", "bk", "bv", "bo", "u_bias",
                                                           "ln1_w", "ln1_b"))).items():
        a["a1_" + n] = x
    a["f1_w1"] = T(i["L1_attn_W1"])
    a["f1_w2"] = T(i["L1_attn_W2"]).reshape(4, 4, P, D).transpose(0, 2, 1, 3)
    a["f1_ln"] = np.stack([i["L1_attn_ln2_w"], i["L1_attn_ln2_b"]], 2)
    a["f1_b1"] = i["L1_attn_b1"].reshape(4, 4, P).transpose(0, 2, 1)
    a["f1_b2"] = i["L1_attn_b2"][:, :, None]
    e = i["L1_ffn_expert_w"]
    a["r1_we"] = e.transpose(2, 0, 1).reshape(D, -1)
    a["r1_be"] = i["L1_ffn_expert_b"].reshape(-1)
    a["r1_gate"], a["r1_wc"] = i["L1_ffn_gate_w"].T, i["L1_ffn_combine_w"].T
    wq, wk, wv = (i["L2_attn_w" + n].reshape(D, D) for n in "qkv")
    a["p2_wqkv"] = np.concatenate([wq, wk, wv], 1)
    a["p2_wT"] = np.stack([wq.T, wk.T], 1)
    a["p2_omega"], a["p2_wo"] = i["L2_attn_omega"].T, i["L2_attn_wo"]
    a["g2_w1"], a["g2_w2"] = i["L2_attn_w1"], i["L2_attn_w2"].reshape(4, P, D).transpose(1, 0, 2)
    a["g2_ln"] = np.stack([i["L2_attn_ln1_g"], i["L2_attn_ln1_b"]], 1)
    a["g2_b1"], a["g2_b2"] = i["L2_attn_b1"].reshape(4, P).T, i["L2_attn_b2"][:, None]
    a["n2_gb"] = np.stack([i["L2_attn_ln2_g"], i["L2_attn_ln2_b"]], 0)
    a["q2_wg"], a["q2_wu"], a["q2_wd"] = (i["L2_ffn_w_" + n] for n in ("gate", "up", "down"))
    a["a3_w"] = i["L3_attn_W"]
    a["a3_bqk"], a["a3_bv"] = i["L3_attn_b"][:2 * D].reshape(2, D).T, i["L3_attn_b"][None, 2 * D:]
    f = {n: i["L3_ffn_" + n] for n in ("base_W", "base_b", "disc_mu", "disc_sigma", "down_W", "down_b", "up_W",
                                       "up_b", "conv_W", "conv_b")}
    a["f3_base"], a["f3_baseb"] = f["base_W"].T, f["base_b"][:, None]
    a["f3_mu"], a["f3_sigma"] = f["disc_mu"].T, f["disc_sigma"].T
    a["f3_down"] = f["down_W"].transpose(1, 0, 2)
    a["f3_up"] = f["up_W"].transpose(1, 0, 2)
    a["f3_conv"] = f["conv_W"].transpose(2, 0, 1)
    a["f3_downb"], a["f3_upb"], a["f3_convb"] = (f[n].T for n in ("down_b", "up_b", "conv_b"))
    return a


def program(nc, a, out):
    core = load_core(nc, a, lambda name, shape, dt=F32: nc.alloc_sbuf_tensor(name, shape, dt))
    stage_a0(nc, core, a)
    stage_f0(nc, core, a)
    stage_a1(nc, core, a)
    stage_r1(nc, core, a)
    stage_l2(nc, core, a)
    stage_q2(nc, core, a)
    stage_a3(nc, core, a)
    stage_f3(nc, core, a)
    store_out(nc, core["x"], out)


def kernel(**inputs):
    import numpy as np
    import concourse.bacc as bacc
    from concourse.bass_utils import run_bass_kernel_spmd

    laid = dict(constants(), x=np.asarray(inputs["L0_attn_x"]),
                **layout_all({name: np.asarray(x) for name, x in inputs.items()}))
    nc = bacc.Bacc("TRN2", target_bir_lowering=False, num_devices=1)
    arrays, a = {}, {}
    for name, x in laid.items():
        x = np.ascontiguousarray(x)
        arrays[f"in_{name}_dram"] = x
        a[name] = nc.dram_tensor(f"in_{name}_dram", x.shape, mybir.dt.from_np(x.dtype), kind="ExternalInput").ap()
    out = nc.dram_tensor("out_0_dram", (SEQS, SEQ, D), F32, kind="ExternalOutput").ap()
    program(nc, a, out)
    result = run_bass_kernel_spmd(nc, [arrays], core_ids=[0])
    return result.results[0]["out_0_dram"]
```

```python
import math

import concourse.bass as bass
from concourse import mybir
from contextlib import ExitStack

F32, BF16, I32 = mybir.dt.float32, mybir.dt.bfloat16, mybir.dt.int32
ALU = mybir.AluOpType
ACT = mybir.ActivationFunctionType
AX = mybir.AxisListType

P = 128
D = 128
SEQS, SEQ = 32, 256
TILES = SEQS * SEQ // P
QT = SEQ // P
BLK = 512
BT = BLK // P
BLOCKS = TILES // BT
HEADS, HD = 16, 8
GROUPS, GH = 4, 4
NEG = -1.0e30


class Chain:

    def __init__(self, eng):
        self.eng = eng

    def link(self, ins):
        self.eng.drain()


def rows(buf, first, count):
    return buf[:, bass.ds(first, count), :]


def ln_stats(v, chain, src, stats, moments, done):
    nt = src.shape[1]
    for t in range(nt):
        ins = v.bn_stats(stats[:, t, :], src[:, t, :])
    chain.link(ins)
    for t in range(nt):
        ins = v.bn_aggr(moments[:, t, :], stats[:, t, :])
    ins.then_inc(done, 1)


def ln_rstd(g, chain, moments, veps, minus_half, rstd, eps, done, apart):
    nt = rstd.shape[1]
    g.sem_inc(apart, 1)
    chain.link(g.tensor_scalar_add(veps[:, 0:nt], moments[:, 0:nt, 1], eps))
    g.tensor_tensor(rstd[:, 0:nt], veps[:, 0:nt], minus_half[:, 0:nt], op=ALU.pow).then_inc(done, 1)


def ln_apply(v, src, moments, rstd, xn):
    for t in range(src.shape[1]):
        ins = v.tensor_scalar(xn[:, t, :], src[:, t, :], moments[:, t, 0:1], rstd[:, t:t + 1],
                              ALU.subtract, ALU.mult)
    return ins


class Held:

    def __init__(self, nc, stack, tag):
        self.nc, self.stack, self.tag, self.sems = nc, stack, tag, []

    def sb(self, name, shape, dt=F32):
        return self.stack.enter_context(self.nc.sbuf_tensor(self.tag + name, shape, dt))

    def ps(self, name, shape, dt=F32):
        return self.stack.enter_context(self.nc.psum_tensor(self.tag + name, shape, dt))

    def sem(self, names):
        made = [self.stack.enter_context(self.nc.semaphore(self.tag + n)) for n in names.split()]
        self.sems += made
        return made if len(made) > 1 else made[0]

    def clear(self):
        for s in self.sems:
            self.nc.gpsimd.sem_clear(s)
        self.nc.all_engine_barrier()


def rounds(eng, step, count, behind=False):
    step(-1, True, False, False)
    step(0, True, True, False)
    with eng.Fori(0, count - 2) as i:
        step(i + 1, True, True, behind)
    step(count - 1, False, True, behind)
    if behind:
        step(count, False, False, True)


def later(n, least):
    return not isinstance(n, int) or n >= least


def row_moments(nc, core, tag, store, eps):
    with ExitStack() as stack:
        k = Held(nc, stack, tag)
        stats = k.sb("stats", [P, BT, 6]); moments = k.sb("moments", [P, BT, 2])
        veps = k.sb("veps", [P, TILES]); mhalf = k.sb("mhalf", [P, TILES])
        setup, veps_done, rstd_done = k.sem("setup veps_done rstd_done")
        with nc.Block() as block:
            @block.gpsimd
            def _(g):
                g.memset(mhalf[:, :], -0.5).then_inc(setup, 1)
                g.wait_ge(setup, 1)
                g.wait_ge(veps_done, 1)
                g.tensor_tensor(core["rstd"][:, :], veps[:, :], mhalf[:, :], op=ALU.pow).then_inc(rstd_done, 1)

            @block.vector
            def _(v):
                with v.Fori(0, BLOCKS) as n:
                    src = rows(store, n * BT, BT)
                    for t in range(BT):
                        v.bn_stats(stats[:, t, :], src[:, t, :])
                    v.drain()
                    for t in range(BT):
                        v.bn_aggr(moments[:, t, :], stats[:, t, :])
                    v.drain()
                    v.tensor_copy(core["mean"][:, bass.ds(n * BT, BT)], moments[:, :, 0])
                    v.tensor_scalar(veps[:, bass.ds(n * BT, BT)], moments[:, :, 1], eps, None, ALU.add)
                    v.drain()
                v.sem_inc(veps_done, 1)
                v.wait_ge(rstd_done, 1)
                v.drain()
        k.clear()


def normalised(v, core, src, first, centred, dst):
    nt = src.shape[1]
    wide = lambda m: core[m][:, bass.ds(first, nt)].unsqueeze(2).broadcast_to((P, nt, D))
    v.tensor_tensor(centred, src, wide("mean"), op=ALU.subtract)
    v.drain()
    return v.tensor_tensor(dst, centred, wide("rstd"), op=ALU.mult)

QPART = [0, 1, 2, 0, 1, 0]
KPART = [0, 0, 0, 1, 1, 2]


def attention(nc, core, tag, store, eps, w, rel, layer=None):
    NS = 3 if rel else 2
    K = 96 if rel else P
    READS = 6 * NS
    W_IN = 16 * (14 if rel else 8)
    SCALE = float(HD) ** -0.5
    with ExitStack() as held:
        def sb(name, shape, dt=F32):
            return held.enter_context(nc.sbuf_tensor(tag + name, shape, dt))

        def ps(name, shape, dt=F32):
            return held.enter_context(nc.psum_tensor(tag + name, shape, dt))

        sems = []

        def sem(name):
            s = held.enter_context(nc.semaphore(tag + name))
            sems.append(s)
            return s

        wq = sb("wq", [P, 3 * D]); wo = sb("wo", [P, D])
        bqk = sb("bqk", [P, 2]); bv = sb("bv", [1, D]); bo = sb("bo", [1, D])
        ones1 = sb("ones1", [1, P])
        mhalf = sb("mhalf", [P, QT])
        maskq = sb("maskq", [P, P], BF16); maskk = sb("maskk", [P, P], BF16)
        esel = sb("esel", [P, HEADS, P], BF16)
        stats = sb("stats", [P, QT, 6]); moments = sb("moments", [P, QT, 2])
        veps = sb("veps", [P, QT]); rstd = sb("rstd", [P, QT])
        xn = sb("xn", [P, QT, D]); xnT = [sb(f"xnT{b}", [P, SEQ]) for b in range(2)]
        f32s = sb("f32s", [P, NS, SEQ]); rest = sb("rest", [P, NS, SEQ])
        parts = [sb(f"parts{b}", [P, NS, 3, SEQ], BF16) for b in range(2)]
        sq = [sb(f"sq{b}", [K, HEADS, SEQ], BF16) for b in range(2)]
        sk = [sb(f"sk{b}", [K, HEADS, SEQ], BF16) for b in range(2)]
        vaug = [sb(f"vaug{b}", [P, QT, HEADS, 32]) for b in range(2)]
        mx = sb("mx", [P, QT, HEADS])
        mparts = sb("mparts", [P, QT, 2, HEADS], BF16)
        mT = sb("mT", [P, SEQ], BF16)
        prob = [sb(f"prob{b}", [P, 3 * BLK]) for b in range(2)]
        ctxp = [sb(f"ctxp{b}", [P, GROUPS, SEQ]) for b in range(2)]
        rec = sb("rec", [P, QT, HEADS]); cn = sb("cn", [P, QT, D]); cT = sb("cT", [P, SEQ])
        if rel:
            lnw = sb("lnw", [P, 2]); u12 = sb("u12", [P, 2 * D])
            b12 = sb("b12", [P, 4]); b12s = sb("b12s", [P, 2])
            turn = sb("turn", [P, 2, SEQ]); u1 = sb("u1", [P, SEQ]); u2 = sb("u2", [P, SEQ])
        else:
            guard = sb("guard", [P, QT, D]); isnum = sb("isnum", [P, QT, D], I32)
            zeros = sb("zeros", [P, QT, D])
            osb = sb("osb", [P, QT, D])
        scratch = [nc.dram_tensor(f"{tag}scratch{b}", (NS, 3, P, SEQ), BF16).ap() for b in range(2)]

        slot = [ps(f"slot{b}", [P, 3 * BLK]) for b in range(2)]
        ring = ps("ring", [P, BLK])
        pctx = ps("pctx", [P, BLK])
        bank = [slot[0][:, 0:BLK], slot[0][:, BLK:2 * BLK], slot[0][:, 2 * BLK:3 * BLK],
                slot[1][:, 0:BLK], slot[1][:, BLK:2 * BLK], slot[1][:, 2 * BLK:3 * BLK]]
        AT = dict(T=ring[:, 0:SEQ], C0=bank[0], C1=bank[1], Q=pctx[:, 0:SEQ], K=ring[:, 0:SEQ],
                  V=bank[3][:, 0:SEQ], U1=bank[4][:, 0:SEQ], U2=bank[5][:, 0:SEQ],
                  M=ring[:, 0:P].bitcast(BF16)[0:32, :], CT=pctx[:, 0:SEQ], OP=pctx[:, 0:SEQ])

        (w_in, setup, stats_done, rstd_done, xn_done, xnT_done, first_pe, v_pe, max_pe, out_pe, q_taken, k_taken, v_taken,
         u_taken, f32_done, parts_done, wrote0, wrote1, stack0, stack1, slot_pe, mx_done,
         mp_done, mT_done, exp_done, pv_done, ctx_taken, c_taken, cT_done, op_taken, apart, padded,
         ) = [sem(x) for x in (
             "w_in setup stats_done rstd_done xn_done xnT_done first_pe v_pe max_pe out_pe q_taken k_taken v_taken u_taken "
             "f32_done parts_done wrote0 wrote1 stack0 stack1 slot_pe mx_done mp_done mT_done "
             "exp_done pv_done ctx_taken c_taken cT_done op_taken apart padded").split()]
        wrote, stack = [wrote0, wrote1], [stack0, stack1]
        S1 = ["T", "Q", "K"] + (["U1", "U2"] if rel else [])
        S3 = ["C0", "C1", "CT", "OP"]

        def first(m, name):
            return m * len(S1) + S1.index(name) + 1

        def last(o, name):
            return o * len(S3) + S3.index(name) + 1

        def every_round(eng, step):
            step(-2, 0, -1, True, False, False, False)
            step(-1, 1, -1, True, True, False, False)
            step(0, 0, 0, True, True, True, False)
            with eng.Fori(0, (SEQS - 4) // 2) as i:
                step(i * 2 + 1, 1, i, True, True, True, True)
                step(i * 2 + 2, 0, i + 1, True, True, True, True)
            step(SEQS - 3, 1, SEQS // 2 - 2, True, True, True, True)
            step(SEQS - 2, 0, SEQS // 2 - 1, False, True, True, True)
            step(SEQS - 1, 1, SEQS // 2 - 1, False, False, True, True)
            step(SEQS, 0, SEQS // 2, False, False, False, True)

        with nc.Block() as block:
            @block.sync
            def _(sp):
                sp.wait_ge(padded, 2)
                loads = [(wq, w["wq"]), (wo, w["wo"]), (bqk, w["bqk"]), (bv, w["bv"]), (bo, w["bo"])]
                if rel:
                    loads += [(lnw, w["lnw"]), (u12, w["u12"]), (b12, w["b12"])]
                for dst, src in loads:
                    sp.dma_start(dst[:, :], src if layer is None else src[layer]).then_inc(w_in, 16)
                sp.dma_start(maskq[:, :], core["maskq"]).then_inc(w_in, 16)
                sp.dma_start(maskk[:, :], core["maskk"]).then_inc(w_in, 16)
                sp.dma_start(esel[0:32, :, :], core["esel"]).then_inc(w_in, 16)
                if rel:
                    sp.dma_start(turn[:, :, :], core["turn"]).then_inc(w_in, 16)
                    for b in range(2):
                        sp.dma_start(sk[b][48:96, :, :], core["kturn"].unsqueeze(1).broadcast_to((48, HEADS, SEQ))
                                     ).then_inc(w_in, 16)

                def step(n, b, half, qk, val, att, outp):
                    if not qk:
                        return
                    m = n + 2
                    sp.wait_ge(parts_done, m + 1)
                    if not isinstance(m, int) or m >= 2:
                        sp.wait_ge(pv_done, (m - 1) * GROUPS)
                    sp.dma_start(scratch[b].rearrange("c s p t -> p (c s) t"),
                                 parts[b][:, :, :, :].rearrange("p c s t -> p (c s) t")).then_inc(wrote[b], 16)
                    sp.wait_ge(wrote[b], (half + 2) * 16)
                    for c in range(6):
                        for comp, dst, part in ((0, sq[b], QPART[c]), (1, sk[b], KPART[c]),
                                                (2, sq[b], QPART[c]))[:NS]:
                            lo = c * HD + (48 if comp == 2 else 0)
                            sp.dma_start(dst[lo:lo + HD, :, :],
                                         scratch[b][comp, part].rearrange("(h r) t -> r h t", r=HD)
                                         ).then_inc(stack[b], 16)
                if not rel:
                    sp.wait_ge(padded, 6)
                every_round(sp, step)

            @block.gpsimd
            def _(g):
                chain = Chain(g)
                g.memset(mhalf[:, :], -0.5).then_inc(setup, 1)
                g.memset(ones1[:, :], 1.0).then_inc(setup, 1)
                for b in range(2):
                    g.memset(vaug[b][:, :, :, HD:32], 0.0).then_inc(setup, 1)
                g.wait_ge(setup, 4)
                for b in range(2):
                    g.memset(vaug[b][:, :, :, HD:HD + 1], 1.0).then_inc(setup, 1)
                if not rel:
                    g.wait_ge(padded, 2)
                    for b in range(2):
                        g.memset(sq[b][:, :, :], 0.0).then_inc(padded, 1)
                    g.memset(zeros[:, :, :], 0.0).then_inc(setup, 1)
                else:
                    g.wait_ge(w_in, W_IN)
                    g.tensor_tensor(b12s[:, :], b12[:, 0:2], b12[:, 2:4], op=ALU.add).then_inc(setup, 1)
                g.wait_ge(setup, 7)

                def step(n, b, half, qk, val, att, outp):
                    if not qk:
                        return
                    m = n + 2
                    g.wait_ge(stats_done, m + 1)
                    ln_rstd(g, chain, moments, veps, mhalf, rstd, eps, rstd_done, apart)
                    g.wait_ge(q_taken, m + 1)
                    g.wait_ge(k_taken, m + 1)
                    if rel:
                        g.wait_ge(f32_done, m + 1)
                    if not isinstance(m, int) or m >= 2:
                        g.wait_ge(wrote[b], (half + 1) * 16)
                    g.sem_inc(apart, 1)
                    pt = parts[b]
                    chain.link(g.tensor_copy(pt[:, :, 0, :], f32s[:, :, :]))
                    chain.link(g.tensor_tensor(rest[:, :, :], f32s[:, :, :], pt[:, :, 0, :], op=ALU.subtract))
                    chain.link(g.tensor_copy(pt[:, :, 1, :], rest[:, :, :]))
                    g.tensor_tensor(pt[:, :, 2, :], rest[:, :, :], pt[:, :, 1, :], op=ALU.subtract
                                    ).then_inc(parts_done, 1)
                every_round(g, step)

            @block.vector
            def _(v):
                chain = Chain(v)
                v.memset(esel[:, :, :], 0.0).then_inc(padded, 1)
                v.memset(mT[:, :], 0.0).then_inc(padded, 1)
                if not rel:
                    for b in range(2):
                        v.memset(sk[b][:, :, :], 0.0).then_inc(padded, 1)
                v.wait_ge(w_in, W_IN)
                v.wait_ge(setup, 7)

                def step(n, b, half, qk, val, att, outp):
                    m, o = n + 2, n - 1
                    v.drain()
                    if qk:
                        src = rows(store, m * QT, QT)
                        ln_stats(v, chain, src, stats, moments, stats_done)
                        v.wait_ge(rstd_done, m + 1)
                        if not isinstance(m, int) or m >= 1:
                            v.wait_ge(xnT_done, m)
                        ln_apply(v, src, moments, rstd, xn).then_inc(xn_done, 1)
                    if att:
                        for gr in range(GROUPS):
                            v.wait_ge(slot_pe, n * 8 + gr + 1)
                            sl = slot[gr % 2]
                            for t in range(QT):
                                w_ = P * (t + 1)
                                src = (sl[:, 0:BLK] if t == 0 else sl[:, BLK:3 * BLK]).rearrange(
                                    "p (h k) -> p h k", k=w_)
                                ins = v.tensor_reduce(mx[:, t, gr * GH:(gr + 1) * GH], src, op=ALU.max,
                                                      axis=AX.X, negate=True)
                            ins.then_inc(mx_done, 1)
                        v.wait_ge(mx_done, n * 4 + 4)
                        if not isinstance(n, int) or n >= 1:
                            v.wait_ge(mT_done, n)
                        chain.link(v.tensor_copy(mparts[:, :, 0, :], mx[:, :, :]))
                        v.tensor_tensor(mparts[:, :, 1, :], mx[:, :, :], mparts[:, :, 0, :],
                                        op=ALU.subtract).then_inc(mp_done, 1)
                    if outp:
                        for t in range(QT):
                            v.wait_ge(out_pe, last(o, "C%d" % t))
                            src = AT["C%d" % t].rearrange("p (h e) -> p h e", e=32)
                            chain.link(v.reciprocal(rec[:, t, :].unsqueeze(2), src[:, :, HD:HD + 1]))
                            v.tensor_tensor(cn[:, t, :].rearrange("p (h e) -> p h e", e=HD),
                                            src[:, :, 0:HD], rec[:, t, :].unsqueeze(2).broadcast_to((P, HEADS, HD)),
                                            op=ALU.mult).then_inc(c_taken, 1)
                    if qk and rel:
                        v.wait_ge(first_pe, first(m, "U1"))
                        v.scalar_tensor_tensor(out=u1[:, :], in0=AT["U1"], scalar=b12s[:, 0:1],
                                               in1=turn[:, 0, :], op0=ALU.add, op1=ALU.mult).then_inc(u_taken, 1)
                        v.wait_ge(first_pe, first(m, "U2"))
                        v.scalar_tensor_tensor(out=u2[:, :], in0=AT["U2"], scalar=b12s[:, 1:2],
                                               in1=turn[:, 1, :], op0=ALU.add, op1=ALU.mult).then_inc(u_taken, 1)
                        v.wait_ge(u_taken, m * 2 + 2)
                        if not isinstance(m, int) or m >= 1:
                            v.wait_ge(parts_done, m)
                        v.tensor_tensor(f32s[:, 2, :], u1[:, :], u2[:, :], op=ALU.add).then_inc(f32_done, 1)
                    if outp:
                        v.wait_ge(out_pe, last(o, "OP"))
                        dst = rows(store, o * QT, QT)
                        got = AT["OP"].rearrange("p (t d) -> p t d", d=D)
                        if rel:
                            v.tensor_tensor(dst, got, dst, op=ALU.add).then_inc(op_taken, 1)
                        else:
                            chain.link(v.tensor_copy(osb[:, :, :], got))
                            chain.link(v.tensor_tensor(isnum[:, :, :], osb[:, :, :], osb[:, :, :], op=ALU.is_equal))
                            chain.link(v.tensor_copy(guard[:, :, :], zeros[:, :, :]))
                            chain.link(v.copy_predicated(guard[:, :, :], isnum[:, :, :], osb[:, :, :]))
                            v.tensor_tensor(dst, guard[:, :, :], dst, op=ALU.add).then_inc(op_taken, 1)
                every_round(v, step)

            @block.scalar
            def _(act):
                act.wait_ge(w_in, W_IN)
                act.wait_ge(setup, 7)

                def step(n, b, half, qk, val, att, outp):
                    m, vb, o = n + 2, 1 - b, n - 1
                    if qk:
                        act.wait_ge(first_pe, first(m, "T"))
                        if not isinstance(m, int) or m >= 2:
                            act.wait_ge(v_pe, m - 1)
                        if rel:
                            act.activation(xnT[b][:, :], AT["T"], ACT.Identity, bias=lnw[:, 1:2],
                                           scale=lnw[:, 0:1]).then_inc(xnT_done, 1)
                        else:
                            act.activation(xnT[b][:, :], AT["T"], ACT.Copy).then_inc(xnT_done, 1)
                        if not isinstance(m, int) or m >= 1:
                            act.wait_ge(parts_done, m)
                        act.wait_ge(first_pe, first(m, "Q"))
                        act.activation(f32s[:, 0, :], AT["Q"], ACT.Identity, bias=bqk[:, 0:1]
                                       ).then_inc(q_taken, 1)
                        act.wait_ge(first_pe, first(m, "K"))
                        act.activation(f32s[:, 1, :], AT["K"], ACT.Identity, bias=bqk[:, 1:2]
                                       ).then_inc(k_taken, 1)
                    if val:
                        act.wait_ge(v_pe, n + 2)
                        act.activation(vaug[vb][:, :, :, 0:HD],
                                       AT["V"].rearrange("p (t h e) -> p t h e", t=QT, e=HD),
                                       ACT.Copy).then_inc(v_taken, 1)
                    if att:
                        act.wait_ge(max_pe, n + 1)
                        act.activation(mT[0:32, :], AT["M"], ACT.Copy).then_inc(mT_done, 1)
                    if outp:
                        act.wait_ge(out_pe, last(o, "CT"))
                        act.activation(cT[:, :], AT["CT"], ACT.Copy).then_inc(cT_done, 1)
                    if att:
                        def exps(gr):
                            act.wait_ge(slot_pe, n * 8 + 4 + gr + 1)
                            if gr >= 2 or not isinstance(n, int) or n >= 1:
                                act.wait_ge(pv_done, n * 4 + gr - 1)
                            act.activation(prob[gr % 2][:, :], slot[gr % 2][:, :], ACT.Exp, scale=SCALE
                                           ).then_inc(exp_done, 1)

                        def take(gr):
                            act.wait_ge(pv_done, n * 4 + gr + 1)
                            act.activation(ctxp[b][:, gr, :], pctx[:, 0:SEQ], ACT.Copy).then_inc(ctx_taken, 1)
                        exps(0)
                        exps(1)
                        take(0)
                        exps(2)
                        take(1)
                        exps(3)
                        take(2)
                        take(3)
                every_round(act, step)

            @block.tensor
            def _(pe):
                pe.wait_ge(w_in, W_IN)
                pe.wait_ge(setup, 7)
                if not rel:
                    pe.wait_ge(padded, 6)
                ident, identb = core["ident"], core["identb"]

                def step(n, b, half, qk, val, att, outp):
                    m, vb, o, ob = n + 2, 1 - b, n - 1, 1 - b
                    known = isinstance(n, int)

                    def project(name, lhs):
                        pe.matmul(AT[name], lhs, xnT[b][:, :], start=True, stop=True
                                  ).then_inc(first_pe, 1)

                    def maxima(n, b, gr):
                        sl = slot[gr % 2]
                        if gr >= 2:
                            pe.wait_ge(mx_done, n * 4 + gr - 1)
                        for t in range(QT):
                            w_ = P * (t + 1)
                            for j in range(GH):
                                h = gr * GH + j
                                base = (0 if t == 0 else BLK) + j * w_
                                pe.matmul(sl[:, base:base + w_], sq[b][0:K, h, t * P:(t + 1) * P],
                                          sk[b][0:K, h, 0:w_], start=True, stop=False)
                                ins = pe.matmul(sl[:, base + w_ - P:base + w_], identb, maskq[:, :],
                                                start=False, stop=True)
                        ins.then_inc(slot_pe, 1)

                    def scores(gr):
                        sl = slot[gr % 2]
                        if gr >= 2:
                            pe.wait_ge(exp_done, n * 4 + gr - 1)
                        for t in range(QT):
                            w_ = SEQ - P * t
                            for j in range(GH):
                                h = gr * GH + j
                                base = (0 if t == 0 else 2 * BLK) + j * w_
                                pe.matmul(sl[:, base:base + w_], esel[:, h, :], mT[:, t * P:SEQ],
                                          start=True, stop=False)
                                pe.matmul(sl[:, base:base + w_], sk[b][0:K, h, t * P:(t + 1) * P],
                                          sq[b][0:K, h, t * P:SEQ], start=False, stop=False)
                                ins = pe.matmul(sl[:, base:base + P], identb, maskk[:, :], start=False, stop=True)
                        ins.then_inc(slot_pe, 1)

                    def values(gr):
                        pe.wait_ge(exp_done, n * 4 + gr + 1)
                        if gr >= 1:
                            pe.wait_ge(ctx_taken, n * 4 + gr)
                        elif outp:
                            pe.wait_ge(op_taken, o + 1)
                        pb = prob[gr % 2]
                        for j in range(GH):
                            h = gr * GH + j
                            out = pctx[32 * j:32 * j + 32, 0:SEQ]
                            pe.matmul(out, vaug[b][:, 0, h, :], pb[:, j * SEQ:(j + 1) * SEQ],
                                      start=True, stop=False)
                            ins = pe.matmul(out[:, P:SEQ], vaug[b][:, 1, h, :],
                                            pb[:, 2 * BLK + j * P:2 * BLK + (j + 1) * P], start=False, stop=True)
                        ins.then_inc(pv_done, 1)

                    if qk:
                        pe.wait_ge(xn_done, m + 1)
                        if not known or m >= 1:
                            pe.wait_ge(k_taken, m)
                        for t in range(QT):
                            ins = pe.transpose(AT["T"][:, t * P:(t + 1) * P], xn[:, t, :], ident)
                        ins.then_inc(first_pe, 1)
                    if att:
                        if known and n == 0:
                            pe.wait_ge(v_taken, 1)
                            if rel:
                                pe.wait_ge(u_taken, 4)
                        maxima(n, b, 1)
                    if qk:
                        pe.wait_ge(xnT_done, m + 1)
                        if not known or m >= 1:
                            pe.wait_ge(q_taken, m)
                        if outp:
                            pe.wait_ge(ctx_taken, o * 4 + 4)
                        project("Q", wq[:, 0:D])
                    if att:
                        maxima(n, b, 2)
                    if qk:
                        project("K", wq[:, D:2 * D])
                    if att:
                        maxima(n, b, 3)
                        pe.wait_ge(mx_done, n * 4 + 3)
                    if outp:
                        pe.wait_ge(ctx_taken, o * 4 + 4)
                        for t in range(QT):
                            for gr in range(GROUPS):
                                ins = pe.transpose(AT["C%d" % t][:, gr * P:(gr + 1) * P],
                                                   ctxp[ob][:, gr, t * P:(t + 1) * P], ident)
                            ins.then_inc(out_pe, 1)
                    if att:
                        pe.wait_ge(mx_done, n * 4 + 4)
                    if val:
                        for t in range(QT):
                            out = AT["V"][:, t * D:(t + 1) * D]
                            pe.matmul(out, xnT[vb][:, t * P:(t + 1) * P], wq[:, 2 * D:3 * D], start=True, stop=False)
                            ins = pe.matmul(out, ones1[:, :], bv[:, :], start=False, stop=True)
                        ins.then_inc(v_pe, 1)
                    if qk:
                        if rel:
                            if known and m == 1:
                                pe.wait_ge(u_taken, 2)
                            project("U1", u12[:, 0:D])
                            project("U2", u12[:, D:2 * D])
                    if att:
                        pe.wait_ge(mp_done, n + 1)
                        if qk:
                            pe.wait_ge(k_taken, m + 1)
                        for t in range(QT):
                            ins = pe.transpose(AT["M"][:, t * P:(t + 1) * P],
                                               mparts[:, t, :, :].rearrange("p c h -> p (c h)"), identb)
                        ins.then_inc(max_pe, 1)
                    if outp:
                        pe.wait_ge(c_taken, o * 2 + 2)
                        if qk:
                            pe.wait_ge(q_taken, m + 1)
                        for t in range(QT):
                            ins = pe.transpose(AT["CT"][:, t * P:(t + 1) * P], cn[:, t, :], ident)
                        ins.then_inc(out_pe, 1)
                        pe.wait_ge(cT_done, o + 1)
                        for t in range(QT):
                            out = AT["OP"][:, t * D:(t + 1) * D]
                            pe.matmul(out, cT[:, t * P:(t + 1) * P], wo[:, :], start=True, stop=False)
                            ins = pe.matmul(out, ones1[:, :], bo[:, :], start=False, stop=True)
                        ins.then_inc(out_pe, 1)
                    if att:
                        pe.wait_ge(mT_done, n + 1)
                        if qk:
                            pe.wait_ge(q_taken, m + 1)
                        scores(0)
                        if val:
                            pe.wait_ge(v_taken, n + 2)
                        if qk and rel:
                            pe.wait_ge(u_taken, m * 2 + 2)
                        scores(1)
                        values(0)
                        scores(2)
                        values(1)
                        scores(3)
                        values(2)
                    if val:
                        pe.wait_ge(stack[vb], (half + 1 + b) * 16 * READS)
                        maxima(n + 1, vb, 0)
                    if att:
                        values(3)
                every_round(pe, step)
        for s in sems:
            nc.gpsimd.sem_clear(s)
        nc.all_engine_barrier()

def feed_forward(nc, core, tag, store, eps, w, add_to_store, layer=None):
    CH = 4
    with ExitStack() as stack:
        k = Held(nc, stack, tag)
        w1 = k.sb("w1", [P, CH * P]); w2 = k.sb("w2", [P, CH, D])
        lnw = k.sb("lnw", [P, 2]); b1 = k.sb("b1", [P, CH]); b2 = k.sb("b2", [P, 1])
        stats = k.sb("stats", [P, BT, 6]); moments = k.sb("moments", [P, BT, 2])
        veps = k.sb("veps", [P, BT]); rstd = k.sb("rstd", [P, BT]); mhalf = k.sb("mhalf", [P, BT])
        xn = k.sb("xn", [P, BT, D]); xnT = k.sb("xnT", [P, BLK])
        act_out = k.sb("act_out", [P, CH, BLK]); oT = k.sb("oT", [P, BLK])
        pT = k.ps("pT", [P, BLK]); pH = [k.ps(f"pH{c}", [P, BLK]) for c in range(CH)]
        pO = k.ps("pO", [P, BLK]); pR = k.ps("pR", [P, BLK])
        (w_in, setup, apart, stats_done, rstd_done, xn_done, t_pe, xnT_done, h_pe, gelu_done, o_pe, o_done,
         r_pe, r_taken) = k.sem("w_in setup apart stats_done rstd_done xn_done t_pe xnT_done h_pe gelu_done "
                                "o_pe o_done r_pe r_taken")
        W_IN = 16 * 5

        with nc.Block() as block:
            @block.sync
            def _(sp):
                for dst, name in ((w1[:, :], "w1"), (w2[:, :, :], "w2"), (lnw[:, :], "ln"), (b1[:, :], "b1"),
                                  (b2[:, :], "b2")):
                    sp.dma_start(dst, w[name] if layer is None else w[name][layer]).then_inc(w_in, 16)

            @block.gpsimd
            def _(g):
                chain = Chain(g)
                g.memset(mhalf[:, :], -0.5).then_inc(setup, 1)
                g.wait_ge(setup, 1)

                def step(n, ahead, now, back):
                    if ahead:
                        g.wait_ge(stats_done, n + 2)
                        ln_rstd(g, chain, moments, veps, mhalf, rstd, eps, rstd_done, apart)
                rounds(g, step, BLOCKS)

            @block.vector
            def _(v):
                chain = Chain(v)

                def step(n, ahead, now, back):
                    if ahead:
                        m = n + 1
                        src = rows(store, m * BT, BT)
                        v.drain()
                        ln_stats(v, chain, src, stats, moments, stats_done)
                        v.wait_ge(rstd_done, m + 1)
                        if later(m, 1):
                            v.wait_ge(xnT_done, m)
                        ln_apply(v, src, moments, rstd, xn).then_inc(xn_done, 1)
                    if now:
                        v.wait_ge(r_pe, n + 1)
                        dst = rows(store, n * BT, BT)
                        got = pR[:, :].rearrange("p (t d) -> p t d", d=D)
                        if add_to_store:
                            v.tensor_tensor(dst, got, dst, op=ALU.add).then_inc(r_taken, 1)
                        else:
                            v.tensor_copy(dst, got).then_inc(r_taken, 1)
                rounds(v, step, BLOCKS)

            @block.scalar
            def _(act):
                act.wait_ge(w_in, W_IN)

                def step(n, ahead, now, back):
                    if now:
                        for c in range(CH):
                            act.wait_ge(h_pe, n * CH + c + 1)
                            act.activation(act_out[:, c, :], pH[c][:, :], ACT.Gelu, bias=b1[:, c:c + 1]
                                           ).then_inc(gelu_done, 1)
                    if ahead:
                        act.wait_ge(t_pe, n + 2)
                        act.activation(xnT[:, :], pT[:, :], ACT.Identity, bias=lnw[:, 1:2], scale=lnw[:, 0:1]
                                       ).then_inc(xnT_done, 1)
                    if now:
                        act.wait_ge(o_pe, n + 1)
                        if later(n, 1):
                            act.wait_ge(r_pe, n)
                        act.activation(oT[:, :], pO[:, :], ACT.Identity, bias=b2[:, 0:1]).then_inc(o_done, 1)
                rounds(act, step, BLOCKS)

            @block.tensor
            def _(pe):
                pe.wait_ge(w_in, W_IN)

                def step(n, ahead, now, back):
                    if now:
                        pe.wait_ge(xnT_done, n + 1)
                        for c in range(CH):
                            pe.matmul(pH[c][:, :], w1[:, c * P:(c + 1) * P], xnT[:, :], start=True, stop=True
                                      ).then_inc(h_pe, 1)
                        if not add_to_store:
                            pe.matmul(pO[:, :], core["ident"], xnT[:, :], start=True, stop=False)
                    if ahead:
                        pe.wait_ge(xn_done, n + 2)
                        for t in range(BT):
                            ins = pe.transpose(pT[:, t * P:(t + 1) * P], xn[:, t, :], core["ident"])
                        ins.then_inc(t_pe, 1)
                    if now:
                        for c in range(CH):
                            pe.wait_ge(gelu_done, n * CH + c + 1)
                            ins = pe.matmul(pO[:, :], w2[:, c, :], act_out[:, c, :],
                                            start=(c == 0 and add_to_store), stop=(c == CH - 1))
                        ins.then_inc(o_pe, 1)
                        pe.wait_ge(o_done, n + 1)
                        if later(n, 1):
                            pe.wait_ge(r_taken, n)
                        for t in range(BT):
                            ins = pe.transpose(pR[:, t * P:(t + 1) * P], oT[:, t * P:(t + 1) * P], core["ident"])
                        ins.then_inc(r_pe, 1)
                rounds(pe, step, BLOCKS)
        k.clear()


def normalise(nc, core, tag, src_store, eps, then, w=None):
    with ExitStack() as stack:
        k = Held(nc, stack, tag)
        stats = k.sb("stats", [P, BT, 6]); moments = k.sb("moments", [P, BT, 2])
        veps = k.sb("veps", [P, BT]); rstd = k.sb("rstd", [P, BT]); mhalf = k.sb("mhalf", [P, BT])
        xn = k.sb("xn", [P, BT, D]); scaled = k.sb("scaled", [P, BT, D])
        gb = k.sb("gb", [P, 2, D])
        w_in, setup, apart, stats_done, rstd_done = k.sem("w_in setup apart stats_done rstd_done")
        with nc.Block() as block:
            if then == "add":
                @block.sync
                def _(sp):
                    sp.dma_start(gb[:, :, :], w.partition_broadcast(P)).then_inc(w_in, 16)

            @block.gpsimd
            def _(g):
                chain = Chain(g)
                g.memset(mhalf[:, :], -0.5).then_inc(setup, 1)
                g.wait_ge(setup, 1)
                with g.Fori(0, BLOCKS) as n:
                    g.wait_ge(stats_done, n + 1)
                    ln_rstd(g, chain, moments, veps, mhalf, rstd, eps, rstd_done, apart)

            @block.vector
            def _(v):
                chain = Chain(v)
                if then == "add":
                    v.wait_ge(w_in, 16)
                with v.Fori(0, BLOCKS) as n:
                    src = rows(src_store, n * BT, BT)
                    ln_stats(v, chain, src, stats, moments, stats_done)
                    v.wait_ge(rstd_done, n + 1)
                    if then == "init":
                        chain.link(ln_apply(v, src, moments, rstd, rows(core["h"], n * BT, BT)))
                    else:
                        chain.link(ln_apply(v, src, moments, rstd, xn))
                        chain.link(v.tensor_tensor(scaled[:, :, :], xn[:, :, :],
                                                   gb[:, 0:1, :].broadcast_to((P, BT, D)), op=ALU.mult))
                        chain.link(v.tensor_tensor(xn[:, :, :], scaled[:, :, :],
                                                   gb[:, 1:2, :].broadcast_to((P, BT, D)), op=ALU.add))
                        dst = rows(core["x"], n * BT, BT)
                        chain.link(v.tensor_tensor(dst, xn[:, :, :], dst, op=ALU.add))
        k.clear()

def routed_experts(nc, core, tag, w):
    E, GR, EG, TOPK, KG = 64, 8, 8, 8, 4
    CH = E // 2
    OUT_AT, T_AT, LOGIT_AT, COEF_AT = 1, 4, 8, 29
    ROUTE_AT = 11
    with ExitStack() as stack:
        k = Held(nc, stack, tag)
        wg = k.sb("wg", [P, (CH + 1) * P]); wu = k.sb("wu", [P, (CH + 1) * P]); wd = k.sb("wd", [P, CH + 1, D])
        wr = k.sb("wr", [P, E]); bias = k.sb("bias", [P, 1, E]); tri = k.sb("tri", [P, GR * GR])
        selhm = k.sb("selhm", [P, CH, P], BF16); sell = k.sb("sell", [E, CH, P], BF16)
        stats = k.sb("stats", [P, BT, 6]); moments = k.sb("moments", [P, BT, 2])
        veps = k.sb("veps", [P, BT]); rstd = k.sb("rstd", [P, BT]); mhalf = k.sb("mhalf", [P, BT])
        xn = k.sb("xn", [P, BT, D]); nextT = k.sb("nextT", [P, BLK]); xnT = k.sb("xnT", [P, BLK])
        score = k.sb("score", [P, BT, E]); sfc = k.sb("sfc", [P, BT * GR, EG])
        hi4 = k.sb("hi4", [P, BT * GR, 4]); lo4 = k.sb("lo4", [P, BT * GR, 4])
        hi2 = k.sb("hi2", [P, BT * GR, 2]); lo2 = k.sb("lo2", [P, BT * GR, 2]); mid2 = k.sb("mid2", [P, BT * GR, 2])
        hi1 = k.sb("hi1", [P, BT * GR, 1]); lo1 = k.sb("lo1", [P, BT * GR, 1]); mid1 = k.sb("mid1", [P, BT * GR, 1])
        gs = k.sb("gs", [P, BT * GR]); more = k.sb("more", [P, BT * GR, GR]); same = k.sb("same", [P, BT * GR, GR])
        rank = k.sb("rank", [P, BT * GR]); gmask = k.sb("gmask", [P, BT * GR])
        masked = k.sb("masked", [P, BT, E]); top = k.sb("top", [P, BT, 8]); left = k.sb("left", [P, BT, E])
        picked = k.sb("picked", [P, BT, E]); wsum = k.sb("wsum", [P, BT]); winv = k.sb("winv", [P, BT])
        coef = k.sb("coef", [P, BT, E]); crest = k.sb("crest", [P, BT, E])
        chm = k.sb("chm", [P, BT, 2, E], BF16); cl = k.sb("cl", [P, BT, E], BF16)
        nextc = k.sb("nextc", [P, BLK], BF16); nextl = k.sb("nextl", [E, BLK], BF16)
        nowc = k.sb("nowc", [P, BLK], BF16); nowl = k.sb("nowl", [E, BLK], BF16)
        silu = [k.sb(f"silu{b}", [P, BLK]) for b in range(2)]
        gated = k.sb("gated", [P, BLK]); hidden = [k.sb(f"hidden{b}", [P, BLK]) for b in range(2)]
        oT = k.sb("oT", [P, BLK])
        pG = [k.ps(f"pG{b}", [P, BLK]) for b in range(2)]; pU = [k.ps(f"pU{b}", [P, BLK]) for b in range(2)]
        pC = [k.ps(f"pC{b}", [P, BLK]) for b in range(2)]
        pO = k.ps("pO", [P, BLK]); misc = k.ps("misc", [P, BLK])
        miscb = misc[:, :].bitcast(BF16)
        (w_in, setup, apart, stats_done, rstd_done, xn_done, t_pe, nextT_done, logit_pe, score_done, coef_done,
         coef_pe, nextc_done, now_ready, g_pe, silu_done, uc_pe, hidden_done, o_pe, o_done, r_pe, r_taken
         ) = k.sem("w_in setup apart stats_done rstd_done xn_done t_pe nextT_done logit_pe score_done coef_done "
                   "coef_pe nextc_done now_ready g_pe silu_done uc_pe hidden_done o_pe o_done r_pe r_taken")
        NC = CH + 1
        W_IN = 16 * 11

        with nc.Block() as block:
            @block.sync
            def _(sp):
                for dst, src in ((wg[:, 0:CH * P], w["wg"]), (wg[:, CH * P:], w["swg"]), (wu[:, 0:CH * P], w["wu"]),
                                 (wu[:, CH * P:], w["swu"]), (wd[:, 0:CH, :], w["wd"]), (wd[:, CH, :], w["swd"]),
                                 (wr[:, :], w["router"]), (bias[:, 0, :], w["bias"].partition_broadcast(P)),
                                 (tri[:, :], core["tri"].partition_broadcast(P)),
                                 (selhm[:, :, :], core["selhm"]), (sell[:, :, :], core["sell"])):
                    sp.dma_start(dst, src).then_inc(w_in, 16)

            @block.gpsimd
            def _(g):
                chain = Chain(g)
                g.memset(mhalf[:, :], -0.5).then_inc(setup, 1)
                g.wait_ge(setup, 1)

                def step(n, ahead, now, back):
                    if ahead:
                        g.wait_ge(stats_done, n + 2)
                        ln_rstd(g, chain, moments, veps, mhalf, rstd, 1e-5, rstd_done, apart)
                rounds(g, step, BLOCKS, behind=True)

            @block.vector
            def _(v):
                chain = Chain(v)
                v.wait_ge(w_in, W_IN)

                def tt(out, a, b, op):
                    chain.link(v.tensor_tensor(out, a, b, op=op))

                def route(part, m):
                    if part == 0:
                        v.wait_ge(score_done, m + 1)
                        tt(sfc[:, :, :].rearrange("p (t g) e -> p t (g e)", g=GR), score[:, :, :],
                           bias[:, :, :].broadcast_to((P, BT, E)), ALU.add)
                        tt(hi4[:, :, :], sfc[:, :, 0:4], sfc[:, :, 4:8], ALU.max)
                        tt(lo4[:, :, :], sfc[:, :, 0:4], sfc[:, :, 4:8], ALU.min)
                        tt(hi2[:, :, :], hi4[:, :, 0:2], hi4[:, :, 2:4], ALU.max)
                    if part == 1:
                        tt(mid2[:, :, :], hi4[:, :, 0:2], hi4[:, :, 2:4], ALU.min)
                        tt(lo2[:, :, :], lo4[:, :, 0:2], lo4[:, :, 2:4], ALU.max)
                        tt(lo2[:, :, :], lo2[:, :, :], mid2[:, :, :], ALU.max)
                        tt(hi1[:, :, :], hi2[:, :, 0:1], hi2[:, :, 1:2], ALU.max)
                        tt(mid1[:, :, :], hi2[:, :, 0:1], hi2[:, :, 1:2], ALU.min)
                    if part == 2:
                        tt(lo1[:, :, :], lo2[:, :, 0:1], lo2[:, :, 1:2], ALU.max)
                        tt(lo1[:, :, :], lo1[:, :, :], mid1[:, :, :], ALU.max)
                        tt(gs[:, :].unsqueeze(2), hi1[:, :, :], lo1[:, :, :], ALU.add)
                        other = gs[:, :].rearrange("p (t o g) -> p t o g", o=1, g=GR).broadcast_to((P, BT, GR, GR))
                        own = gs[:, :].rearrange("p (t g o) -> p t g o", g=GR, o=1).broadcast_to((P, BT, GR, GR))
                        tt(more[:, :, :].rearrange("p (t g) h -> p t g h", g=GR), other, own, ALU.is_gt)
                    if part == 3:
                        other = gs[:, :].rearrange("p (t o g) -> p t o g", o=1, g=GR).broadcast_to((P, BT, GR, GR))
                        own = gs[:, :].rearrange("p (t g o) -> p t g o", g=GR, o=1).broadcast_to((P, BT, GR, GR))
                        tt(same[:, :, :].rearrange("p (t g) h -> p t g h", g=GR), other, own, ALU.is_equal)
                        before = tri[:, :].unsqueeze(1).broadcast_to((P, BT, GR * GR))
                        flat = same[:, :, :].rearrange("p (t g) h -> p t (g h)", g=GR)
                        tt(flat, flat, before, ALU.mult)
                        tt(more[:, :, :], more[:, :, :], same[:, :, :], ALU.add)
                    if part == 4:
                        chain.link(v.tensor_reduce(rank[:, :], more[:, :, :], op=ALU.add, axis=AX.X))
                        chain.link(v.tensor_scalar(gmask[:, :], rank[:, :], float(KG), None, ALU.is_lt))
                        tt(masked[:, :, :].rearrange("p t (g e) -> p (t g) e", e=EG), sfc[:, :, :],
                           gmask[:, :].unsqueeze(2).broadcast_to((P, BT * GR, EG)), ALU.mult)
                    if part == 5:
                        for t in range(BT):
                            ins = v.max(top[:, t, :], masked[:, t, :])
                        chain.link(ins)
                        for t in range(BT):
                            ins = v.match_replace(left[:, t, :], top[:, t, :], masked[:, t, :], -3.0e38)
                        chain.link(ins)
                    if part == 6:
                        chain.link(v.tensor_scalar(picked[:, :, :], left[:, :, :], -2.0e38, None, ALU.is_lt))
                        tt(picked[:, :, :], picked[:, :, :], score[:, :, :], ALU.mult)
                        chain.link(v.tensor_reduce(wsum[:, :], picked[:, :, :], op=ALU.add, axis=AX.X))
                        chain.link(v.tensor_scalar_add(wsum[:, :], wsum[:, :], 1e-20))
                        chain.link(v.reciprocal(winv[:, :], wsum[:, :]))
                    if part == 7:
                        tt(coef[:, :, :], picked[:, :, :], winv[:, :].unsqueeze(2).broadcast_to((P, BT, E)), ALU.mult)
                        chain.link(v.tensor_scalar(coef[:, :, :], coef[:, :, :], 2.5, None, ALU.mult))
                    if part == 8:
                        chain.link(v.tensor_copy(chm[:, :, 0, :], coef[:, :, :]))
                        tt(crest[:, :, :], coef[:, :, :], chm[:, :, 0, :], ALU.subtract)
                        chain.link(v.tensor_copy(chm[:, :, 1, :], crest[:, :, :]))
                        v.tensor_tensor(cl[:, :, :], crest[:, :, :], chm[:, :, 1, :], op=ALU.subtract
                                        ).then_inc(coef_done, 1)
                PARTS = 9

                def step(n, ahead, now, back):
                    m = n + 1
                    v.drain()
                    if ahead:
                        src = rows(core["x"], m * BT, BT)
                        ln_stats(v, chain, src, stats, moments, stats_done)
                        v.wait_ge(rstd_done, m + 1)
                        if later(m, 1):
                            v.wait_ge(nextT_done, m)
                        ln_apply(v, src, moments, rstd, xn).then_inc(xn_done, 1)
                    for c in range(NC if now else 0):
                        if c == OUT_AT + 1 and back:
                            v.wait_ge(r_pe, n)
                            dst = rows(core["x"], (n - 1) * BT, BT)
                            v.tensor_tensor(dst, misc[:, :].rearrange("p (t d) -> p t d", d=D), dst, op=ALU.add
                                            ).then_inc(r_taken, 1)
                        if ahead and ROUTE_AT <= c < ROUTE_AT + PARTS:
                            route(c - ROUTE_AT, m)
                        v.wait_ge(silu_done, n * NC + c + 1)
                        v.wait_ge(uc_pe, n * NC + c + 1)
                        if c < CH:
                            chain.link(v.tensor_tensor(gated[:, :], pU[c % 2][:, :], silu[c % 2][:, :], op=ALU.mult))
                            v.tensor_tensor(hidden[c % 2][:, :], pC[c % 2][:, :], gated[:, :], op=ALU.mult
                                            ).then_inc(hidden_done, 1)
                            v.drain()
                        else:
                            v.tensor_tensor(hidden[c % 2][:, :], pU[c % 2][:, :], silu[c % 2][:, :], op=ALU.mult
                                            ).then_inc(hidden_done, 1)
                    if ahead and not now:
                        for part in range(PARTS):
                            route(part, m)
                    if ahead:
                        v.wait_ge(nextc_done, m + 1)
                        if now:
                            v.wait_ge(uc_pe, (n + 1) * NC)
                        v.tensor_copy(xnT[:, :], nextT[:, :])
                        v.tensor_copy(nowc[:, :], nextc[:, :])
                        v.tensor_copy(nowl[:, :], nextl[:, :]).then_inc(now_ready, 1)
                    if back and not now:
                        v.wait_ge(r_pe, n)
                        dst = rows(core["x"], (n - 1) * BT, BT)
                        v.tensor_tensor(dst, misc[:, :].rearrange("p (t d) -> p t d", d=D), dst, op=ALU.add
                                        ).then_inc(r_taken, 1)
                rounds(v, step, BLOCKS, behind=True)

            @block.scalar
            def _(act):
                act.wait_ge(w_in, W_IN)

                def take_T(m):
                    act.wait_ge(t_pe, m + 1)
                    if later(m, 1):
                        act.wait_ge(now_ready, m)
                    act.activation(nextT[:, :], misc[:, :], ACT.Copy).then_inc(nextT_done, 1)

                def take_logits(m):
                    act.wait_ge(logit_pe, m + 1)
                    if later(m, 1):
                        act.wait_ge(coef_done, m)
                    act.activation(score[:, :, :], misc[:, 0:BT * E].rearrange("p (t e) -> p t e", e=E),
                                   ACT.Sigmoid).then_inc(score_done, 1)

                def take_coef(m):
                    act.wait_ge(coef_pe, m + 1)
                    act.activation(nextc[:, :], miscb[:, 0:BLK], ACT.Copy)
                    act.activation(nextl[:, :], miscb[0:E, BLK:2 * BLK], ACT.Copy).then_inc(nextc_done, 1)

                def step(n, ahead, now, back):
                    m = n + 1
                    for c in range(NC if now else 0):
                        if ahead and c == T_AT:
                            take_T(m)
                        if ahead and c == LOGIT_AT:
                            take_logits(m)
                        if ahead and c == COEF_AT:
                            take_coef(m)
                        act.wait_ge(g_pe, n * NC + c + 1)
                        if c >= 2 or later(n, 1):
                            act.wait_ge(hidden_done, n * NC + c - 1)
                        act.activation(silu[c % 2][:, :], pG[c % 2][:, :], ACT.Silu).then_inc(silu_done, 1)
                    if ahead and not now:
                        take_T(m)
                        take_logits(m)
                        take_coef(m)
                    if now:
                        act.wait_ge(o_pe, n + 1)
                        if later(n, 1):
                            act.wait_ge(r_pe, n)
                        act.activation(oT[:, :], pO[:, :], ACT.Copy).then_inc(o_done, 1)
                rounds(act, step, BLOCKS, behind=True)

            @block.tensor
            def _(pe):
                pe.wait_ge(w_in, W_IN)
                ident, identb = core["ident"], core["identb"]

                def make_T(m):
                    pe.wait_ge(xn_done, m + 1)
                    if later(m, 1):
                        pe.wait_ge(nextc_done, m)
                    for t in range(BT):
                        ins = pe.transpose(misc[:, t * P:(t + 1) * P], xn[:, t, :], ident)
                    ins.then_inc(t_pe, 1)

                def make_logits(m):
                    pe.wait_ge(nextT_done, m + 1)
                    for t in range(BT):
                        ins = pe.matmul(misc[:, t * E:(t + 1) * E], nextT[:, t * P:(t + 1) * P], wr[:, :],
                                        start=True, stop=True)
                    ins.then_inc(logit_pe, 1)

                def make_coef(m):
                    pe.wait_ge(coef_done, m + 1)
                    for t in range(BT):
                        pe.transpose(miscb[:, t * P:(t + 1) * P], chm[:, t, :, :].rearrange("p c e -> p (c e)"),
                                     identb)
                        ins = pe.transpose(miscb[0:E, BLK + t * P:BLK + (t + 1) * P], cl[:, t, :], identb)
                    ins.then_inc(coef_pe, 1)

                def make_out(o):
                    pe.wait_ge(o_done, o + 1)
                    for t in range(BT):
                        ins = pe.transpose(misc[:, t * P:(t + 1) * P], oT[:, t * P:(t + 1) * P], ident)
                    ins.then_inc(r_pe, 1)

                def step(n, ahead, now, back):
                    m = n + 1

                    def down(c):
                        pe.wait_ge(hidden_done, n * NC + c + 1)
                        if c == 0 and later(n, 1):
                            pe.wait_ge(o_done, n)
                        ins = pe.matmul(pO[:, :], wd[:, c, :], hidden[c % 2][:, :], start=(c == 0),
                                        stop=(c == NC - 1))
                        if c == NC - 1:
                            ins.then_inc(o_pe, 1)

                    if now:
                        pe.wait_ge(now_ready, n + 1)
                    for c in range(NC if now else 0):
                        if c == OUT_AT and back:
                            pe.wait_ge(nextc_done, n + 1)
                            make_out(n - 1)
                        if ahead and c == T_AT:
                            if back:
                                pe.wait_ge(r_taken, n)
                            make_T(m)
                        if ahead and c == LOGIT_AT:
                            make_logits(m)
                        if ahead and c == COEF_AT:
                            make_coef(m)
                        if c >= 2 or later(n, 1):
                            pe.wait_ge(hidden_done, n * NC + c - 1)
                        pe.matmul(pG[c % 2][:, :], wg[:, c * P:(c + 1) * P], xnT[:, :], start=True, stop=True
                                  ).then_inc(g_pe, 1)
                        ins = pe.matmul(pU[c % 2][:, :], wu[:, c * P:(c + 1) * P], xnT[:, :], start=True, stop=True)
                        if c < CH:
                            pe.matmul(pC[c % 2][:, :], selhm[:, c, :], nowc[:, :], start=True, stop=False)
                            ins = pe.matmul(pC[c % 2][:, :], sell[:, c, :], nowl[:, :], start=False, stop=True)
                        ins.then_inc(uc_pe, 1)
                        if c >= 1:
                            down(c - 1)
                    if now:
                        down(NC - 1)
                    if ahead and not now:
                        make_T(m)
                        make_logits(m)
                        make_coef(m)
                    if back and not now:
                        make_out(n - 1)
                rounds(pe, step, BLOCKS, behind=True)
        k.clear()

def top2_experts(nc, core, tag, w):
    E = 8
    with ExitStack() as stack:
        k = Held(nc, stack, tag)
        we = k.sb("we", [P, E * D]); wgate = k.sb("wgate", [P, E]); wc = k.sb("wc", [P, D])
        be = k.sb("be", [P, E * D]); tri = k.sb("tri", [P, E * E])
        stats = k.sb("stats", [P, BT, 6]); moments = k.sb("moments", [P, BT, 2])
        veps = k.sb("veps", [P, BT]); rstd = k.sb("rstd", [P, BT]); mhalf = k.sb("mhalf", [P, BT])
        xn = k.sb("xn", [P, BT, D]); xnT = k.sb("xnT", [P, BLK])
        lg = k.sb("lg", [P, BT, E]); mx = k.sb("mx", [P, BT]); ex = k.sb("ex", [P, BT, E])
        sm = k.sb("sm", [P, BT]); inv = k.sb("inv", [P, BT]); pr = k.sb("pr", [P, BT, E])
        more = k.sb("more", [P, BT * E, E]); same = k.sb("same", [P, BT * E, E]); rank = k.sb("rank", [P, BT, E])
        coef = k.sb("coef", [P, BT, E])
        pre = [k.sb(f"pre{b}", [P, E * D]) for b in range(2)]
        silu = [k.sb(f"silu{b}", [P, E, D]) for b in range(2)]
        part = [k.sb(f"part{b}", [P, E, D]) for b in range(2)]
        mixed = [k.sb(f"mixed{b}", [P, D]) for b in range(2)]; mixT = k.sb("mixT", [P, D])
        pT = k.ps("pT", [P, BLK]); pL = k.ps("pL", [P, BLK])
        pE = [k.ps(f"pE{b}", [P, E * D]) for b in range(2)]
        pM = k.ps("pM", [P, BLK]); pO = k.ps("pO", [P, BLK])
        (w_in, setup, apart, stats_done, rstd_done, xn_done, t_pe, xnT_done, logit_pe, max_done, exp_done,
         coef_done, e_pe, pre_done, silu_done, part_done, mixed_done, m_pe, mixT_done, o_pe, x_done
         ) = k.sem("w_in setup apart stats_done rstd_done xn_done t_pe xnT_done logit_pe max_done exp_done "
                   "coef_done e_pe pre_done silu_done part_done mixed_done m_pe mixT_done o_pe x_done")
        W_IN = 16 * 5
        with nc.Block() as block:
            @block.sync
            def _(sp):
                for dst, src in ((we, w["we"]), (wgate, w["gate"]), (wc, w["wc"]),
                                 (be, w["be"].partition_broadcast(P)), (tri, core["tri"].partition_broadcast(P))):
                    sp.dma_start(dst[:, :], src).then_inc(w_in, 16)

            @block.gpsimd
            def _(g):
                chain = Chain(g)
                g.memset(mhalf[:, :], -0.5).then_inc(setup, 1)
                g.wait_ge(setup, 1)

                def step(n, ahead, now, back):
                    if ahead:
                        g.wait_ge(stats_done, n + 2)
                        ln_rstd(g, chain, moments, veps, mhalf, rstd, 1e-5, rstd_done, apart)
                    if now:
                        for t in range(BT):
                            g.wait_ge(coef_done, n + 1)
                            g.wait_ge(silu_done, n * BT + t + 1)
                            g.sem_inc(apart, 1)
                            if t >= 2:
                                g.wait_ge(mixed_done, n * BT + t - 1)
                            g.tensor_tensor(part[t % 2][:, :, :], silu[t % 2][:, :, :],
                                            coef[:, t, :].unsqueeze(2).broadcast_to((P, E, D)), op=ALU.mult
                                            ).then_inc(part_done, 1)
                rounds(g, step, BLOCKS)

            @block.vector
            def _(v):
                chain = Chain(v)
                v.wait_ge(w_in, W_IN)

                def tt(out, a, b, op):
                    chain.link(v.tensor_tensor(out, a, b, op=op))

                def route(n):
                    v.wait_ge(logit_pe, n + 1)
                    logits = pL[:, 0:BT * E].rearrange("p (t e) -> p t e", e=E)
                    chain.link(v.tensor_reduce(mx[:, :], logits, op=ALU.max, axis=AX.X))
                    v.tensor_tensor(lg[:, :, :], logits, mx[:, :].unsqueeze(2).broadcast_to((P, BT, E)),
                                    op=ALU.subtract).then_inc(max_done, 1)
                    v.wait_ge(exp_done, n + 1)
                    chain.link(v.tensor_reduce(sm[:, :], ex[:, :, :], op=ALU.add, axis=AX.X))
                    chain.link(v.reciprocal(inv[:, :], sm[:, :]))
                    tt(pr[:, :, :], ex[:, :, :], inv[:, :].unsqueeze(2).broadcast_to((P, BT, E)), ALU.mult)
                    other = pr[:, :, :].unsqueeze(2).broadcast_to((P, BT, E, E))
                    own = pr[:, :, :].unsqueeze(3).broadcast_to((P, BT, E, E))
                    tt(more[:, :, :].rearrange("p (t g) h -> p t g h", g=E), other, own, ALU.is_gt)
                    tt(same[:, :, :].rearrange("p (t g) h -> p t g h", g=E), other, own, ALU.is_equal)
                    flat = same[:, :, :].rearrange("p (t g) h -> p t (g h)", g=E)
                    tt(flat, flat, tri[:, :].unsqueeze(1).broadcast_to((P, BT, E * E)), ALU.mult)
                    tt(more[:, :, :], more[:, :, :], same[:, :, :], ALU.add)
                    chain.link(v.tensor_reduce(rank[:, :, :].rearrange("p t e -> p (t e)"), more[:, :, :],
                                               op=ALU.add, axis=AX.X))
                    chain.link(v.tensor_scalar(rank[:, :, :], rank[:, :, :], 2.0, None, ALU.is_lt))
                    v.tensor_tensor(coef[:, :, :], rank[:, :, :], pr[:, :, :], op=ALU.mult).then_inc(coef_done, 1)

                def mix(n):
                    for t in range(BT + 1):
                        if t < BT:
                            v.wait_ge(e_pe, n * BT + t + 1)
                            v.tensor_tensor(pre[t % 2][:, :], pE[t % 2][:, :], be[:, :], op=ALU.add
                                            ).then_inc(pre_done, 1)
                        if t >= 1:
                            v.wait_ge(part_done, n * BT + t)
                            if t >= 3:
                                v.wait_ge(m_pe, n * BT + t - 2)
                            v.tensor_reduce(mixed[(t - 1) % 2][:, :],
                                            part[(t - 1) % 2][:, :, :].rearrange("p e d -> p d e"),
                                            op=ALU.add, axis=AX.X).then_inc(mixed_done, 1)

                def step(n, ahead, now, back):
                    m = n + 1
                    v.drain()
                    if now:
                        route(n)
                    if ahead:
                        src = rows(core["x"], m * BT, BT)
                        tt(src, src, rows(core["h"], m * BT, BT), ALU.add)
                        ln_stats(v, chain, src, stats, moments, stats_done)
                        v.wait_ge(rstd_done, m + 1)
                        if now:
                            v.wait_ge(t_pe, n + 1)
                        ln_apply(v, src, moments, rstd, xn).then_inc(xn_done, 1)
                    if now:
                        mix(n)
                        dst = rows(core["x"], n * BT, BT)
                        v.wait_ge(o_pe, n * BT + BT)
                        tt(dst, pO[:, :].rearrange("p (t d) -> p t d", d=D), dst, ALU.add)
                        v.sem_inc(x_done, 1)
                rounds(v, step, BLOCKS)

            @block.scalar
            def _(act):
                act.wait_ge(w_in, W_IN)

                def step(n, ahead, now, back):
                    m = n + 1
                    if now:
                        act.wait_ge(max_done, n + 1)
                        act.activation(ex[:, :, :], lg[:, :, :], ACT.Exp).then_inc(exp_done, 1)
                    for t in range(BT + 2):
                        if now and t < BT:
                            act.wait_ge(pre_done, n * BT + t + 1)
                            act.activation(silu[t % 2][:, :, :].rearrange("p e d -> p (e d)"), pre[t % 2][:, :],
                                           ACT.Silu).then_inc(silu_done, 1)
                        if now and t >= 2:
                            act.wait_ge(m_pe, n * BT + t - 1)
                            act.activation(mixT[:, :], pM[:, 0:D], ACT.Copy).then_inc(mixT_done, 1)
                        if ahead and t == BT - 1:
                            act.wait_ge(t_pe, m + 1)
                            act.activation(xnT[:, :], pT[:, :], ACT.Copy).then_inc(xnT_done, 1)
                rounds(act, step, BLOCKS)

            @block.tensor
            def _(pe):
                pe.wait_ge(w_in, W_IN)

                def step(n, ahead, now, back):
                    m = n + 1
                    if now:
                        pe.wait_ge(xnT_done, n + 1)
                        for t in range(BT):
                            ins = pe.matmul(pL[:, t * E:(t + 1) * E], xnT[:, t * P:(t + 1) * P], wgate[:, :],
                                            start=True, stop=True)
                        ins.then_inc(logit_pe, 1)
                    for t in range(BT + 2):
                        if now and t < BT:
                            if t >= 2:
                                pe.wait_ge(pre_done, n * BT + t - 1)
                            elif later(n, 1):
                                pe.wait_ge(pre_done, n * BT)
                            for half in range(2):
                                ins = pe.matmul(pE[t % 2][:, half * BLK:(half + 1) * BLK], xnT[:, t * P:(t + 1) * P],
                                                we[:, half * BLK:(half + 1) * BLK], start=True, stop=True)
                            ins.then_inc(e_pe, 1)
                        if now and t >= 2:
                            pe.wait_ge(mixed_done, n * BT + t - 1)
                            if later(n, 1):
                                pe.wait_ge(x_done, n)
                            pe.transpose(pM[:, 0:D], mixed[t % 2][:, :], core["ident"]).then_inc(m_pe, 1)
                            pe.wait_ge(mixT_done, n * BT + t - 1)
                            pe.matmul(pO[:, (t - 2) * D:(t - 1) * D], mixT[:, :], wc[:, :], start=True, stop=True
                                      ).then_inc(o_pe, 1)
                        if ahead and t == BT - 1:
                            pe.wait_ge(xn_done, m + 1)
                            for u in range(BT):
                                ins = pe.transpose(pT[:, u * P:(u + 1) * P], xn[:, u, :], core["ident"])
                            ins.then_inc(t_pe, 1)
                rounds(pe, step, BLOCKS)
        k.clear()


def performer(nc, core, tag, w):
    M = 32
    HM = HEADS * M
    KS = float(HD) ** -0.25
    LOGM = -0.5 * math.log(M)
    row_moments(nc, core, tag + "m_", core["x"], 1e-5)
    with ExitStack() as stack:
        k = Held(nc, stack, tag)
        wqkv = k.sb("wqkv", [P, 3 * D]); wT = k.sb("wT", [P, 2, P]); omega = k.sb("omega", [P, HM])
        wf = k.sb("wf", [P, 2, HM]); wo = k.sb("wo", [P, D]); diag = k.sb("diag", [P, GH * 9])
        logm = k.sb("logm", [P, 1])
        centred = k.sb("centred", [P, QT, D]); xn = k.sb("xn", [P, QT, D]); xnT = k.sb("xnT", [P, SEQ])
        sqr = k.sb("sqr", [P, 2 * D]); sqsum = k.sb("sqsum", [P, 2 * HEADS]); stab = k.sb("stab", [P, 2 * HEADS])
        shift = k.sb("shift", [P, 2 * HEADS]); arg = k.sb("arg", [P, 2, HM]); ex = k.sb("ex", [P, 2, HM])
        phi = k.sb("phi", [P, QT, 2, HM]); vaug = k.sb("vaug", [P, QT, HEADS, 9])
        phiT = k.sb("phiT", [P, QT, HM]); kv = k.sb("kv", [P, GROUPS, GH * 9])
        rec = k.sb("rec", [P, HEADS]); ctx = k.sb("ctx", [P, QT, D]); ctxT = k.sb("ctxT", [P, SEQ])
        pT = k.ps("pT", [P, BLK]); pF = [k.ps(f"pF{b}", [P, 2 * HM]) for b in range(2)]; pV = k.ps("pV", [P, BLK])
        pP = k.ps("pP", [P, BLK]); pK = k.ps("pK", [P, BLK])
        pN, pO = pK, pK
        (w_in, setup, wf_pe, wf_done, xn_done, t_pe, xnT_done, f_pe, sq_done,
         arg_done, ex_done, phi_done, v_done, pp_pe, phiT_done, kv_pe, kv_done, n_pe, ctx_done, c_pe, ctxT_done,
         o_pe) = k.sem(
            "w_in setup wf_pe wf_done xn_done t_pe xnT_done f_pe sq_done "
            "arg_done ex_done phi_done v_done pp_pe phiT_done kv_pe kv_done n_pe ctx_done c_pe ctxT_done "
            "o_pe")
        W_IN = 16 * (4 + HEADS)
        with nc.Block() as block:
            @block.sync
            def _(sp):
                sp.dma_start(wqkv[:, :], w["wqkv"]).then_inc(w_in, 16)
                sp.dma_start(wT[:, :, :], w["wT"]).then_inc(w_in, 16)
                sp.dma_start(wo[:, :], w["wo"]).then_inc(w_in, 16)
                sp.dma_start(diag[:, :], core["diag"]).then_inc(w_in, 16)
                sp.wait_ge(setup, 1)
                for h in range(HEADS):
                    sp.dma_start(omega[h * HD:(h + 1) * HD, h * M:(h + 1) * M], w["omega"]).then_inc(w_in, 16)

            @block.gpsimd
            def _(g):
                g.memset(omega[:, :], 0.0).then_inc(setup, 1)
                g.memset(vaug[:, :, :, 8:9], 1.0).then_inc(setup, 1)
                g.memset(logm[:, :], LOGM).then_inc(setup, 1)

            @block.vector
            def _(v):
                chain = Chain(v)
                v.wait_ge(w_in, W_IN)
                v.wait_ge(setup, 3)

                def args(m, t):
                    v.wait_ge(f_pe, m * QT + t + 1)
                    feats = pF[t][:, :].rearrange("p (h m) -> p h m", m=M)
                    chain.link(v.tensor_reduce(stab[:, :], feats, op=ALU.max, axis=AX.X))
                    v.wait_ge(sq_done, m * QT + t + 1)
                    chain.link(v.tensor_reduce(sqsum[:, :], sqr[:, :].rearrange("p (h e) -> p h e", e=HD),
                                               op=ALU.add, axis=AX.X))
                    chain.link(v.tensor_tensor(shift[:, :], stab[:, :], sqsum[:, :], op=ALU.add))
                    v.tensor_tensor(arg[:, :, :].rearrange("p c (h m) -> p (c h) m", m=M), feats,
                                    shift[:, :].unsqueeze(2).broadcast_to((P, 2 * HEADS, M)), op=ALU.subtract
                                    ).then_inc(arg_done, 1)

                def context(n, t):
                    v.wait_ge(n_pe, n * QT + t + 1)
                    num = pN[:, 0:HEADS * 9].rearrange("p (h e) -> p h e", e=9)
                    chain.link(v.reciprocal(rec[:, :].unsqueeze(2), num[:, :, 8:9]))
                    v.tensor_tensor(ctx[:, t, :].rearrange("p (h e) -> p h e", e=HD), num[:, :, 0:HD],
                                    rec[:, :].unsqueeze(2).broadcast_to((P, HEADS, HD)), op=ALU.mult
                                    ).then_inc(ctx_done, 1)

                def features(m, t):
                    v.wait_ge(ex_done, m * QT + t + 1)
                    v.tensor_scalar(phi[:, t, :, :], ex[:, :, :], 1e-6, None, ALU.add).then_inc(phi_done, 1)

                def step(n, ahead, now, back):
                    m = n + 1
                    v.drain()
                    if ahead:
                        normalised(v, core, rows(core["x"], m * QT, QT), m * QT, centred[:, :, :], xn[:, :, :]
                                   ).then_inc(xn_done, 1)
                        v.drain()
                        v.tensor_copy(rows(core["h"], m * QT, QT), xn[:, :, :])
                    if now:
                        v.wait_ge(kv_pe, n + 1)
                        v.tensor_tensor(kv[:, :, :], pK[:, 0:GROUPS * GH * 9].rearrange("p (g c) -> p g c", g=GROUPS),
                                        diag[:, :].unsqueeze(1).broadcast_to((P, GROUPS, GH * 9)), op=ALU.mult
                                        ).then_inc(kv_done, 1)
                        context(n, 0)
                    if ahead:
                        v.drain()
                        args(m, 0)
                    if now:
                        v.drain()
                        context(n, 1)
                    if ahead:
                        features(m, 0)
                        v.drain()
                        args(m, 1)
                    if now:
                        v.wait_ge(o_pe, n + 1)
                        dst = rows(core["h"], n * QT, QT)
                        v.tensor_tensor(dst, pO[:, 0:SEQ].rearrange("p (t d) -> p t d", d=D), dst, op=ALU.add)
                    if ahead:
                        features(m, 1)
                rounds(v, step, SEQS)

            @block.scalar
            def _(act):
                act.wait_ge(w_in, W_IN)
                act.wait_ge(setup, 3)
                act.wait_ge(wf_pe, 1)
                act.activation(wf[:, :, :].rearrange("p c m -> p (c m)"), pF[0][:, :], ACT.Copy, scale=KS
                               ).then_inc(wf_done, 1)

                def lengths(m, t):
                    act.wait_ge(f_pe, m * QT + t + 1)
                    act.activation(sqr[:, :], pV[:, 0:2 * D], ACT.Square, scale=KS * 0.5 ** 0.5
                                   ).then_inc(sq_done, 1)
                    act.activation(vaug[:, t, :, 0:HD], pV[:, 2 * D:3 * D].rearrange("p (h e) -> p h e", e=HD),
                                   ACT.Copy).then_inc(v_done, 1)

                def exponentials(m, t):
                    act.wait_ge(arg_done, m * QT + t + 1)
                    if t == 1:
                        act.wait_ge(phi_done, m * QT + 1)
                    act.activation(ex[:, :, :], arg[:, :, :], ACT.Exp, bias=logm[:, 0:1]).then_inc(ex_done, 1)

                def step(n, ahead, now, back):
                    m = n + 1
                    if now:
                        act.wait_ge(pp_pe, n * QT + 1)
                        act.activation(phiT[:, 0, :], pP[:, :], ACT.Copy).then_inc(phiT_done, 1)
                    if ahead:
                        act.wait_ge(t_pe, m + 1)
                        act.activation(xnT[:, :], pT[:, 0:SEQ], ACT.Copy).then_inc(xnT_done, 1)
                    if now:
                        act.wait_ge(pp_pe, n * QT + 2)
                        act.activation(phiT[:, 1, :], pP[:, :], ACT.Copy).then_inc(phiT_done, 1)
                    if ahead:
                        lengths(m, 0)
                        exponentials(m, 0)
                        lengths(m, 1)
                    if now:
                        act.wait_ge(c_pe, n + 1)
                        act.activation(ctxT[:, :], pT[:, 0:SEQ], ACT.Copy).then_inc(ctxT_done, 1)
                    if ahead:
                        exponentials(m, 1)
                rounds(act, step, SEQS)

            @block.tensor
            def _(pe):
                pe.wait_ge(w_in, W_IN)
                pe.wait_ge(setup, 3)
                ident = core["ident"]
                for c in range(2):
                    ins = pe.matmul(pF[0][:, c * HM:(c + 1) * HM], wT[:, c, :], omega[:, :], start=True, stop=True)
                ins.then_inc(wf_pe, 1)
                pe.wait_ge(wf_done, 1)

                def random_features(m, t):
                    if t == 1:
                        pe.wait_ge(v_done, m * QT + 1)
                    tok = xnT[:, t * P:(t + 1) * P]
                    for c in range(2):
                        pe.matmul(pF[t][:, c * HM:(c + 1) * HM], tok, wf[:, c, :], start=True, stop=True)
                    pe.matmul(pV[:, 0:3 * D], tok, wqkv[:, :], start=True, stop=True).then_inc(f_pe, 1)

                def phi_turned(n, t):
                    if t == 1:
                        pe.wait_ge(phiT_done, n * QT + 1)
                    for gr in range(GROUPS):
                        ins = pe.transpose(pP[:, gr * P:(gr + 1) * P], phi[:, t, 0, gr * P:(gr + 1) * P], ident)
                    ins.then_inc(pp_pe, 1)

                def numerators(n, t):
                    pe.wait_ge(phiT_done, n * QT + t + 1)
                    if t == 1:
                        pe.wait_ge(ctx_done, n * QT + 1)
                    else:
                        pe.wait_ge(kv_done, n + 1)
                    for gr in range(GROUPS):
                        ins = pe.matmul(pN[:, gr * 36:(gr + 1) * 36], phiT[:, t, gr * P:(gr + 1) * P],
                                        kv[:, gr, :], start=True, stop=True)
                    ins.then_inc(n_pe, 1)

                def step(n, ahead, now, back):
                    m = n + 1
                    if now:
                        pe.wait_ge(phi_done, n * QT + 2)
                        pe.wait_ge(v_done, n * QT + 2)
                        for gr in range(GROUPS):
                            for t in range(QT):
                                ins = pe.matmul(pK[:, gr * 36:(gr + 1) * 36], phi[:, t, 1, gr * P:(gr + 1) * P],
                                                vaug[:, t, gr * GH:(gr + 1) * GH, :].rearrange("p h e -> p (h e)"),
                                                start=(t == 0), stop=(t == QT - 1))
                        ins.then_inc(kv_pe, 1)
                        phi_turned(n, 0)
                    if ahead:
                        pe.wait_ge(xn_done, m + 1)
                        for t in range(QT):
                            ins = pe.transpose(pT[:, t * P:(t + 1) * P], xn[:, t, :], ident)
                        ins.then_inc(t_pe, 1)
                    if now:
                        phi_turned(n, 1)
                        numerators(n, 0)
                    if ahead:
                        pe.wait_ge(xnT_done, m + 1)
                        random_features(m, 0)
                    if now:
                        numerators(n, 1)
                    if ahead:
                        random_features(m, 1)
                    if now:
                        pe.wait_ge(ctx_done, n * QT + 2)
                        for t in range(QT):
                            ins = pe.transpose(pT[:, t * P:(t + 1) * P], ctx[:, t, :], ident)
                        ins.then_inc(c_pe, 1)
                        pe.wait_ge(ctxT_done, n + 1)
                        for t in range(QT):
                            ins = pe.matmul(pO[:, t * D:(t + 1) * D], ctxT[:, t * P:(t + 1) * P], wo[:, :],
                                            start=True, stop=True)
                        ins.then_inc(o_pe, 1)
                rounds(pe, step, SEQS)
        k.clear()

def fp4_feed_forward(nc, core, tag, w):
    I, B16 = 352, 16
    WIDE = BT * I
    CUTS = [(0, 128), (128, 128), (256, 96)]
    row_moments(nc, core, tag + "m_", core["x"], 1e-5)
    with ExitStack() as stack:
        k = Held(nc, stack, tag)
        raw = k.sb("raw", [P, 6, D]); rawd = k.sb("rawd", [P, I]); wdone = k.sb("wdone", [P, 6, D])
        wdoned = k.sb("wdoned", [P, I])
        wgu = k.sb("wgu", [P, 2 * I]); wd = k.sb("wd", [P, 3, D])
        centred = k.sb("centred", [P, BT, D])
        xn = k.sb("xn", [P, BT, D]); xq = k.sb("xq", [P, BT, D]); xqT = k.sb("xqT", [P, BLK])
        amax = k.sb("amax", [P, WIDE // B16]); scl = k.sb("scl", [P, WIDE // B16]); inv = k.sb("inv", [P, WIDE // B16])
        mag = k.sb("mag", [P, WIDE]); low = k.sb("low", [P, WIDE]); high = k.sb("high", [P, WIDE])
        silu = [k.sb(f"silu{b}", [P, I]) for b in range(2)]
        up = [k.sb(f"up{b}", [P, I]) for b in range(2)]
        hid = [k.sb(f"hid{b}", [P, BT, I]) for b in range(2)]; hq = k.sb("hq", [P, BT, I])
        hT = [k.sb(f"hT{b}", [P, 3 * P]) for b in range(2)]
        pT = k.ps("pT", [P, BLK])
        pG = [k.ps(f"pG{b}", [P, BLK]) for b in range(2)]; pU = [k.ps(f"pU{b}", [P, BLK]) for b in range(2)]
        pH = k.ps("pH", [P, BLK]); pO = k.ps("pO", [P, BLK])
        (w_in, setup, apart, wq_done, wt_pe, wt_done, xq_done, t_pe, xqT_done, gu_pe, silu_done,
         hid_done, hq_done, h_pe, hT_done, o_pe, x_done) = k.sem(
            "w_in setup apart wq_done wt_pe wt_done xq_done t_pe xqT_done gu_pe silu_done "
            "hid_done hq_done h_pe hT_done o_pe x_done")

        def pairs(eng, step):
            step(-1, 1, True, False, False)
            step(0, 0, True, True, False)
            with eng.Fori(0, (BLOCKS - 2) // 2) as i:
                step(i * 2 + 1, 1, True, True, True)
                step(i * 2 + 2, 0, True, True, True)
            step(BLOCKS - 1, 1, False, True, True)
            step(BLOCKS, 0, False, False, True)

        with nc.Block() as block:
            @block.sync
            def _(sp):
                sp.wait_ge(setup, 1)
                for c, name in ((0, "wg"), (3, "wu")):
                    sp.dma_start(raw[:, c:c + 2, :], w[name][0:2 * P, :].rearrange("(c p) d -> p c d", p=P)
                                 ).then_inc(w_in, 16)
                    sp.dma_start(raw[0:I - 2 * P, c + 2, :], w[name][2 * P:I, :]).then_inc(w_in, 16)
                sp.dma_start(rawd[:, :], w["wd"]).then_inc(w_in, 16)

            @block.gpsimd
            def _(g):
                g.memset(raw[:, :, :], 0.0).then_inc(setup, 1)

                def step(n, b, ahead, now, back):
                    if not ahead:
                        return
                    m, mb = n + 1, 1 - b
                    for t in range(BT):
                        g.wait_ge(silu_done, m * BT + t + 1)
                        if later(m, 2):
                            g.wait_ge(hq_done, m - 1)
                        g.sem_inc(apart, 1)
                        g.tensor_tensor(hid[mb][:, t, :], up[t % 2][:, :], silu[t % 2][:, :], op=ALU.mult
                                        ).then_inc(hid_done, 1)
                pairs(g, step)

            @block.vector
            def _(v):
                chain = Chain(v)
                v.wait_ge(w_in, 80)

                def quantise(src, dst, width):
                    nb = width // B16
                    am, sc, iv = amax[:, 0:nb], scl[:, 0:nb], inv[:, 0:nb]
                    ma, lo, hi = mag[:, 0:width], low[:, 0:width], high[:, 0:width]
                    by16 = lambda x: x.rearrange("p (b e) -> p b e", e=B16)
                    link = chain.link
                    link(v.tensor_reduce(am, by16(src), op=ALU.max, axis=AX.X, apply_absolute_value=True))
                    link(v.tensor_scalar(sc, am, 1.0 / 6.0, 1e-12, ALU.mult, ALU.max))
                    link(v.reciprocal(iv, sc))
                    link(v.tensor_tensor(by16(ma), by16(src), iv.unsqueeze(2).broadcast_to((P, nb, B16)), op=ALU.mult))
                    link(v.tensor_scalar(ma.bitcast(I32), ma.bitcast(I32), 0x7FFFFFFF, None, ALU.bitwise_and))
                    link(v.tensor_scalar(lo, ma, 0.25, None, ALU.is_gt))
                    for mid in (0.75, 1.25, 1.75):
                        link(v.scalar_tensor_tensor(out=lo, in0=ma, scalar=mid, in1=lo, op0=ALU.is_gt, op1=ALU.add))
                    link(v.tensor_scalar(hi, ma, 5.0, 2.0, ALU.is_gt, ALU.mult))
                    for mid in (2.5, 3.5):
                        link(v.scalar_tensor_tensor(out=hi, in0=ma, scalar=mid, in1=hi, op0=ALU.is_gt, op1=ALU.add))
                    link(v.scalar_tensor_tensor(out=hi, in0=lo, scalar=0.5, in1=hi, op0=ALU.mult, op1=ALU.add))
                    link(v.tensor_tensor(by16(lo), by16(hi), sc.unsqueeze(2).broadcast_to((P, nb, B16)), op=ALU.mult))
                    return v.scalar_tensor_tensor(out=dst.bitcast(I32), in0=src.bitcast(I32), scalar=-2147483648,
                                                  in1=lo.bitcast(I32), op0=ALU.bitwise_and, op1=ALU.bitwise_or)

                chain.link(quantise(raw[:, :, :].rearrange("p c d -> p (c d)"),
                                    wdone[:, :, :].rearrange("p c d -> p (c d)"), 6 * D))
                quantise(rawd[:, :], wdoned[:, :], I).then_inc(wq_done, 1)

                def step(n, b, ahead, now, back):
                    m, o = n + 1, n - 1
                    v.drain()
                    if ahead:
                        chain.link(normalised(v, core, rows(core["x"], m * BT, BT), m * BT, centred[:, :, :],
                                              xn[:, :, :]))
                        if later(m, 1):
                            v.wait_ge(t_pe, m)
                        chain.link(quantise(xn[:, :, :].rearrange("p t d -> p (t d)"),
                                            xq[:, :, :].rearrange("p t d -> p (t d)"), BLK))
                        v.sem_inc(xq_done, 1)
                    if back:
                        v.wait_ge(o_pe, o + 1)
                        dst = rows(core["x"], o * BT, BT)
                        v.tensor_tensor(dst, pO[:, :].rearrange("p (t d) -> p t d", d=D), dst, op=ALU.add
                                        ).then_inc(x_done, 1)
                    if now:
                        v.wait_ge(hid_done, n * BT + BT)
                        if later(n, 1):
                            v.wait_ge(h_pe, n * BT)
                        quantise(hid[b][:, :, :].rearrange("p t d -> p (t d)"),
                                 hq[:, :, :].rearrange("p t d -> p (t d)"), WIDE).then_inc(hq_done, 1)
                pairs(v, step)

            @block.scalar
            def _(act):
                act.wait_ge(wt_pe, 1)
                for c in range(2):
                    act.activation(wgu[:, c * I:(c + 1) * I], pG[c][:, 0:I], ACT.Copy)
                for c, (lo, cnt) in enumerate(CUTS):
                    ins = act.activation(wd[0:cnt, c, :], pH[0:cnt, c * P:(c + 1) * P], ACT.Copy)
                ins.then_inc(wt_done, 1)

                def step(n, b, ahead, now, back):
                    m = n + 1
                    if ahead:
                        act.wait_ge(t_pe, m + 1)
                        act.activation(xqT[:, :], pT[:, :], ACT.Copy).then_inc(xqT_done, 1)
                        for t in range(BT):
                            act.wait_ge(gu_pe, m * BT + t + 1)
                            if t >= 2 or later(m, 1):
                                act.wait_ge(hid_done, m * BT + t - 1)
                            act.activation(up[t % 2][:, :], pU[t % 2][:, 0:I], ACT.Copy)
                            act.activation(silu[t % 2][:, :], pG[t % 2][:, 0:I], ACT.Silu).then_inc(silu_done, 1)
                    if now:
                        for t in range(BT):
                            act.wait_ge(h_pe, n * BT + t + 1)
                            act.activation(hT[t % 2][:, 0:2 * P], pH[:, 0:2 * P], ACT.Copy)
                            act.activation(hT[t % 2][0:96, 2 * P:3 * P], pH[0:96, 2 * P:3 * P], ACT.Copy
                                           ).then_inc(hT_done, 1)
                pairs(act, step)

            @block.tensor
            def _(pe):
                ident = core["ident"]
                pe.wait_ge(wq_done, 1)
                for c in range(2):
                    for j, (lo, cnt) in enumerate(CUTS):
                        pe.transpose(pG[c][:, lo:lo + cnt], wdone[0:cnt, 3 * c + j, :], ident[0:cnt, 0:cnt])
                for j, (lo, cnt) in enumerate(CUTS):
                    ins = pe.transpose(pH[0:cnt, j * P:(j + 1) * P], wdoned[:, lo:lo + cnt], ident)
                ins.then_inc(wt_pe, 1)
                pe.wait_ge(wt_done, 1)

                def step(n, b, ahead, now, back):
                    m = n + 1
                    if ahead:
                        pe.wait_ge(xq_done, m + 1)
                        for t in range(BT):
                            ins = pe.transpose(pT[:, t * P:(t + 1) * P], xq[:, t, :], ident)
                        ins.then_inc(t_pe, 1)
                        pe.wait_ge(xqT_done, m + 1)
                        for t in range(BT):
                            if t >= 2:
                                pe.wait_ge(silu_done, m * BT + t - 1)
                            tok = xqT[:, t * P:(t + 1) * P]
                            pe.matmul(pG[t % 2][:, 0:I], tok, wgu[:, 0:I], start=True, stop=True)
                            pe.matmul(pU[t % 2][:, 0:I], tok, wgu[:, I:2 * I], start=True, stop=True
                                      ).then_inc(gu_pe, 1)
                    if now:
                        pe.wait_ge(hq_done, n + 1)
                        if later(n, 1):
                            pe.wait_ge(x_done, n)
                        for t in range(BT + 1):
                            if t < BT:
                                if t >= 1:
                                    pe.wait_ge(hT_done, n * BT + t)
                                for j, (lo, cnt) in enumerate(CUTS):
                                    ins = pe.transpose(pH[0:cnt, j * P:(j + 1) * P], hq[:, t, lo:lo + cnt], ident)
                                ins.then_inc(h_pe, 1)
                            if t >= 1:
                                pe.wait_ge(hT_done, n * BT + t)
                                for j, (lo, cnt) in enumerate(CUTS):
                                    ins = pe.matmul(pO[:, (t - 1) * D:t * D],
                                                    hT[(t - 1) % 2][0:cnt, j * P:(j + 1) * P],
                                                    wd[0:cnt, j, :], start=(j == 0), stop=(j == 2))
                        ins.then_inc(o_pe, 1)
                pairs(pe, step)
        k.clear()


def one_head_attention(nc, core, tag, w):
    SCALE = float(D) ** -0.5
    row_moments(nc, core, tag + "m_", core["x"], 1e-5)
    with ExitStack() as stack:
        k = Held(nc, stack, tag)
        wqkv = k.sb("wqkv", [P, 3 * D]); bqk = k.sb("bqk", [P, 2]); bv = k.sb("bv", [1, D])
        ones1 = k.sb("ones1", [1, P]); maskq = k.sb("maskq", [P, P], BF16)
        centred = k.sb("centred", [P, QT, D])
        xn = k.sb("xn", [P, QT, D]); xnT = k.sb("xnT", [P, SEQ])
        q = k.sb("q", [P, SEQ]); key = k.sb("key", [P, SEQ]); val = k.sb("val", [P, QT, D])
        mx = k.sb("mx", [P, QT]); negm = k.sb("negm", [P, QT]); ssum = k.sb("ssum", [P, QT]); rec = k.sb("rec", [P, QT])
        prob = k.sb("prob", [P, 3 * P]); probT = k.sb("probT", [P, 3 * P])
        pT = k.ps("pT", [P, BLK]); pQ = k.ps("pQ", [P, BLK]); pK = k.ps("pK", [P, BLK]); pV = k.ps("pV", [P, BLK])
        pS = k.ps("pS", [P, BLK]); pP = k.ps("pP", [P, BLK]); pO = k.ps("pO", [P, BLK])
        (w_in, setup, xn_done, t_pe, xnT_done, qkv_pe, qk_done, val_done, s_pe, max_done,
         exp_done, pt_pe, probT_done, o_pe, x_done) = k.sem(
            "w_in setup xn_done t_pe xnT_done qkv_pe qk_done val_done s_pe max_done "
            "exp_done pt_pe probT_done o_pe x_done")
        COLS = [(0, 0, P), (1, P, 3 * P)]
        with nc.Block() as block:
            @block.sync
            def _(sp):
                for dst, src in ((wqkv, w["w"]), (bqk, w["bqk"]), (bv, w["bv"]), (maskq, core["maskq"])):
                    sp.dma_start(dst[:, :], src).then_inc(w_in, 16)

            @block.gpsimd
            def _(g):
                g.memset(ones1[:, :], 1.0).then_inc(setup, 1)

            @block.vector
            def _(v):
                chain = Chain(v)

                def step(n, ahead, now, back):
                    m = n + 1
                    v.drain()
                    if ahead:
                        if now:
                            v.wait_ge(t_pe, n + 1)
                        normalised(v, core, rows(core["x"], m * QT, QT), m * QT, centred[:, :, :], xn[:, :, :]
                                   ).then_inc(xn_done, 1)
                    if now:
                        dst = rows(core["x"], n * QT, QT)
                        v.wait_ge(s_pe, n + 1)
                        for t, lo, hi in COLS:
                            ins = v.tensor_reduce(mx[:, t:t + 1], pS[:, lo:hi], op=ALU.max, axis=AX.X, negate=True)
                        chain.link(ins)
                        v.tensor_scalar(negm[:, :], mx[:, :], SCALE, None, ALU.mult).then_inc(max_done, 1)
                        v.wait_ge(exp_done, n + 1)
                        chain.link(v.reciprocal(rec[:, :], ssum[:, :]))
                        v.wait_ge(o_pe, n + 1)
                        for t in range(QT):
                            v.scalar_tensor_tensor(out=dst[:, t, :], in0=pO[:, t * D:(t + 1) * D],
                                                   scalar=rec[:, t:t + 1], in1=dst[:, t, :],
                                                   op0=ALU.mult, op1=ALU.add)
                        v.sem_inc(x_done, 1)
                rounds(v, step, SEQS)

            @block.scalar
            def _(act):
                act.wait_ge(w_in, 64)

                def step(n, ahead, now, back):
                    m = n + 1
                    if ahead:
                        act.wait_ge(t_pe, m + 1)
                        act.activation(xnT[:, :], pT[:, 0:SEQ], ACT.Copy).then_inc(xnT_done, 1)
                    if now:
                        act.wait_ge(max_done, n + 1)
                        for t, lo, hi in COLS:
                            ins = act.activation(prob[:, lo:hi], pS[:, lo:hi], ACT.Exp, bias=negm[:, t:t + 1],
                                                 scale=SCALE, accum_out=ssum[:, t:t + 1])
                        ins.then_inc(exp_done, 1)
                    if ahead:
                        act.wait_ge(qkv_pe, m + 1)
                        act.activation(q[:, :], pQ[:, 0:SEQ], ACT.Identity, bias=bqk[:, 0:1])
                        act.activation(key[:, :], pK[:, 0:SEQ], ACT.Identity, bias=bqk[:, 1:2]).then_inc(qk_done, 1)
                    if now:
                        act.wait_ge(pt_pe, n + 1)
                        act.activation(probT[:, :], pP[:, 0:3 * P], ACT.Copy).then_inc(probT_done, 1)
                    if ahead:
                        if now:
                            act.wait_ge(o_pe, n + 1)
                        act.activation(val[:, :, :].rearrange("p t d -> p (t d)"), pV[:, 0:SEQ], ACT.Copy
                                       ).then_inc(val_done, 1)
                rounds(act, step, SEQS)

            @block.tensor
            def _(pe):
                ident = core["ident"]
                pe.wait_ge(w_in, 64)
                pe.wait_ge(setup, 1)

                def step(n, ahead, now, back):
                    m = n + 1
                    if now:
                        pe.wait_ge(qk_done, n + 1)
                        for t, lo, hi in COLS:
                            pe.matmul(pS[:, lo:hi], q[:, t * P:(t + 1) * P], key[:, 0:hi - lo], start=True, stop=False)
                            ins = pe.matmul(pS[:, hi - P:hi], core["identb"], maskq[:, :], start=False, stop=True)
                        ins.then_inc(s_pe, 1)
                    if ahead:
                        pe.wait_ge(xn_done, m + 1)
                        for t in range(QT):
                            ins = pe.transpose(pT[:, t * P:(t + 1) * P], xn[:, t, :], ident)
                        ins.then_inc(t_pe, 1)
                        pe.wait_ge(xnT_done, m + 1)
                        if now:
                            pe.wait_ge(val_done, n + 1)
                        pe.matmul(pQ[:, 0:SEQ], wqkv[:, 0:D], xnT[:, :], start=True, stop=True)
                        pe.matmul(pK[:, 0:SEQ], wqkv[:, D:2 * D], xnT[:, :], start=True, stop=True)
                        for t in range(QT):
                            out = pV[:, t * D:(t + 1) * D]
                            pe.matmul(out, xnT[:, t * P:(t + 1) * P], wqkv[:, 2 * D:3 * D], start=True, stop=False)
                            ins = pe.matmul(out, ones1[:, :], bv[:, :], start=False, stop=True)
                        ins.then_inc(qkv_pe, 1)
                    if now:
                        pe.wait_ge(exp_done, n + 1)
                        for c in range(3):
                            ins = pe.transpose(pP[:, c * P:(c + 1) * P], prob[:, c * P:(c + 1) * P], ident)
                        ins.then_inc(pt_pe, 1)
                        pe.wait_ge(probT_done, n + 1)
                        pe.wait_ge(val_done, n + 1)
                        if later(n, 1):
                            pe.wait_ge(x_done, n)
                        pe.matmul(pO[:, 0:D], probT[:, 0:P], val[:, 0, :], start=True, stop=True)
                        pe.matmul(pO[:, D:2 * D], probT[:, P:2 * P], val[:, 0, :], start=True, stop=False)
                        pe.matmul(pO[:, D:2 * D], probT[:, 2 * P:3 * P], val[:, 1, :], start=False, stop=True
                                  ).then_inc(o_pe, 1)
                rounds(pe, step, SEQS)
        k.clear()


def adapters(nc, core, tag, w):
    E, R = 8, 64
    W = R + D + D + 3
    row_moments(nc, core, tag + "m_", core["x"], 1e-5)
    with ExitStack() as stack:
        k = Held(nc, stack, tag)
        every = k.sb("every", [P, E, W]); biases = k.sb("biases", [P, 3, E]); base = k.sb("base", [P, D]); baseb = k.sb("baseb", [P, 1])
        mu = k.sb("mu", [P, E]); sigma = k.sb("sigma", [P, E]); var = k.sb("var", [P, E]); iv = k.sb("iv", [P, E])
        muiv = k.sb("muiv", [P, E]); cross = k.sb("cross", [P, E]); square = k.sb("square", [P, E])
        iota = k.sb("iota", [1, E]); ones1 = k.sb("ones1", [1, P]); onescol = k.sb("onescol", [P, 1])
        centred = k.sb("centred", [P, QT, D])
        xn = k.sb("xn", [P, QT, D]); xnT = k.sb("xnT", [P, SEQ]); sqr = k.sb("sqr", [P, SEQ])
        sum1 = k.sb("sum1", [P, 1]); sum2 = k.sb("sum2", [P, 1]); mean1 = k.sb("mean1", [P, 1])
        mean2 = k.sb("mean2", [P, 1])
        gain = k.sb("gain", [1, E]); best = k.sb("best", [1, E]); at = k.sb("at", [1, E], mybir.dt.uint32)
        atf = k.sb("atf", [1, 1]); hot = k.sb("hot", [1, E]); hotb = k.sb("hotb", [P, E])
        picked = [k.sb(f"picked{b}", [P, W]) for b in range(2)]; mine = k.sb("mine", [P, W]); outb = k.sb("outb", [P, 1])
        hT = k.sb("hT", [R, SEQ]); aT = k.sb("aT", [P, SEQ]); yT = k.sb("yT", [P, SEQ])
        pT = k.ps("pT", [P, BLK]); pL = k.ps("pL", [P, BLK]); pB = k.ps("pB", [P, BLK]); pH = k.ps("pH", [P, BLK])
        pA = k.ps("pA", [P, BLK]); pY = k.ps("pY", [P, BLK]); pR = k.ps("pR", [P, BLK])
        (w_in, setup, disc_done, xn_done, t_pe, xnT_done, sq_done, mean_done, l_pe,
         hot_done, b_pe, mine_done, h_pe, hT_done, a_pe, aT_done, y_pe, yT_done, r_pe, x_done) = k.sem(
            "w_in setup disc_done xn_done t_pe xnT_done sq_done mean_done l_pe "
            "hot_done b_pe mine_done h_pe hT_done a_pe aT_done y_pe yT_done r_pe x_done")
        W_IN = 16 * 11
        DOWN, UP, CONV, BD, BU, BC = 0, R, R + D, R + 2 * D, R + 2 * D + 1, R + 2 * D + 2
        with nc.Block() as block:
            @block.sync
            def _(sp):
                sp.wait_ge(setup, 2)
                for dst, src in ((every[:, :, DOWN:DOWN + R], w["down"]), (every[0:R, :, UP:UP + D], w["up"]),
                                 (every[:, :, CONV:CONV + D], w["conv"]), (biases[0:R, 0, :], w["downb"]),
                                 (biases[:, 1, :], w["upb"]), (biases[:, 2, :], w["convb"]),
                                 (base[:, :], w["base"]), (baseb[:, :], w["baseb"]), (mu[:, :], w["mu"]),
                                 (sigma[:, :], w["sigma"]), (iota[:, :], core["iota8"])):
                    sp.dma_start(dst, src).then_inc(w_in, 16)

            @block.gpsimd
            def _(g):
                g.memset(every[:, :, :], 0.0).then_inc(setup, 1)
                g.memset(biases[:, :, :], 0.0).then_inc(setup, 1)
                g.memset(ones1[:, :], 1.0).then_inc(setup, 1)
                g.memset(onescol[:, :], 1.0).then_inc(setup, 1)

            @block.vector
            def _(v):
                chain = Chain(v)
                link = chain.link
                v.wait_ge(w_in, W_IN)
                v.wait_ge(setup, 4)
                v.tensor_copy(every[:, :, BD:BC + 1], biases[:, :, :].rearrange("p b e -> p e b"))
                link(v.tensor_tensor(var[:, :], sigma[:, :], sigma[:, :], op=ALU.mult))
                link(v.reciprocal(iv[:, :], var[:, :]))
                link(v.tensor_tensor(muiv[:, :], mu[:, :], iv[:, :], op=ALU.mult))
                link(v.tensor_scalar(cross[:, :], muiv[:, :], -2.0, None, ALU.mult))
                v.tensor_tensor(square[:, :], muiv[:, :], mu[:, :], op=ALU.mult).then_inc(disc_done, 1)

                def step(n, ahead, now, back):
                    m = n + 1
                    v.drain()
                    if ahead:
                        normalised(v, core, rows(core["x"], m * QT, QT), m * QT, centred[:, :, :], xn[:, :, :]
                                   ).then_inc(xn_done, 1)
                        v.wait_ge(xnT_done, m + 1)
                        link(v.tensor_reduce(sum1[:, :], xnT[:, :], op=ALU.add, axis=AX.X))
                        v.wait_ge(sq_done, m + 1)
                        v.tensor_scalar(mean1[:, :], sum1[:, :], 1.0 / SEQ, None, ALU.mult)
                        v.tensor_scalar(mean2[:, :], sum2[:, :], 1.0 / SEQ, None, ALU.mult).then_inc(mean_done, 1)
                        v.wait_ge(l_pe, m + 1)
                        link(v.tensor_scalar(gain[:, :], pL[0:1, 0:E], -1.0 / D, None, ALU.mult))
                        link(v.max(best[:, :], gain[:, :]))
                        link(v.max_index(at[:, :], best[:, :], gain[:, :]))
                        link(v.tensor_copy(atf[:, :], at[:, 0:1]))
                        v.tensor_scalar(hot[:, :], iota[:, :], atf[:, 0:1], None, ALU.is_equal).then_inc(hot_done, 1)
                        v.wait_ge(b_pe, m + 1)
                        link(v.tensor_copy(hotb[:, :], pB[:, 0:E]))
                        link(v.tensor_scalar(picked[0][:, :], every[:, 0, :], hotb[:, 0:1], None, ALU.mult))
                        for e in range(1, E):
                            if e == E - 1 and now:
                                v.wait_ge(yT_done, n + 1)
                            dst = mine if e == E - 1 else picked[e % 2]
                            link(v.scalar_tensor_tensor(out=dst[:, :], in0=every[:, e, :], scalar=hotb[:, e:e + 1],
                                                        in1=picked[1 - e % 2][:, :], op0=ALU.mult, op1=ALU.add))
                        v.tensor_tensor(outb[:, :], mine[:, BC:BC + 1], baseb[:, :], op=ALU.add
                                        ).then_inc(mine_done, 1)
                    if now:
                        dst = rows(core["x"], n * QT, QT)
                        v.wait_ge(r_pe, n + 1)
                        v.tensor_tensor(dst, pR[:, 0:SEQ].rearrange("p (t d) -> p t d", d=D), dst, op=ALU.add
                                        ).then_inc(x_done, 1)
                rounds(v, step, SEQS)

            @block.scalar
            def _(act):
                def step(n, ahead, now, back):
                    m = n + 1
                    if now:
                        act.wait_ge(mine_done, n + 1)
                        act.wait_ge(h_pe, n + 1)
                        act.activation(hT[:, :], pH[0:R, 0:SEQ], ACT.Relu, bias=mine[0:R, BD:BD + 1]
                                       ).then_inc(hT_done, 1)
                    if ahead:
                        act.wait_ge(t_pe, m + 1)
                        act.activation(xnT[:, :], pT[:, 0:SEQ], ACT.Copy).then_inc(xnT_done, 1)
                        act.activation(sqr[:, :], pT[:, 0:SEQ], ACT.Square, accum_out=sum2[:, 0:1]
                                       ).then_inc(sq_done, 1)
                    if now:
                        act.wait_ge(a_pe, n + 1)
                        act.activation(aT[:, :], pA[:, 0:SEQ], ACT.Identity, bias=mine[:, BU:BU + 1]
                                       ).then_inc(aT_done, 1)
                        act.wait_ge(y_pe, n + 1)
                        act.activation(yT[:, :], pY[:, 0:SEQ], ACT.Identity, bias=outb[:, 0:1]).then_inc(yT_done, 1)
                rounds(act, step, SEQS)

            @block.tensor
            def _(pe):
                ident = core["ident"]
                pe.wait_ge(w_in, W_IN)
                pe.wait_ge(disc_done, 1)

                def step(n, ahead, now, back):
                    m = n + 1
                    if now:
                        pe.wait_ge(mine_done, n + 1)
                        pe.matmul(pH[0:R, 0:SEQ], mine[:, DOWN:DOWN + R], xnT[:, :], start=True, stop=True
                                  ).then_inc(h_pe, 1)
                        pe.matmul(pY[:, 0:SEQ], base[:, :], xnT[:, :], start=True, stop=False)
                    if ahead:
                        pe.wait_ge(xn_done, m + 1)
                        for t in range(QT):
                            ins = pe.transpose(pT[:, t * P:(t + 1) * P], xn[:, t, :], ident)
                        ins.then_inc(t_pe, 1)
                    if now:
                        pe.wait_ge(hT_done, n + 1)
                        pe.matmul(pA[:, 0:SEQ], mine[0:R, UP:UP + D], hT[:, :], start=True, stop=True
                                  ).then_inc(a_pe, 1)
                    if ahead:
                        pe.wait_ge(mean_done, m + 1)
                        pe.matmul(pL[0:1, 0:E], mean2[:, :], iv[:, :], start=True, stop=False)
                        pe.matmul(pL[0:1, 0:E], mean1[:, :], cross[:, :], start=False, stop=False)
                        pe.matmul(pL[0:1, 0:E], onescol[:, :], square[:, :], start=False, stop=True).then_inc(l_pe, 1)
                    if now:
                        pe.wait_ge(aT_done, n + 1)
                        pe.matmul(pY[:, 0:SEQ], mine[:, CONV:CONV + D], aT[:, :], start=False, stop=True
                                  ).then_inc(y_pe, 1)
                    if ahead:
                        pe.wait_ge(hot_done, m + 1)
                        pe.matmul(pB[:, 0:E], ones1[:, :], hot[:, :], start=True, stop=True).then_inc(b_pe, 1)
                    if now:
                        pe.wait_ge(yT_done, n + 1)
                        if later(n, 1):
                            pe.wait_ge(x_done, n)
                        for t in range(QT):
                            ins = pe.transpose(pR[:, t * P:(t + 1) * P], yT[:, t * P:(t + 1) * P], ident)
                        ins.then_inc(r_pe, 1)
                rounds(pe, step, SEQS)
        k.clear()

def part_of(a, prefix):
    return {n[len(prefix):]: x for n, x in a.items() if n.startswith(prefix)}


def stage_a0(nc, core, a):
    attention(nc, core, "a0_", core["x"], 1e-5, part_of(a, "a0_"), False)


def stage_f0(nc, core, a):
    routed_experts(nc, core, "f0_", part_of(a, "f0_"))


def stage_a1(nc, core, a):
    normalise(nc, core, "i1_", core["x"], 1e-5, "init")
    with nc.Fori(0, 4) as layer:
        attention(nc, core, "a1_", core["h"], 1e-6, part_of(a, "a1_"), True, layer)
        feed_forward(nc, core, "f1_", core["h"], 1e-6, part_of(a, "f1_"), True, layer)


def stage_r1(nc, core, a):
    top2_experts(nc, core, "r1_", part_of(a, "r1_"))


def stage_l2(nc, core, a):
    performer(nc, core, "p2_", part_of(a, "p2_"))
    feed_forward(nc, core, "g2_", core["h"], 1e-6, part_of(a, "g2_"), False)
    normalise(nc, core, "n2_", core["h"], 1e-6, "add", a["n2_gb"])


def stage_q2(nc, core, a):
    fp4_feed_forward(nc, core, "q2_", part_of(a, "q2_"))


def stage_a3(nc, core, a):
    one_head_attention(nc, core, "a3_", part_of(a, "a3_"))


def stage_f3(nc, core, a):
    adapters(nc, core, "f3_", part_of(a, "f3_"))



def load_core(nc, a, pool):
    core = {}
    x = pool("x_store", [P, TILES, D])
    h = pool("h_store", [P, TILES, D])
    ident = pool("ident", [P, P])
    identb = pool("identb", [P, P], BF16)
    core["mean"], core["rstd"] = pool("row_mean", [P, TILES]), pool("row_rstd", [P, TILES])
    got = nc.alloc_semaphore("core_in")
    with nc.Block() as block:
        @block.sync
        def _(sp):
            sp.dma_start(ident[:, :], a["ident"]).then_inc(got, 16)
            sp.dma_start(identb[:, :], a["identb"]).then_inc(got, 16)
            for c in range(8):
                sp.dma_start(x[:, c * 8:(c + 1) * 8, :],
                             a["x"].rearrange("s (t p) d -> p (s t) d", p=P)[:, c * 8:(c + 1) * 8, :]
                             ).then_inc(got, 16)
            sp.wait_ge(got, 160)
    core.update(x=x, h=h, ident=ident[:, :], identb=identb[:, :])
    for name in ("maskq", "maskk", "esel", "turn", "kturn", "tri", "selhm", "sell", "diag", "iota8"):
        core[name] = a[name]
    return core


def store_out(nc, store, out):
    put = nc.alloc_semaphore("out_written")
    with nc.Block() as block:
        @block.sync
        def _(sp):
            for c in range(8):
                sp.dma_start(out.rearrange("s (t p) d -> p (s t) d", p=P)[:, c * 8:(c + 1) * 8, :],
                             store[:, c * 8:(c + 1) * 8, :]).then_inc(put, 16)
            sp.wait_ge(put, 128)

def constants():
    import numpy as np
    c = {}
    eye = np.eye(P, dtype=np.float32)
    q, k = np.arange(P)[:, None], np.arange(P)[None, :]
    above = np.where(k > q, NEG, 0.0).astype(np.float32)
    b16 = lambda t: t.astype(mybir.dt.np(BF16))
    c["ident"], c["identb"] = eye, b16(eye)
    c["maskq"], c["maskk"] = b16(above), b16(above.T)
    e = np.zeros((32, HEADS, P), np.float32)
    for h in range(HEADS):
        e[h, h], e[16 + h, h] = 1, 1
    c["esel"] = b16(e)
    inv = 1.0 / 10000.0 ** (np.arange(0, HD, 2) / HD)
    ang = np.arange(SEQ)[None, :] * inv[:, None]
    sin, cos = np.sin(ang), np.cos(ang)
    turn = np.stack([np.concatenate([sin, -cos]), np.concatenate([cos, sin])], 1)
    c["turn"] = np.tile(turn, (HEADS, 1, 1)).astype(np.float32)
    kt = np.concatenate([cos, sin]).astype(np.float32)
    parts = []
    for _ in range(3):
        parts.append(b16(kt))
        kt = kt - parts[-1].astype(np.float32)
    c["kturn"] = np.concatenate([parts[i] for i in KPART])
    c["diag"] = np.kron(np.eye(GH, dtype=np.float32), np.ones((32, 9), np.float32))
    c["iota8"] = np.arange(8, dtype=np.float32)[None]
    c["tri"] = np.tril(np.ones((8, 8), np.float32), -1).reshape(64)
    sel = np.zeros((64, 32, 128), np.float32)
    for e in range(64):
        sel[e, e // 2, 64 * (e % 2):64 * (e % 2) + 64] = 1
    c["selhm"], c["sell"] = b16(np.concatenate([sel, sel])), b16(sel)
    return c


TURN_A = [h * HD + r % 4 for h in range(HEADS) for r in range(HD)]
TURN_B = [h * HD + 4 + r % 4 for h in range(HEADS) for r in range(HD)]


def layout_rel(wq, wk, wv, wo, bq, bk, bv, bo, u, lnw, lnb):
    import numpy as np
    T = lambda m: m.transpose(0, 2, 1)
    uf = u.reshape(u.shape[0], D)
    return dict(
        wq=np.concatenate([T(wq), T(wk), T(wv)], 2), wo=T(wo),
        bqk=np.stack([bq, bk], 2), bv=bv[:, None, :], bo=bo[:, None, :], lnw=np.stack([lnw, lnb], 2),
        u12=np.concatenate([T(wq)[:, :, TURN_A], T(wq)[:, :, TURN_B]], 2),
        b12=np.stack([bq[:, TURN_A], bq[:, TURN_B], uf[:, TURN_A], uf[:, TURN_B]], 2))


def layout_all(i):
    import numpy as np
    T = lambda m: m.transpose(0, 2, 1)
    a = {}
    a["a0_wq"], a["a0_wo"] = i["L0_attn_w_in"].T, i["L0_attn_w_out"].T
    a["a0_bqk"] = i["L0_attn_b_in"][:2 * D].reshape(2, D).T
    a["a0_bv"], a["a0_bo"] = i["L0_attn_b_in"][None, 2 * D:], i["L0_attn_b_out"][None]
    a["f0_wg"] = i["L0_ffn_Wg"].transpose(1, 0, 2).reshape(D, -1)
    a["f0_wu"] = i["L0_ffn_Wu"].transpose(1, 0, 2).reshape(D, -1)
    a["f0_wd"] = i["L0_ffn_Wd"].reshape(32, P, D).transpose(1, 0, 2)
    a["f0_swg"], a["f0_swu"], a["f0_swd"] = i["L0_ffn_SWg"], i["L0_ffn_SWu"], i["L0_ffn_SWd"]
    a["f0_router"], a["f0_bias"] = i["L0_ffn_router_w"].T, i["L0_ffn_e_bias"]
    for n, x in layout_rel(*(i["L1_attn_" + n] for n in ("Wq", "Wk", "Wv", "Wo", "bq", "bk", "bv", "bo", "u_bias",
                                                           "ln1_w", "ln1_b"))).items():
        a["a1_" + n] = x
    a["f1_w1"] = T(i["L1_attn_W1"])
    a["f1_w2"] = T(i["L1_attn_W2"]).reshape(4, 4, P, D).transpose(0, 2, 1, 3)
    a["f1_ln"] = np.stack([i["L1_attn_ln2_w"], i["L1_attn_ln2_b"]], 2)
    a["f1_b1"] = i["L1_attn_b1"].reshape(4, 4, P).transpose(0, 2, 1)
    a["f1_b2"] = i["L1_attn_b2"][:, :, None]
    e = i["L1_ffn_expert_w"]
    a["r1_we"] = e.transpose(2, 0, 1).reshape(D, -1)
    a["r1_be"] = i["L1_ffn_expert_b"].reshape(-1)
    a["r1_gate"], a["r1_wc"] = i["L1_ffn_gate_w"].T, i["L1_ffn_combine_w"].T
    wq, wk, wv = (i["L2_attn_w" + n].reshape(D, D) for n in "qkv")
    a["p2_wqkv"] = np.concatenate([wq, wk, wv], 1)
    a["p2_wT"] = np.stack([wq.T, wk.T], 1)
    a["p2_omega"], a["p2_wo"] = i["L2_attn_omega"].T, i["L2_attn_wo"]
    a["g2_w1"], a["g2_w2"] = i["L2_attn_w1"], i["L2_attn_w2"].reshape(4, P, D).transpose(1, 0, 2)
    a["g2_ln"] = np.stack([i["L2_attn_ln1_g"], i["L2_attn_ln1_b"]], 1)
    a["g2_b1"], a["g2_b2"] = i["L2_attn_b1"].reshape(4, P).T, i["L2_attn_b2"][:, None]
    a["n2_gb"] = np.stack([i["L2_attn_ln2_g"], i["L2_attn_ln2_b"]], 0)
    a["q2_wg"], a["q2_wu"], a["q2_wd"] = (i["L2_ffn_w_" + n] for n in ("gate", "up", "down"))
    a["a3_w"] = i["L3_attn_W"]
    a["a3_bqk"], a["a3_bv"] = i["L3_attn_b"][:2 * D].reshape(2, D).T, i["L3_attn_b"][None, 2 * D:]
    f = {n: i["L3_ffn_" + n] for n in ("base_W", "base_b", "disc_mu", "disc_sigma", "down_W", "down_b", "up_W",
                                       "up_b", "conv_W", "conv_b")}
    a["f3_base"], a["f3_baseb"] = f["base_W"].T, f["base_b"][:, None]
    a["f3_mu"], a["f3_sigma"] = f["disc_mu"].T, f["disc_sigma"].T
    a["f3_down"] = f["down_W"].transpose(1, 0, 2)
    a["f3_up"] = f["up_W"].transpose(1, 0, 2)
    a["f3_conv"] = f["conv_W"].transpose(2, 0, 1)
    a["f3_downb"], a["f3_upb"], a["f3_convb"] = (f[n].T for n in ("down_b", "up_b", "conv_b"))
    return a


def program(nc, a, out):
    core = load_core(nc, a, lambda name, shape, dt=F32: nc.alloc_sbuf_tensor(name, shape, dt))
    stage_a0(nc, core, a)
    stage_f0(nc, core, a)
    stage_a1(nc, core, a)
    stage_r1(nc, core, a)
    stage_l2(nc, core, a)
    stage_q2(nc, core, a)
    stage_a3(nc, core, a)
    stage_f3(nc, core, a)
    store_out(nc, core["x"], out)


def kernel(**inputs):
    import numpy as np
    import concourse.bacc as bacc
    from concourse.bass_utils import run_bass_kernel_spmd

    laid = dict(constants(), x=np.asarray(inputs["L0_attn_x"]),
                **layout_all({name: np.asarray(x) for name, x in inputs.items()}))
    nc = bacc.Bacc("TRN2", target_bir_lowering=False, num_devices=1)
    arrays, a = {}, {}
    for name, x in laid.items():
        x = np.ascontiguousarray(x)
        arrays[f"in_{name}_dram"] = x
        a[name] = nc.dram_tensor(f"in_{name}_dram", x.shape, mybir.dt.from_np(x.dtype), kind="ExternalInput").ap()
    out = nc.dram_tensor("out_0_dram", (SEQS, SEQ, D), F32, kind="ExternalOutput").ap()
    program(nc, a, out)
    result = run_bass_kernel_spmd(nc, [arrays], core_ids=[0])
    return result.results[0]["out_0_dram"]
```
